# Optimizing a Trainium2 kernel written in Bass

```python
import numpy as np
import jax
import jax.numpy as jnp

def _softmax(x, axis=-1):
    return jax.nn.softmax(x, axis=axis)

def _gelu(x):
    return jax.nn.gelu(x, approximate=True)

def _silu(x):
    return jax.nn.silu(x)

def _sigmoid(x):
    return jax.nn.sigmoid(x)

def _layernorm(x, axis=-1, eps=1e-05):
    m = jnp.mean(x, axis=axis, keepdims=True)
    v = jnp.var(x, axis=axis, keepdims=True)
    return (x - m) / jnp.sqrt(v + eps)

def _scatter_add(tgt, idx, src, axis=0):
    return tgt.at[idx].add(src)

def _segment_sum(src, seg, n):
    return jax.ops.segment_sum(src, seg, n)
kernel_name = 'mk_prb_d1_jaxref_r8_c470a9'

def setup_inputs(seed: int=0):
    np.random.seed(seed)
    _w = jnp.asarray

    def _L0_attn_setup():
        import jax, jax.numpy as jnp
        import numpy as np
        N_HEADS = 16
        D_MODEL = 128
        D_HEAD = 64
        MAX_SEQ_LEN = 128

        def _pos_bias(rel_pos_bias, T):
            i = jnp.arange(T)[:, None]
            j = jnp.arange(T)[None, :]
            idx = jnp.clip(MAX_SEQ_LEN - 1 - (i - j), 0, MAX_SEQ_LEN - 1)
            bias = rel_pos_bias[:, idx]
            return jnp.where((j <= i)[None], bias, 0.0)
        key = jax.random.key(seed)
        ks = jax.random.split(key, 7)
        std = np.sqrt(2.0 / (D_MODEL + D_HEAD)).astype(np.float32)
        hd = N_HEADS * D_HEAD
        Wq = jax.random.normal(ks[0], (D_MODEL, hd), jnp.float32) * std
        Wk = jax.random.normal(ks[1], (D_MODEL, hd), jnp.float32) * std
        Wv = jax.random.normal(ks[2], (D_MODEL, hd), jnp.float32) * std
        Wo = jax.random.normal(ks[3], (hd, D_MODEL), jnp.float32) * (1.0 / np.sqrt(hd))
        bo = jnp.zeros((D_MODEL,), jnp.float32)
        rel_pos_bias = jax.random.normal(ks[4], (N_HEADS, MAX_SEQ_LEN), jnp.float32) * 0.02
        x = jax.random.normal(ks[5], (4, 128, D_MODEL), jnp.float32)
        return {'x': x, 'Wq': Wq, 'Wk': Wk, 'Wv': Wv, 'Wo': Wo, 'bo': bo, 'rel_pos_bias': rel_pos_bias}
    _L0_attn_in = _L0_attn_setup()

    def _L0_ffn_setup():
        import jax, jax.numpy as jnp
        import numpy as np
        DIM = 128
        DEPTH = 2
        HEADS = 8
        DIM_HEAD = 64
        WINDOW = 64
        INNER = HEADS * DIM_HEAD
        HID = int(DIM * 4 * 2 / 3)
        B, N = (2, 1024)
        QK_SCALE = 8.0

        def shift_token(t):
            t1, t2 = jnp.split(t, 2, axis=-1)
            t2 = jnp.pad(t2, ((0, 0), (1, 0), (0, 0)))[:, :-1]
            return jnp.concatenate([t1, t2], axis=-1)

        def l2norm(t):
            return t / jnp.clip(jnp.linalg.norm(t, axis=-1, keepdims=True), 1e-12)

        def rotate_half(x):
            x1, x2 = jnp.split(x, 2, axis=-1)
            return jnp.concatenate([-x2, x1], axis=-1)

        def rotary_xpos(q, k):
            n = q.shape[-2]
            half_idx = jnp.arange(0, DIM_HEAD, 2, dtype=jnp.float32)
            inv_freq = 1.0 / 10000.0 ** (half_idx / DIM_HEAD)
            t = jnp.arange(n, dtype=jnp.float32)
            freqs = t[:, None] * inv_freq[None, :]
            freqs = jnp.concatenate([freqs, freqs], axis=-1)
            base = (half_idx + 0.4 * DIM_HEAD) / (1.4 * DIM_HEAD)
            power = (t - n // 2) / float(WINDOW // 2)
            scale = base[None, :] ** power[:, None]
            scale = jnp.concatenate([scale, scale], axis=-1)
            cos, sin = (jnp.cos(freqs), jnp.sin(freqs))
            q = q * cos * scale + rotate_half(q) * sin * scale
            k = k * cos / scale + rotate_half(k) * sin / scale
            return (q, k)

        def local_attention(q, k, v):
            b, h, n, d = q.shape
            w = n // WINDOW
            bq = q.reshape(b, h, w, WINDOW, d) * QK_SCALE
            bk = k.reshape(b, h, w, WINDOW, d)
            bv = v.reshape(b, h, w, WINDOW, d)

            def look_around(t):
                p = jnp.pad(t, ((0, 0), (0, 0), (1, 0), (0, 0), (0, 0)))
                return jnp.concatenate([p[:, :, :w], p[:, :, 1:]], axis=3)
            bk, bv = (look_around(bk), look_around(bv))
            bt = jnp.arange(n).reshape(w, WINDOW)
            btp = jnp.pad(bt, ((1, 0), (0, 0)), constant_values=-1)
            btk = jnp.concatenate([btp[:w], btp[1:]], axis=1)
            sim = jnp.einsum('bhwid,bhwjd->bhwij', bq, bk)
            i = bt[:, :, None]
            j = btk[:, None, :]
            mask = (i < j) | (i > j + WINDOW) | (j == -1)
            sim = jnp.where(mask, -jnp.finfo(sim.dtype).max, sim)
            attn = jax.nn.softmax(sim, axis=-1)
            out = jnp.einsum('bhwij,bhwjd->bhwid', attn, bv)
            return out.reshape(b, h, n, d)

        def _layer(x, wqkv, qs, ksc, wo, lg, lb, w1, b1, w2, b2):
            b, n, _ = x.shape
            h = shift_token(x)
            qkv = h @ wqkv
            q, k, v = jnp.split(qkv, 3, axis=-1)
            to_heads = lambda t: t.reshape(b, n, HEADS, DIM_HEAD).transpose(0, 2, 1, 3)
            q, k, v = (to_heads(q), to_heads(k), to_heads(v))
            q = l2norm(q) * qs
            k = l2norm(k) * ksc
            q, k = rotary_xpos(q, k)
            o = local_attention(q, k, v)
            o = o.transpose(0, 2, 1, 3).reshape(b, n, INNER)
            x = x + o @ wo
            h = shift_token(x)
            mu = h.mean(-1, keepdims=True)
            var = h.var(-1, keepdims=True)
            h = (h - mu) / jnp.sqrt(var + 1e-05) * lg + lb
            h = h @ w1 + b1
            a, g = jnp.split(h, 2, axis=-1)
            h = a * jax.nn.gelu(g, approximate=False)
            x = x + h @ w2 + b2
            return x
        key = jax.random.key(seed)
        ks = jax.random.split(key, 6)
        return {'x': jax.random.normal(ks[0], (B, N, DIM), jnp.float32), 'wqkv': jax.random.normal(ks[1], (DEPTH, DIM, 3 * INNER), jnp.float32) * 0.02, 'q_scale': jnp.ones((DEPTH, DIM_HEAD), jnp.float32), 'k_scale': jnp.ones((DEPTH, DIM_HEAD), jnp.float32), 'wo': jax.random.normal(ks[2], (DEPTH, INNER, DIM), jnp.float32) * 0.02, 'ln_g': jnp.ones((DEPTH, DIM), jnp.float32), 'ln_b': jnp.zeros((DEPTH, DIM), jnp.float32), 'w1': jax.random.normal(ks[3], (DEPTH, DIM, 2 * HID), jnp.float32) * 0.02, 'b1': jnp.zeros((DEPTH, 2 * HID), jnp.float32), 'w2': jax.random.normal(ks[4], (DEPTH, HID, DIM), jnp.float32) * 0.02, 'b2': jnp.zeros((DEPTH, DIM), jnp.float32)}
    _L0_ffn_in = _L0_ffn_setup()
    _d = {'L0_attn_x': _L0_attn_in['x'], 'L0_attn_Wq': _L0_attn_in['Wq'], 'L0_attn_Wk': _L0_attn_in['Wk'], 'L0_attn_Wv': _L0_attn_in['Wv'], 'L0_attn_Wo': _L0_attn_in['Wo'], 'L0_attn_bo': _L0_attn_in['bo'], 'L0_attn_rel_pos_bias': _L0_attn_in['rel_pos_bias'], 'L0_ffn_wqkv': _L0_ffn_in['wqkv'], 'L0_ffn_q_scale': _L0_ffn_in['q_scale'], 'L0_ffn_k_scale': _L0_ffn_in['k_scale'], 'L0_ffn_wo': _L0_ffn_in['wo'], 'L0_ffn_ln_g': _L0_ffn_in['ln_g'], 'L0_ffn_ln_b': _L0_ffn_in['ln_b'], 'L0_ffn_w1': _L0_ffn_in['w1'], 'L0_ffn_b1': _L0_ffn_in['b1'], 'L0_ffn_w2': _L0_ffn_in['w2'], 'L0_ffn_b2': _L0_ffn_in['b2']}
    _x0 = _d['L0_attn_x']
    _d['L0_attn_x'] = jax.random.normal(jax.random.fold_in(jax.random.key(seed), 1), (16, 512, 128), dtype=_x0.dtype)
    del _x0
    return _d

def reference(L0_attn_x, L0_attn_Wq, L0_attn_Wk, L0_attn_Wv, L0_attn_Wo, L0_attn_bo, L0_attn_rel_pos_bias, L0_ffn_wqkv, L0_ffn_q_scale, L0_ffn_k_scale, L0_ffn_wo, L0_ffn_ln_g, L0_ffn_ln_b, L0_ffn_w1, L0_ffn_b1, L0_ffn_w2, L0_ffn_b2):

    def _L0_attn_ref(x, Wq, Wk, Wv, Wo, bo, rel_pos_bias):
        import jax, jax.numpy as jnp
        import numpy as np
        N_HEADS = 16
        D_MODEL = 128
        D_HEAD = 64
        MAX_SEQ_LEN = 128

        def _pos_bias(rel_pos_bias, T):
            i = jnp.arange(T)[:, None]
            j = jnp.arange(T)[None, :]
            idx = jnp.clip(MAX_SEQ_LEN - 1 - (i - j), 0, MAX_SEQ_LEN - 1)
            bias = rel_pos_bias[:, idx]
            return jnp.where((j <= i)[None], bias, 0.0)
        B, T, _ = x.shape
        H, dh = (N_HEADS, D_HEAD)
        q = (x @ Wq).reshape(B, T, H, dh).transpose(0, 2, 1, 3)
        k = (x @ Wk).reshape(B, T, H, dh).transpose(0, 2, 1, 3)
        v = (x @ Wv).reshape(B, T, H, dh).transpose(0, 2, 1, 3)
        logits = jnp.einsum('bhqd,bhkd->bhqk', q, k)
        i = jnp.arange(T)[:, None]
        j = jnp.arange(T)[None, :]
        causal = jnp.where(j > i, -jnp.inf, 0.0)
        logits = logits + causal[None, None] + _pos_bias(rel_pos_bias, T)[None]
        logits = logits / dh
        probs = jax.nn.softmax(logits, axis=-1)
        out = jnp.einsum('bhqk,bhkd->bhqd', probs, v)
        out = out.transpose(0, 2, 1, 3).reshape(B, T, H * dh)
        return out @ Wo + bo

    def _L0_ffn_ref(x, wqkv, q_scale, k_scale, wo, ln_g, ln_b, w1, b1, w2, b2):
        import jax, jax.numpy as jnp
        import numpy as np
        DIM = 128
        DEPTH = 2
        HEADS = 8
        DIM_HEAD = 64
        WINDOW = 64
        INNER = HEADS * DIM_HEAD
        HID = int(DIM * 4 * 2 / 3)
        B, N = (2, 1024)
        QK_SCALE = 8.0

        def shift_token(t):
            t1, t2 = jnp.split(t, 2, axis=-1)
            t2 = jnp.pad(t2, ((0, 0), (1, 0), (0, 0)))[:, :-1]
            return jnp.concatenate([t1, t2], axis=-1)

        def l2norm(t):
            return t / jnp.clip(jnp.linalg.norm(t, axis=-1, keepdims=True), 1e-12)

        def rotate_half(x):
            x1, x2 = jnp.split(x, 2, axis=-1)
            return jnp.concatenate([-x2, x1], axis=-1)

        def rotary_xpos(q, k):
            n = q.shape[-2]
            half_idx = jnp.arange(0, DIM_HEAD, 2, dtype=jnp.float32)
            inv_freq = 1.0 / 10000.0 ** (half_idx / DIM_HEAD)
            t = jnp.arange(n, dtype=jnp.float32)
            freqs = t[:, None] * inv_freq[None, :]
            freqs = jnp.concatenate([freqs, freqs], axis=-1)
            base = (half_idx + 0.4 * DIM_HEAD) / (1.4 * DIM_HEAD)
            power = (t - n // 2) / float(WINDOW // 2)
            scale = base[None, :] ** power[:, None]
            scale = jnp.concatenate([scale, scale], axis=-1)
            cos, sin = (jnp.cos(freqs), jnp.sin(freqs))
            q = q * cos * scale + rotate_half(q) * sin * scale
            k = k * cos / scale + rotate_half(k) * sin / scale
            return (q, k)

        def local_attention(q, k, v):
            b, h, n, d = q.shape
            w = n // WINDOW
            bq = q.reshape(b, h, w, WINDOW, d) * QK_SCALE
            bk = k.reshape(b, h, w, WINDOW, d)
            bv = v.reshape(b, h, w, WINDOW, d)

            def look_around(t):
                p = jnp.pad(t, ((0, 0), (0, 0), (1, 0), (0, 0), (0, 0)))
                return jnp.concatenate([p[:, :, :w], p[:, :, 1:]], axis=3)
            bk, bv = (look_around(bk), look_around(bv))
            bt = jnp.arange(n).reshape(w, WINDOW)
            btp = jnp.pad(bt, ((1, 0), (0, 0)), constant_values=-1)
            btk = jnp.concatenate([btp[:w], btp[1:]], axis=1)
            sim = jnp.einsum('bhwid,bhwjd->bhwij', bq, bk)
            i = bt[:, :, None]
            j = btk[:, None, :]
            mask = (i < j) | (i > j + WINDOW) | (j == -1)
            sim = jnp.where(mask, -jnp.finfo(sim.dtype).max, sim)
            attn = jax.nn.softmax(sim, axis=-1)
            out = jnp.einsum('bhwij,bhwjd->bhwid', attn, bv)
            return out.reshape(b, h, n, d)

        def _layer(x, wqkv, qs, ksc, wo, lg, lb, w1, b1, w2, b2):
            b, n, _ = x.shape
            h = shift_token(x)
            qkv = h @ wqkv
            q, k, v = jnp.split(qkv, 3, axis=-1)
            to_heads = lambda t: t.reshape(b, n, HEADS, DIM_HEAD).transpose(0, 2, 1, 3)
            q, k, v = (to_heads(q), to_heads(k), to_heads(v))
            q = l2norm(q) * qs
            k = l2norm(k) * ksc
            q, k = rotary_xpos(q, k)
            o = local_attention(q, k, v)
            o = o.transpose(0, 2, 1, 3).reshape(b, n, INNER)
            x = x + o @ wo
            h = shift_token(x)
            mu = h.mean(-1, keepdims=True)
            var = h.var(-1, keepdims=True)
            h = (h - mu) / jnp.sqrt(var + 1e-05) * lg + lb
            h = h @ w1 + b1
            a, g = jnp.split(h, 2, axis=-1)
            h = a * jax.nn.gelu(g, approximate=False)
            x = x + h @ w2 + b2
            return x
        for l in range(DEPTH):
            x = _layer(x, wqkv[l], q_scale[l], k_scale[l], wo[l], ln_g[l], ln_b[l], w1[l], b1[l], w2[l], b2[l])
        return x
    x = L0_attn_x
    xn = _layernorm(x, axis=-1)
    x = x + _L0_attn_ref(xn, L0_attn_Wq, L0_attn_Wk, L0_attn_Wv, L0_attn_Wo, L0_attn_bo, L0_attn_rel_pos_bias) + _L0_ffn_ref(xn, L0_ffn_wqkv, L0_ffn_q_scale, L0_ffn_k_scale, L0_ffn_wo, L0_ffn_ln_g, L0_ffn_ln_b, L0_ffn_w1, L0_ffn_b1, L0_ffn_w2, L0_ffn_b2)
    return x

_drawn_inputs = setup_inputs


def setup_inputs(seed=0):
    import zlib

    import numpy as np

    out = dict(_drawn_inputs(seed))
    spreads = {'L0_attn_bo': (0.0, 0.8),
     'L0_ffn_q_scale': (1.0, 0.6),
     'L0_ffn_k_scale': (1.0, 0.6),
     'L0_ffn_ln_g': (1.0, 0.6),
     'L0_ffn_ln_b': (0.0, 0.8),
     'L0_ffn_b1': (0.0, 0.8),
     'L0_ffn_b2': (0.0, 0.436)}
    factors = {'L0_attn_Wq': 4.413,
     'L0_attn_Wk': 4.458,
     'L0_attn_rel_pos_bias': 64.0,
     'L0_ffn_wqkv': 3.735,
     'L0_ffn_wo': 3.735,
     'L0_ffn_w1': 6.182,
     'L0_ffn_w2': 6.092}
    for name, (base, spread) in spreads.items():
        noise = np.random.default_rng([zlib.crc32(name.encode()), seed]).standard_normal(out[name].shape)
        drawn = base * np.exp(spread * noise) if base else spread * noise
        out[name] = jnp.asarray(drawn.astype(out[name].dtype))
    for name, factor in factors.items():
        out[name] = (out[name] * factor).astype(out[name].dtype)
    return out
```

```python
import numpy as np
import concourse.bass as bass
from concourse import mybir
from contextlib import ExitStack

F32 = mybir.dt.float32
ALU = mybir.AluOpType
ACT = mybir.ActivationFunctionType
AX = mybir.AxisListType

P = 128
B, T, D = 16, 512, 128
TT = T // P
NT = B * TT
H, DH = 16, 64
HP = H // 2
HD = H * DH
NREL = 128
EXT = 384
NEG = -1.0e30
LN_EPS = 1e-5
FH = 8
FI = FH * DH
FC = FI // P
WIN = 64
KEYS = P + WIN
HID = 341
CH = [128, 128, 85]
DEPTH = 2

LOFF = [0, 128, 384, 768]
LSZ = 1280
POFF = [0, 512, 896, 1152]
RING = 4
LAG = 2

AHEAD_ITEMS = {13: ["XT"], 14: ["Q0", "V0", "V1"], 15: ["K0", "V2", "V3"]}
SLOT_ITEMS = {0: ["Q1"], 1: ["K1"], 2: ["Q2", "V4"], 3: ["K2", "V5"], 4: ["Q3", "V6"], 5: ["K3", "V7"],
              6: ["Q4"], 7: ["K4"], 8: ["Q5"], 9: ["K5"], 10: ["Q6"], 11: ["K6"], 12: ["Q7"], 13: ["K7"]}
ORDER = [x for g in sorted(AHEAD_ITEMS) for x in AHEAD_ITEMS[g]] + \
        [x for g in sorted(SLOT_ITEMS) for x in SLOT_ITEMS[g]]
NI = len(ORDER)


def at(b, per, k):
    if isinstance(b, int):
        return max(per * b + k, 0)
    return b * per + k


def head_slots(eng, slot):
    for g in range(H):
        slot(0, g)
    with eng.Fori(1, B - 1) as b:
        for g in range(H):
            slot(b, g)
    for g in range(H):
        slot(B - 1, g)
    for g in range(LAG):
        slot(B, g)


def has_scores(b):
    return not isinstance(b, int) or b < B


def has_ahead(b):
    return not isinstance(b, int) or b < B - 1


def lagging(b, g, lag=LAG):
    if g >= lag:
        return b, g - lag
    if isinstance(b, int) and b == 0:
        return None
    return b - 1, g - lag + H


def slot_items(b, g):
    out = []
    if has_scores(b):
        out += [(x, b) for x in SLOT_ITEMS.get(g, [])]
    if has_ahead(b):
        out += [(x, b + 1) for x in AHEAD_ITEMS.get(g, [])]
    return out


def causal_attention(nc, c, x, Wq, Wk, Wv, Wo, bo, rel, ext_dram):
    acc, xf, ident, bank = c["acc"], c["xf"], c["ident"], c["bank"]
    with ExitStack() as ctx:
        def sb(name, shape, dt=F32):
            return ctx.enter_context(nc.sbuf_tensor(name, shape, dt))

        def sem(name):
            return ctx.enter_context(nc.semaphore(name))

        wq, wk, wv = sb("wq", [P, HD]), sb("wk", [P, HD]), sb("wv", [P, HD])
        wo = sb("wo", [P, HP, D])
        bo_b = sb("bo_b", [P, D])
        bias_tab = sb("bias_tab", [P, H, T])
        stats = sb("stats", [P, TT, 6])
        mv = sb("mv", [P, 2, TT, 2])
        ve = sb("ve", [P, 2, TT])
        rstd = sb("rstd", [P, 2, TT])
        mhalf = sb("mhalf", [P, TT])
        xs = sb("xs", [P, TT, D])
        xnT = sb("xnT", [P, T])
        qT = sb("qT", [P, 2, T])
        kT = sb("kT", [P, 2, T])
        v = sb("v", [P, TT, HD])
        L = sb("L", [P, RING, LSZ])
        nmax = sb("nmax", [P, RING, TT])
        rsum = sb("rsum", [P, RING, TT])
        rinv = sb("rinv", [P, RING, TT])
        PT = sb("PT", [P, 2, LSZ])
        OT = sb("OT", [P, HP, T])
        ext = PT[0:H, 0, 0:EXT]

        far_rows = OT[:].rearrange("p c t -> p (c t)")[:, 0:H * NREL]

        ps_scores, ps_probsT, ps_heads, ps_item = bank[0:2], bank[2:4], bank[4:6], bank[6:8]

        s_w = sem("weights_loaded")
        s_x = sem("x_loaded")
        s_rel = sem("rel_loaded")
        s_ext = sem("ext_built")
        s_extd = sem("ext_in_dram")
        s_tab = sem("bias_tab_loaded")
        s_gate_dve = sem("gate_dve")
        s_gate_pool = sem("gate_pool")
        s_far = sem("far_bias_filled")
        s_id0 = sem("ident_zeroed")
        s_id = sem("ident_built")
        s_mh = sem("mhalf_set")
        s_st = sem("stats_done")
        s_mv = sem("mean_var_done")
        s_ve = sem("var_eps_done")
        s_rstd = sem("rstd_done")
        s_xf = sem("xf_done")
        s_bo = sem("bo_added")
        s_xs = sem("batch_staged")
        s_item = sem("item_done")
        s_itev = sem("item_out")
        s_S = sem("scores_done")
        s_L = sem("logits_done")
        s_E = sem("exp_done")
        s_R = sem("rinv_done")
        s_N = sem("probs_done")
        s_T = sem("probsT_done")
        s_TE = sem("probsT_out")
        s_PV = sem("pv_done")
        s_O = sem("heads_out")
        s_out = sem("out_proj_done")

        block = ctx.enter_context(nc.Block())

        @block.sync
        def _(sp):
            xv = x.rearrange("b (t p) d -> p (b t) d", p=P)
            for q in range(4):
                sp.dma_start(acc[:, 16 * q:16 * q + 16, :], xv[:, 16 * q:16 * q + 16, :]).then_inc(s_x, 16)
            sp.wait_ge(s_ext, 3)
            sp.dma_start(ext_dram, ext.unsqueeze(1).to_broadcast([H, P, EXT])).then_inc(s_extd, 16)
            sp.wait_ge(s_extd, 16)
            toeplitz = bass.AP(ext_dram.tensor, P - 1, [[EXT - 1, P], [P * EXT, H], [1, 2 * P]])
            sp.dma_start(bias_tab[:, :, T - 2 * P:T], toeplitz).then_inc(s_tab, 16)
            sp.wait_ge(s_xf, NT)
            sp.dma_start(xs[:], xf[:, 0:TT, :]).then_inc(s_xs, 16)

            def stage(b):
                sp.wait_ge(s_item, at(b, NI, 1))
                sp.dma_start(xs[:], xf[:, bass.ds(b * TT + TT, TT), :]).then_inc(s_xs, 16)
            with sp.Fori(0, B - 1) as b:
                stage(b)

        @block.gpsimd
        def _(pool):
            nc.gpsimd.memset(ident[:], 0.0).then_inc(s_id0, 1)
            nc.gpsimd.memset(mhalf[:], -0.5).then_inc(s_mh, 1)
            pool.wait_ge(s_id0, 1)
            nc.gpsimd.affine_select(out=ident[:], in_=ident[:], compare_op=ALU.not_equal, fill=1.0, base=0,
                                    pattern=[[-1, P]], channel_multiplier=1).then_inc(s_id, 1)
            pool.wait_ge(s_mh, 1)
            with pool.Fori(0, B // 2) as i:
                for r in range(2):
                    pool.wait_ge(s_ve, i * 2 + (r + 1))
                    nc.gpsimd.tensor_tensor(rstd[:, r, :], ve[:, r, :], mhalf[:], ALU.pow).then_inc(s_rstd, 1)
            pool.wait_ge(s_xf, NT)
            pool.wait_ge(s_w, 16 * 5)
            for q in range(4):
                a = acc[:, 16 * q:16 * q + 16, :]
                nc.gpsimd.tensor_tensor(a, a, bo_b[:].unsqueeze(1).to_broadcast([P, 16, D]),
                                        ALU.add).then_inc(s_bo, 1)

            def slot(b, g):
                head = lagging(b, g, 1)
                if head is None or (isinstance(b, int) and b == B and g >= 1):
                    return
                hb, h = head
                pool.wait_ge(s_R, at(hb, H, h + 1))
                pool.sem_inc(s_gate_pool, 1)
                for i in range(TT):
                    a = L[:, h % RING, LOFF[i]:LOFF[i] + (i + 1) * P]
                    nc.gpsimd.tensor_scalar(a, a, rinv[:, h % RING, i:i + 1], 1.0, ALU.mult,
                                            ALU.mult).then_inc(s_N, 1)
            head_slots(pool, slot)

        @block.scalar
        def _(act):
            act.dma_start(wq[:], Wq).then_inc(s_w, 16)
            act.dma_start(wk[:], Wk).then_inc(s_w, 16)
            act.dma_start(wv[:], Wv).then_inc(s_w, 16)
            act.dma_start(wo[:], Wo.rearrange("(c p) n -> p c n", p=P)).then_inc(s_w, 16)
            act.dma_start(bo_b[:], bo.partition_broadcast(P)).then_inc(s_w, 16)
            act.dma_start(ext[:, P:P + NREL], rel).then_inc(s_rel, 16)
            act.dma_start(far_rows, bass.AP(rel.tensor, 0, [[0, P], [1, H * NREL]])).then_inc(s_rel, 16)

            def evacuate(name, b):
                k = ORDER.index(name)
                act.wait_ge(s_item, at(b, NI, k + 1))
                src = ps_item[k % 2][:]
                if name == "XT":
                    dst = xnT[:]
                elif name[0] in "QK":
                    p = int(name[1])
                    act.wait_ge(s_S, at(b, 4 * H, 8 * (p - 1)))
                    dst = (qT if name[0] == "Q" else kT)[:, p % 2, :]
                else:
                    half, t = divmod(int(name[1]), TT)
                    act.wait_ge(s_PV, at(b, 4 * H, 32 * (half + 1) - 4 * H))
                    dst = v[:, t, half * 512:half * 512 + 512]
                nc.scalar.activation(dst, src, ACT.Copy).then_inc(s_itev, 1)

            for g in sorted(AHEAD_ITEMS):
                for name in AHEAD_ITEMS[g]:
                    evacuate(name, 0)

            def slot(b, g):
                if not has_scores(b):
                    return
                items = slot_items(b, g)
                for i in range(TT):
                    act.wait_ge(s_L, at(b, 4 * H, 4 * g + i + 1))
                    a = L[:, g % RING, LOFF[i]:LOFF[i] + (i + 1) * P]
                    nc.scalar.activation(a, a, ACT.Exp, bias=nmax[:, g % RING, i:i + 1], scale=-1.0,
                                         accum_out=rsum[:, g % RING, i:i + 1]).then_inc(s_E, 1)
                    for item in {1: items[0:1], 2: items[1:2], 3: items[2:]}.get(i, []):
                        evacuate(*item)
            head_slots(act, slot)

        @block.vector
        def _(dve):
            def gate_dve():
                dve.sem_inc(s_gate_dve, 1)

            dve.wait_ge(s_rel, 32)
            nc.vector.tensor_copy(ext[:, 0:P], ext[:, P:P + 1].to_broadcast([H, P])).then_inc(s_ext, 1)
            nc.vector.memset(ext[:, P + NREL:EXT], NEG).then_inc(s_ext, 2)
            nc.vector.tensor_copy(bias_tab[:, :, 0:T - 2 * P],
                                  far_rows[:, ::NREL].unsqueeze(2).to_broadcast([P, H, T - 2 * P])).then_inc(s_far, 1)
            dve.wait_ge(s_x, 64)

            def statistics(b, r):
                for t in range(TT):
                    nc.vector.bn_stats(stats[:, t, :], acc[:, bass.ds(b * TT + t, 1), :].squeeze(1)).then_inc(s_st, 1)
                dve.wait_ge(s_st, b * TT + TT)
                gate_dve()
                for t in range(TT):
                    nc.vector.bn_aggr(mv[:, r, t, :], stats[:, t, :]).then_inc(s_mv, 1)
                dve.wait_ge(s_mv, b * TT + TT)
                nc.vector.tensor_scalar(ve[:, r, :], mv[:, r, :, 1], LN_EPS, None, ALU.add).then_inc(s_ve, 1)

            def normalise(b, r):
                dve.wait_ge(s_rstd, b + 1)
                for t in range(TT):
                    nc.vector.tensor_scalar(xf[:, bass.ds(b * TT + t, 1), :].squeeze(1),
                                            acc[:, bass.ds(b * TT + t, 1), :].squeeze(1),
                                            mv[:, r, t, 0:1], rstd[:, r, t:t + 1],
                                            ALU.subtract, ALU.mult).then_inc(s_xf, 1)
            statistics(0, 0)
            with dve.Fori(0, B // 2 - 1) as i:
                statistics(i * 2 + 1, 1)
                normalise(i * 2, 0)
                statistics(i * 2 + 2, 0)
                normalise(i * 2 + 1, 1)
            statistics(B - 1, 1)
            normalise(B - 2, 0)
            normalise(B - 1, 1)
            dve.wait_ge(s_far, 1)
            dve.wait_ge(s_tab, 16)

            def slot(b, g):
                tail = lagging(b, g)
                for i in range(TT):
                    if has_scores(b):
                        n = 4 * g + i
                        dve.wait_ge(s_S, at(b, 4 * H, n + 1))
                        if i == 0:
                            dve.wait_ge(s_T, at(b, 4 * H, 4 * (g - RING + 1)))
                        gate_dve()
                        nc.vector.tensor_tensor_reduce(
                            out=L[:, g % RING, LOFF[i]:LOFF[i] + (i + 1) * P], in0=ps_scores[i % 2][:, 0:(i + 1) * P],
                            in1=bias_tab[:, g, T - (i + 1) * P:T], scale=-1.0 / DH, scalar=3.0e38,
                            op0=ALU.add, op1=ALU.min, accum_out=nmax[:, g % RING, i:i + 1]).then_inc(s_L, 1)
                    if i == 1:
                        head = lagging(b, g, 1)
                        if head is not None and not (isinstance(b, int) and b == B and g >= 1):
                            hb, h = head
                            dve.wait_ge(s_E, at(hb, 4 * H, 4 * h + 4))
                            nc.vector.reciprocal(rinv[:, h % RING, :], rsum[:, h % RING, :]).then_inc(s_R, 1)
                    if tail is not None and i == 1 and tail[1] == 0:
                        add_batch(tail[0] - 1)
                    if tail is not None:
                        hb, h = tail
                        n = 4 * h + i
                        dve.wait_ge(s_T, at(hb, 4 * H, n + 1))
                        if i == 0:
                            dve.wait_ge(s_PV, at(hb, 4 * H, 4 * (h - 1)))
                        nc.vector.tensor_copy(PT[:, h % 2, POFF[i]:POFF[i] + T - i * P],
                                              ps_probsT[i % 2][:, 0:T - i * P]).then_inc(s_TE, 1)
                        if i == 3 and h % 2 == 1:
                            p = h // 2
                            dve.wait_ge(s_PV, at(hb, 4 * H, n + 1))
                            if p == 0:
                                dve.wait_ge(s_out, at(hb, 1, 0))
                            nc.vector.tensor_copy(OT[:, p, :], ps_heads[p % 2][:]).then_inc(s_O, 1)

            def add_batch(b):
                if isinstance(b, int) and b < 0:
                    return
                dve.wait_ge(s_out, at(b, 1, 1))
                if isinstance(b, int) and b == 0:
                    dve.wait_ge(s_bo, 4)
                a = acc[:, bass.ds(b * TT, TT), :]
                nc.vector.tensor_tensor(a, ps_heads[0][:].rearrange("p (t d) -> p t d", d=D), a,
                                        ALU.add).then_inc(s_O, 1)
            head_slots(dve, slot)
            add_batch(B - 1)

        @block.tensor
        def _(pe):
            pe.wait_ge(s_id, 1)
            pe.wait_ge(s_w, 16 * 5)

            def make(name, b):
                k = ORDER.index(name)
                pe.wait_ge(s_itev, at(b, NI, max(k - 1, 0)))
                out = ps_item[k % 2]
                if name == "XT":
                    pe.wait_ge(s_xs, at(b, 16, 16))
                    for t in range(TT):
                        last = nc.tensor.transpose(out[:, t * P:t * P + P], xs[:, t, :], ident[:])
                else:
                    pe.wait_ge(s_itev, at(b, NI, 1))
                    if name[0] in "QK":
                        p = int(name[1])
                        w = wq if name[0] == "Q" else wk
                        last = nc.tensor.matmul(out[:], w[:, p * P:p * P + P], xnT[:], start=True, stop=True)
                    else:
                        half, t = divmod(int(name[1]), TT)
                        last = nc.tensor.matmul(out[:], xnT[:, t * P:t * P + P], wv[:, half * 512:half * 512 + 512],
                                                start=True, stop=True)
                last.then_inc(s_item, 1)

            for g in sorted(AHEAD_ITEMS):
                for name in AHEAD_ITEMS[g]:
                    make(name, 0)

            def scores(b, g, i):
                p, r = g // 2, DH * (g % 2)
                n = 4 * g + i
                if g % 2 == 0 and i == 0:
                    pe.wait_ge(s_itev, at(b, NI, ORDER.index(f"K{p}") + 1))
                pe.wait_ge(s_L, at(b, 4 * H, n - 1))
                nc.tensor.matmul(ps_scores[i % 2][:, 0:(i + 1) * P], qT[r:r + DH, p % 2, i * P:i * P + P],
                                 kT[r:r + DH, p % 2, 0:(i + 1) * P], start=True, stop=True).then_inc(s_S, 1)

            def transposes(b, g, j):
                n = 4 * g + j
                if j == 0:
                    pe.wait_ge(s_N, at(b, 4 * H, 4 * g + 4))
                pe.wait_ge(s_TE, at(b, 4 * H, n - 1))
                for i in range(j, TT):
                    last = nc.tensor.transpose(ps_probsT[j % 2][:, (i - j) * P:(i - j) * P + P],
                                               L[:, g % RING, LOFF[i] + j * P:LOFF[i] + j * P + P], ident[:])
                last.then_inc(s_T, 1)

            def values(b, g, j):
                p, r = g // 2, DH * (g % 2)
                n = 4 * g + j
                pe.wait_ge(s_TE, at(b, 4 * H, n + 1))
                if j == 0 and g % 2 == 0:
                    pe.wait_ge(s_O, at(b, HP + 1, p - 1 if p else 0))
                if j == 0 and g % 8 == 0:
                    last_v = "V3" if g == 0 else "V7"
                    pe.wait_ge(s_itev, at(b, NI, ORDER.index(last_v) + 1))
                nc.tensor.matmul(ps_heads[p % 2][r:r + DH, j * P:T], v[:, j, g * DH:g * DH + DH],
                                 PT[:, g % 2, POFF[j]:POFF[j] + T - j * P], start=(j == 0),
                                 stop=(j == TT - 1)).then_inc(s_PV, 1)

            def out_projection(b):
                pe.wait_ge(s_O, at(b, HP + 1, HP))
                for t in range(TT):
                    for p in range(HP):
                        last = nc.tensor.matmul(ps_heads[0][:, t * D:t * D + D], OT[:, p, t * P:t * P + P],
                                                wo[:, p, :], start=(p == 0), stop=(p == HP - 1))
                last.then_inc(s_out, 1)

            def slot(b, g):
                tail = lagging(b, g)
                items = slot_items(b, g)
                if tail is not None and tail[1] == 0 and not (isinstance(b, int) and b == 0):
                    out_projection(tail[0] - 1)
                for i in range(TT):
                    if has_scores(b):
                        scores(b, g, i)
                    if tail is not None:
                        transposes(*tail, i)
                        if i > 0:
                            values(*tail, i - 1)
                    for item in {1: items[0:1], 2: items[1:2], 3: items[2:]}.get(i, []):
                        make(*item)
                if tail is not None:
                    values(*tail, TT - 1)
            head_slots(pe, slot)
            out_projection(B - 1)


def tile_slots(eng, slot, lag):
    for t in range(TT):
        slot(0, t)
    with eng.Fori(1, B - 1) as b:
        for t in range(TT):
            slot(b, t)
    for t in range(TT):
        slot(B - 1, t)
    for t in range(lag):
        slot(B, t)


def tile_back(b, t, lag):
    if isinstance(b, int) and b == 0 and t < lag:
        return None
    hb, ht = (b, t - lag) if t >= lag else (b - 1, t - lag + TT)
    if isinstance(hb, int) and hb >= B:
        return None
    return hb, ht


def batch_slots(eng, slot, lag):
    for b in range(lag):
        slot(b)
    with eng.Fori(lag, B) as b:
        slot(b)
    for b in range(B, B + lag):
        slot(b)


def batch_back(b, lag):
    if isinstance(b, int) and not 0 <= b - lag < B:
        return None
    return b - lag


def load_shifted(sp, hs, xf, b, t, s_hs):
    x_t = xf[:, bass.ds(b * TT + t, 1), :].squeeze(1)
    half = D // 2
    sp.dma_start(hs[:, t, 0:half], x_t[:, 0:half]).then_inc(s_hs, 16)
    sp.dma_start(hs[1:P, t, half:D], x_t[0:P - 1, half:D]).then_inc(s_hs, 16)
    if t > 0:
        x_p = xf[:, bass.ds(b * TT + t - 1, 1), :].squeeze(1)
        sp.dma_start(hs[0:1, t, half:D], x_p[P - 1:P, half:D]).then_inc(s_hs, 16)


def shifted_count(t):
    return 48 if t > 0 else 32


def load_attention_weights(eng, c, d, l, s):
    def row(a):
        return a[bass.ds(l, 1), :].partition_broadcast(P) if False else a[bass.ds(l, 1), :].to_broadcast([P, DH])
    eng.dma_start(c["wqkv"][:], d["wqkv"][bass.ds(l, 1), :, :].squeeze(0)).then_inc(s, 16)
    eng.dma_start(c["wo4"][:], d["wo"][bass.ds(l, 1), :, :].squeeze(0).rearrange("(c p) n -> p c n", p=P)).then_inc(s, 16)
    eng.dma_start(c["qk_scale"][:, 0, :], row(d["q_scale"])).then_inc(s, 16)
    eng.dma_start(c["qk_scale"][:, 1, :], row(d["k_scale"])).then_inc(s, 16)


def local_attention(nc, c, d, l, w):
    xf, ident, bank, hs, sem = c["xf"], c["ident"], c["bank"], c["hs"], w["attn"]
    ps_q, ps_k, ps_v, ps_s, ps_t, ps_o = bank[0], bank[1], bank[2], bank[3:5], bank[5:7], bank[7]
    hT, sq, ssq, rn, rq8 = w["hT"], w["sq"], w["ssq"], w["rn"], w["rq8"]
    qa, qb, kn, ka, kb = w["qa"], w["qb"], w["kn"], w["ka"], w["kb"]
    qr, kr, qT, kT, v, L, nmax, rsum, rinv, PT, OT = (w[n] for n in (
        "qr", "kr", "qT", "kT", "v", "L", "nmax", "rsum", "rinv", "PT", "OT"))
    tab, mask = w["tab"], w["mask"]

    block_ctx = nc.Block()
    block = block_ctx.__enter__()

    def first_key(t):
        return WIN if t == 0 else 0

    def Lh(par, h, lo, hi):
        o = WIN + h * KEYS
        return L[:, par, o + lo:o + hi]

    @block.sync
    def _(sp):
        def slot(b, t):
            if isinstance(b, int) and b >= B:
                return
            if not (isinstance(b, int) and b == 0):
                sp.wait_ge(sem["hT_done"], at(b, TT, t - TT + 1))
            load_shifted(sp, hs, xf, b, t, sem[f"hs{t}"])
        tile_slots(sp, slot, 0)
        s = sem["weights"]
        sp.dma_start(c["w1"][:], d["w1"][bass.ds(l, 1), :, :].squeeze(0)).then_inc(s, 16)
        sp.dma_start(c["w2"][:, 0:2, :], d["w2"][bass.ds(l, 1), 0:2 * P, :].squeeze(0).rearrange("(c p) n -> p c n", p=P)).then_inc(s, 16)
        sp.dma_start(c["w2"][0:CH[2], 2, :], d["w2"][bass.ds(l, 1), 2 * P:HID, :].squeeze(0)).then_inc(s, 16)
        sp.dma_start(c["w2"][CH[2]:CH[2] + 1, 2, :], d["b2"][bass.ds(l, 1), :]).then_inc(s, 16)
        with nc.allow_non_contiguous_dma(reason="a few columns, once a layer"):
            sp.dma_start(c["ln"][:, 0:1], d["ln_g"][bass.ds(l, 1), :].rearrange("l p -> p l")).then_inc(s, 16)
            sp.dma_start(c["ln"][:, 1:2], d["ln_b"][bass.ds(l, 1), :].rearrange("l p -> p l")).then_inc(s, 16)
            for part in range(2):
                for j in range(3):
                    o = part * HID + j * P
                    sp.dma_start(c["b1"][0:CH[j], part * 3 + j:part * 3 + j + 1],
                                 d["b1"][bass.ds(l, 1), o:o + CH[j]].rearrange("l p -> p l")).then_inc(s, 16)
        sp.wait_ge(s, 16 * 12)

    @block.gpsimd
    def _(pool):
        for n in w["mlp"].values():
            pool.sem_clear(n)
        for k in range(4):
            nc.gpsimd.tensor_tensor(tab[:, :, k, :], w["rope"][:, :, k, :],
                                    c["qk_scale"][:, k // 2, :].unsqueeze(1).to_broadcast([P, TT, DH]),
                                    ALU.mult).then_inc(sem["tab"], 1)
        pool.wait_ge(sem["tab"], 4)

        def halves(a, r):
            return a[:, :].rearrange("p (h r e) -> p h r e", h=FH, r=2)[:, :, r, :]

        def slot(b, t):
            tail = tile_back(b, t, 2)
            if tail is not None:
                tb, tt = tail
                lo = first_key(tt)
                for part in range(2):
                    pool.wait_ge(sem["rinv"], at(tb, TT, tt + 1))
                    h0 = part * 4
                    o = WIN + h0 * KEYS
                    a = L[:, tt % 2, o:o + 4 * KEYS].rearrange("p (h k) -> p h k", h=4)[:, :, lo:KEYS]
                    nc.gpsimd.tensor_tensor(a, a, rinv[:, tt % 2, h0:h0 + 4].unsqueeze(2).to_broadcast([P, 4, KEYS - lo]),
                                            ALU.mult).then_inc(sem["probs"], 1)
            if not isinstance(b, int) or b < B:
                r = t % 2
                pool.wait_ge(sem["ssq"], at(b, TT, t + 1))
                nc.gpsimd.tensor_tensor(rn[:, r, :], ssq[:, r, :], w["mhalf"][:], ALU.pow).then_inc(sem["rn"], 1)
                pool.wait_ge(sem["rn"], at(b, TT, t + 1))
                pool.wait_ge(sem["logits"], at(b, 8 * TT, 8 * (t - 1)))
                pool.sem_inc(w["gate_pool"], 1)
                nc.gpsimd.tensor_scalar(rq8[:, r, :], rn[:, r, 0:FH], -8.0, 1.0, ALU.mult, ALU.mult).then_inc(sem["rq8"], 1)
                pool.wait_ge(sem["qab"], at(b, TT, t + 1))
                pool.wait_ge(sem["qT_done"], at(b, TT, t))
                for s in range(2):
                    nc.gpsimd.tensor_tensor(halves(qr, s), halves(qa, s), halves(qb, 1 - s), ALU.add).then_inc(sem["qr"], 1)
                pool.wait_ge(sem["kn"], at(b, TT, t + 1))
                kn3 = kn[:].rearrange("p (h e) -> p h e", h=FH)
                for k, dst in ((2, ka), (3, kb)):
                    nc.gpsimd.tensor_tensor(dst[:].rearrange("p (h e) -> p h e", h=FH), kn3,
                                            tab[:, t, k, :].unsqueeze(1).to_broadcast([P, FH, DH]), ALU.mult).then_inc(sem["kab"], 1)
                pool.wait_ge(sem["kab"], at(b, 2 * TT, 2 * t + 2))
                pool.wait_ge(sem["kT_done"], at(b, TT, t))
                for s in range(2):
                    nc.gpsimd.tensor_tensor(halves(kr, s), halves(ka, s), halves(kb, 1 - s), ALU.add).then_inc(sem["kr"], 1)
        tile_slots(pool, slot, 2)

    @block.scalar
    def _(act):
        def slot(b, t):
            now = tile_back(b, t, 0)
            one = tile_back(b, t, 1)
            if now is not None:
                act.wait_ge(sem["hT_done"], at(b, TT, t + 1))
                nc.scalar.activation(hT[:, t % 2, :], ps_t[0][:, 0:P], ACT.Copy).then_inc(sem["hT_out"], 1)
            if one is not None:
                ob, ot = one
                act.wait_ge(sem["qT_done"], at(ob, TT, ot + 1))
                act.wait_ge(sem["scores"], at(ob, 8 * TT, 8 * ot))
                nc.scalar.activation(qT[:], ps_t[1][:], ACT.Copy).then_inc(sem["qT_out"], 1)
            for h in range(FH):
                if one is not None:
                    act.wait_ge(sem["logits"], at(ob, 8 * TT, 8 * ot + h + 1))
                    a = Lh(ot % 2, h, first_key(ot), KEYS)
                    nc.scalar.activation(a, a, ACT.Exp, bias=nmax[:, ot % 2, h:h + 1], scale=-1.0,
                                         accum_out=rsum[:, ot % 2, h:h + 1]).then_inc(sem["exp"], 1)
                if now is not None and h in (0, 2):
                    k = h // 2
                    act.wait_ge(sem["qkv_done"], at(b, 3 * TT, 3 * t + k + 1))
                    act.wait_ge(sem["ssq"], at(b, TT, t))
                    nc.scalar.activation(sq[:, k, :], (ps_q, ps_k)[k][:], ACT.Square).then_inc(sem["sq"], 1)
                if now is not None and h == 4:
                    act.wait_ge(sem["qkv_done"], at(b, 3 * TT, 3 * t + 3))
                    act.wait_ge(sem["pv_done"], at(b, 4 * TT, 4 * (t - 2)))
                    nc.scalar.activation(v[:, t, :], ps_v[:], ACT.Copy).then_inc(sem["v_out"], 1)
        tile_slots(act, slot, 1)

    @block.vector
    def _(dve):
        def gate():
            dve.sem_inc(w["gate_dve"], 1)
        dve.wait_ge(sem["tab"], 4)

        def slot(b, t):
            now, one, two, three = (tile_back(b, t, k) for k in range(4))
            if three is not None:
                xb, xt = three
                dve.wait_ge(sem["wo_done"], at(xb, TT, xt + 1))
                a = xf[:, bass.ds(xb * TT + xt, 1), :].squeeze(1)
                nc.vector.tensor_tensor(a, ps_o[:, 0:D], a, ALU.add).then_inc(sem["x_out"], 1)
            if two is not None:
                tb, tt = two
                dve.wait_ge(sem["exp"], at(tb, 8 * TT, 8 * tt + 8))
                nc.vector.reciprocal(rinv[:, tt % 2, :], rsum[:, tt % 2, :]).then_inc(sem["rinv"], 1)
            if one is not None:
                ob, ot = one
                dve.wait_ge(sem["kT_done"], at(ob, TT, ot + 1))
                if ot <= 1:
                    dve.wait_ge(sem["scores"], at(ob, 8 * TT, 0))
                nc.vector.tensor_copy(kT[:, :, ot * P:ot * P + P],
                                      ps_t[0][:].rearrange("p (c k) -> p c k", c=FC)).then_inc(sem["kT_out"], 1)

            def logits(h):
                if one is None:
                    return
                lo = first_key(ot)
                dve.wait_ge(sem["scores"], at(ob, 8 * TT, 8 * ot + h + 1))
                if h == 0:
                    dve.wait_ge(sem["PT_done"], at(ob, 4 * TT, 4 * (ot - 1)))
                    dve.wait_ge(sem["rq8"], at(ob, TT, ot + 1))
                gate()
                nc.vector.tensor_tensor_reduce(out=Lh(ot % 2, h, lo, KEYS), in0=ps_s[h % 2][:, lo:KEYS], in1=mask[:, lo:KEYS],
                                               scale=rq8[:, ot % 2, h:h + 1], scalar=3.0e38, op0=ALU.add, op1=ALU.min,
                                               accum_out=nmax[:, ot % 2, h:h + 1]).then_inc(sem["logits"], 1)

            def probs(k):
                if two is None:
                    return
                dve.wait_ge(sem["PT_done"], at(tb, 4 * TT, 4 * tt + k + 1))
                dve.wait_ge(sem["pv_done"], at(tb, 4 * TT, 4 * tt + k - 4))
                cols = KEYS if tt > 0 else P
                nc.vector.tensor_copy(PT[:, k, :, 0:cols], ps_t[(k + 1) % 2][:, 0:2 * KEYS].rearrange(
                    "p (a k) -> p a k", a=2)[:, :, 0:cols]).then_inc(sem["PT_out"], 1)

            def rope_q(k, dst):
                if now is None:
                    return
                if k == 0:
                    dve.wait_ge(sem["sq"], at(b, 2 * TT, 2 * t + 1))
                    dve.wait_ge(sem["qr"], at(b, 2 * TT, 2 * t))
                ins = nc.vector.tensor_tensor(dst[:].rearrange("p (h e) -> p h e", h=FH),
                                              ps_q[:].rearrange("p (h e) -> p h e", h=FH),
                                              tab[:, t, k, :].unsqueeze(1).to_broadcast([P, FH, DH]), ALU.mult)
                if k == 1:
                    ins.then_inc(sem["qab"], 1)

            def sums():
                if now is None:
                    return
                r = t % 2
                dve.wait_ge(sem["sq"], at(b, 2 * TT, 2 * t + 2))
                dve.wait_ge(sem["rn"], at(b, TT, t - 1))
                nc.vector.tensor_reduce(w["ssum"][:], sq[:].rearrange("p k (h e) -> p (k h) e", e=DH), AX.X, ALU.add).then_inc(sem["ssum"], 1)
                dve.wait_ge(sem["ssum"], at(b, TT, t + 1))
                nc.vector.tensor_scalar(ssq[:, r, :], w["ssum"][:], 1.0e-24, None, ALU.max).then_inc(sem["ssq"], 1)

            def norm_k():
                if now is None:
                    return
                r = t % 2
                dve.wait_ge(sem["rn"], at(b, TT, t + 1))
                dve.wait_ge(sem["kab"], at(b, 2 * TT, 2 * t))
                nc.vector.tensor_tensor(kn[:].rearrange("p (h e) -> p h e", h=FH),
                                        ps_k[:].rearrange("p (h e) -> p h e", h=FH),
                                        rn[:, r, FH:2 * FH].unsqueeze(2).to_broadcast([P, FH, DH]), ALU.mult).then_inc(sem["kn"], 1)

            logits(0)
            logits(1)
            rope_q(0, qa)
            probs(0)
            logits(2)
            rope_q(1, qb)
            logits(3)
            probs(1)
            sums()
            logits(4)
            logits(5)
            probs(2)
            norm_k()
            logits(6)
            logits(7)
            probs(3)
            if two is not None:
                dve.wait_ge(sem["pv_done"], at(tb, 4 * TT, 4 * tt + 4))
                dve.wait_ge(sem["wo_done"], at(tb, TT, tt))
                nc.vector.tensor_copy(OT[:], ps_o[:].rearrange("p (c q) -> p c q", c=FC)).then_inc(sem["OT_out"], 1)
        tile_slots(dve, slot, 3)

    @block.tensor
    def _(pe):
        def slot(b, t):
            now, one, two, three = (tile_back(b, t, k) for k in range(4))
            if three is not None:
                xb, xt = three
                pe.wait_ge(sem["OT_out"], at(xb, TT, xt + 1))
                for k in range(FC):
                    last = nc.tensor.matmul(ps_o[:, 0:D], OT[:, k, :], c["wo4"][:, k, :], start=(k == 0), stop=(k == FC - 1))
                last.then_inc(sem["wo_done"], 1)
            if now is not None:
                pe.wait_ge(sem[f"hs{t}"], at(b, shifted_count(t), shifted_count(t)))
                pe.wait_ge(sem["PT_out"], at(b, 4 * TT, 4 * (t - 2)))
                nc.tensor.transpose(ps_t[0][:, 0:P], hs[:, t, :], ident[:]).then_inc(sem["hT_done"], 1)
            if one is not None:
                ob, ot = one
                pe.wait_ge(sem["PT_out"], at(ob, 4 * TT, 4 * (ot - 1)))
                pe.wait_ge(sem["qr"], at(ob, 2 * TT, 2 * ot + 2))
                for k in range(FC):
                    last = nc.tensor.transpose(ps_t[1][:, k * P:k * P + P], qr[:, k * P:k * P + P], ident[:])
                last.then_inc(sem["qT_done"], 1)
                pe.wait_ge(sem["kr"], at(ob, 2 * TT, 2 * ot + 2))
                if now is not None:
                    pe.wait_ge(sem["hT_out"], at(b, TT, t + 1))
                for k in range(FC):
                    last = nc.tensor.transpose(ps_t[0][:, k * P:k * P + P], kr[:, k * P:k * P + P], ident[:])
                last.then_inc(sem["kT_done"], 1)
            if now is not None:
                pe.wait_ge(sem["hT_out"], at(b, TT, t + 1))
                pe.wait_ge(sem["sq"], at(b, 2 * TT, 2 * t))
                pe.wait_ge(sem["qab"], at(b, TT, t))
                pe.wait_ge(sem["kn"], at(b, TT, t))
                pe.wait_ge(sem["v_out"], at(b, TT, t))
                for k, ps in enumerate((ps_q, ps_k, ps_v)):
                    nc.tensor.matmul(ps[:], hT[:, t % 2, :], c["wqkv"][:, k * FI:k * FI + FI], start=True,
                                     stop=True).then_inc(sem["qkv_done"], 1)

            def scores(h):
                if one is None:
                    return
                k, r = h // 2, DH * (h % 2)
                if h == 0:
                    pe.wait_ge(sem["qT_out"], at(ob, TT, ot + 1))
                    pe.wait_ge(sem["kT_out"], at(ob, TT, ot + 1))
                pe.wait_ge(sem["logits"], at(ob, 8 * TT, 8 * ot + h - 1))
                lo = first_key(ot)
                nc.tensor.matmul(ps_s[h % 2][:, lo:KEYS], qT[r:r + DH, k, :],
                                 kT[r:r + DH, k, ot * P - WIN + lo:ot * P + P], start=True, stop=True).then_inc(sem["scores"], 1)

            def transposes(k):
                if two is None:
                    return
                tb, tt = two
                pe.wait_ge(sem["probs"], at(tb, 2 * TT, 2 * tt + 1 + k // 2))
                if k == 0 and one is not None:
                    pe.wait_ge(sem["qT_out"], at(ob, TT, ot + 1))
                if k == 1 and one is not None:
                    pe.wait_ge(sem["kT_out"], at(ob, TT, ot + 1))
                if k >= 2:
                    pe.wait_ge(sem["PT_out"], at(tb, 4 * TT, 4 * tt + k - 1))
                ps = ps_t[(k + 1) % 2]
                for a in range(2):
                    h = 2 * k + a
                    last = nc.tensor.transpose(ps[:, a * KEYS:a * KEYS + P], Lh(tt % 2, h, WIN, KEYS), ident[:])
                    if tt > 0:
                        last = nc.tensor.transpose(ps[:, a * KEYS + P:a * KEYS + KEYS], Lh(tt % 2, h, -WIN, WIN)[0:WIN],
                                                   ident[0:WIN, 0:WIN])
                last.then_inc(sem["PT_done"], 1)

            def values(k):
                if two is None:
                    return
                tb, tt = two
                if k == 0 and three is not None:
                    pe.wait_ge(sem["x_out"], at(three[0], TT, three[1] + 1))
                if k == 0:
                    pe.wait_ge(sem["v_out"], at(tb, TT, tt + 1))
                pe.wait_ge(sem["PT_out"], at(tb, 4 * TT, 4 * tt + k + 1))
                for a in range(2):
                    h, r = 2 * k + a, DH * a
                    last = nc.tensor.matmul(ps_o[r:r + DH, k * P:k * P + P], v[:, tt, h * DH:h * DH + DH],
                                            PT[:, k, a, 0:P], start=True, stop=(tt == 0))
                    if tt > 0:
                        last = nc.tensor.matmul(ps_o[r:r + DH, k * P:k * P + WIN], v[WIN:P, tt - 1, h * DH:h * DH + DH],
                                                PT[WIN:P, k, a, P:KEYS], start=False, stop=True)
                last.then_inc(sem["pv_done"], 1)

            scores(0)
            scores(1)
            transposes(0)
            scores(2)
            scores(3)
            transposes(1)
            values(0)
            scores(4)
            scores(5)
            transposes(2)
            values(1)
            scores(6)
            scores(7)
            transposes(3)
            values(2)
            values(3)
        tile_slots(pe, slot, 3)
    block_ctx.__exit__(None, None, None)


def gated_mlp(nc, c, d, l, w):
    xf, ident, bank, hs, sem = c["xf"], c["ident"], c["bank"], c["hs"], w["mlp"]
    ps_g, ps_a, ps_t, ps_y = bank[0:3], bank[3:6], bank[6], bank[7]
    stats, mv, ve, rstd, hn, hT, G, Hh = (w[n] for n in ("stats", "mv", "ve", "rstd", "hn", "mT", "G", "Hh"))

    block_ctx = nc.Block()
    block = block_ctx.__enter__()

    @block.sync
    def _(sp):
        load_attention_weights(sp, c, d, 1 - l, sem["weights"])

        def slot(b):
            for t in range(TT):
                if not (isinstance(b, int) and b == 0):
                    sp.wait_ge(sem["hn"], at(b, TT, t - TT + 1))
                load_shifted(sp, hs, xf, b, t, sem[f"hs{t}"])
        slot(0)
        with sp.Fori(1, B) as b:
            slot(b)
        sp.wait_ge(sem["weights"], 64)

    @block.gpsimd
    def _(pool):
        for n in w["attn"].values():
            pool.sem_clear(n)
        with pool.Fori(0, B) as b:
            pool.wait_ge(sem["ve"], b + 1)
            nc.gpsimd.tensor_tensor(rstd[:], ve[:], w["mhalf"][:, 0:TT], ALU.pow).then_inc(sem["rstd"], 1)

    @block.scalar
    def _(act):
        def slot(b):
            now, one = batch_back(b, 0), batch_back(b, 1)
            if one is not None:
                for j in range(3):
                    act.wait_ge(sem["ga_done"], at(one, 6, 2 * j + 1))
                    n = CH[j]
                    nc.scalar.activation(G[0:n, j, :], ps_g[j][0:n, :], ACT.Gelu, bias=c["b1"][0:n, 3 + j:4 + j]).then_inc(sem["gelu"], 1)
            if now is not None:
                act.wait_ge(sem["T_done"], at(b, 1, 1))
                nc.scalar.activation(hT[:], ps_t[:], ACT.Identity, scale=c["ln"][:, 0:1], bias=c["ln"][:, 1:2]).then_inc(sem["hT_out"], 1)
        batch_slots(act, slot, 1)

    @block.vector
    def _(dve):
        def gate():
            dve.sem_inc(w["gate_dve"], 1)

        def slot(b):
            now, one, two = (batch_back(b, k) for k in range(3))
            if now is not None:
                for t in range(TT):
                    dve.wait_ge(sem[f"hs{t}"], at(b, shifted_count(t), shifted_count(t)))
                    nc.vector.bn_stats(stats[:, t, :], hs[:, t, :]).then_inc(sem["stats"], 1)
                dve.wait_ge(sem["stats"], at(b, TT, TT))
                gate()
                for t in range(TT):
                    nc.vector.bn_aggr(mv[:, t, :], stats[:, t, :]).then_inc(sem["mv"], 1)
                dve.wait_ge(sem["mv"], at(b, TT, TT))
                nc.vector.tensor_scalar(ve[:], mv[:, :, 1], LN_EPS, None, ALU.add).then_inc(sem["ve"], 1)
            if two is not None:
                dve.wait_ge(sem["y_done"], at(two, 1, 1))
                a = xf[:, bass.ds(two * TT, TT), :]
                nc.vector.tensor_tensor(a, ps_y[:].rearrange("p (t d) -> p t d", d=D), a, ALU.add).then_inc(sem["x_out"], 1)
            if one is not None:
                for j in range(3):
                    n = CH[j]
                    dve.wait_ge(sem["gelu"], at(one, 3, j + 1))
                    dve.wait_ge(sem["ga_done"], at(one, 6, 2 * j + 2))
                    nc.vector.scalar_tensor_tensor(out=Hh[0:n, j, :], in0=ps_a[j][0:n, :], scalar=c["b1"][0:n, j:j + 1],
                                                   in1=G[0:n, j, :], op0=ALU.add, op1=ALU.mult).then_inc(sem["H"], 1)
            if now is not None:
                dve.wait_ge(sem["rstd"], at(b, 1, 1))
                dve.wait_ge(sem["T_done"], at(b, 1, 0))
                for t in range(TT):
                    nc.vector.tensor_scalar(hn[:, t, :], hs[:, t, :], mv[:, t, 0:1], rstd[:, t:t + 1],
                                            ALU.subtract, ALU.mult).then_inc(sem["hn"], 1)
        batch_slots(dve, slot, 2)

    @block.tensor
    def _(pe):
        def slot(b):
            now, one, two = (batch_back(b, k) for k in range(3))
            if two is not None:
                pe.wait_ge(sem["H"], at(two, 3, 3))
                if not (isinstance(two, int) and two == 0):
                    pe.wait_ge(sem["x_out"], at(two, 1, 0))
                for t in range(TT):
                    for j in range(3):
                        n = CH[j] + (1 if j == 2 else 0)
                        last = nc.tensor.matmul(ps_y[:, t * D:t * D + D], Hh[0:n, j, t * P:t * P + P], c["w2"][0:n, j, :],
                                                start=(j == 0), stop=(j == 2))
                last.then_inc(sem["y_done"], 1)
            if one is not None:
                pe.wait_ge(sem["hT_out"], at(one, 1, 1))
                for j in range(3):
                    n = CH[j]
                    for part, ps in ((1, ps_g[j]), (0, ps_a[j])):
                        o = part * HID + j * P
                        nc.tensor.matmul(ps[0:n, :], c["w1"][:, o:o + n], hT[:], start=True, stop=True).then_inc(sem["ga_done"], 1)
            if now is not None:
                pe.wait_ge(sem["hn"], at(b, TT, TT))
                for t in range(TT):
                    last = nc.tensor.transpose(ps_t[:, t * P:t * P + P], hn[:, t, :], ident[:])
                last.then_inc(sem["T_done"], 1)
        batch_slots(pe, slot, 2)
    block_ctx.__exit__(None, None, None)


ATTN_SEMS = ["hs0", "hs1", "hs2", "hs3", "weights", "tab", "hT_done", "hT_out", "qkv_done", "sq", "ssum", "ssq", "rn", "rq8",
             "qab", "qr", "kn", "kab", "kr", "qT_done", "qT_out", "kT_done", "kT_out", "scores", "logits", "exp", "rinv",
             "probs", "PT_done", "PT_out", "v_out", "pv_done", "OT_out", "wo_done", "x_out"]
MLP_SEMS = ["hs0", "hs1", "hs2", "hs3", "weights", "stats", "mv", "ve", "rstd", "hn", "T_done", "hT_out", "ga_done", "gelu", "H",
            "y_done", "x_out"]


def transformer(nc, c, d):
    with ExitStack() as ctx:
        w = {}

        def sb(name, shape, dt=F32):
            w[name] = ctx.enter_context(nc.sbuf_tensor("f_" + name, shape, dt))
            return w[name]
        c["hs"] = sb("hs", [P, TT, D])
        c["wqkv"] = sb("wqkv", [P, 3 * FI])
        c["wo4"] = sb("wo4", [P, FC, D])
        c["qk_scale"] = sb("qk_scale", [P, 2, DH])
        c["w1"] = sb("w1", [P, 2 * HID])
        c["w2"] = sb("w2", [P, 3, D])
        c["b1"] = sb("b1", [P, 6])
        c["ln"] = sb("ln", [P, 2])
        sb("rope", [P, TT, 4, DH]), sb("tab", [P, TT, 4, DH]), sb("mask", [P, KEYS]), sb("mhalf", [P, 2 * FH])
        sb("hT", [P, 2, P]), sb("sq", [P, 2, FI]), sb("ssum", [P, 2 * FH]), sb("ssq", [P, 2, 2 * FH])
        sb("rn", [P, 2, 2 * FH]), sb("rq8", [P, 2, FH])
        for n in ("qa", "qb", "kn", "ka", "kb", "qr", "kr"):
            sb(n, [P, FI])
        sb("qT", [P, FC, P]), sb("kT", [P, FC, T]), sb("v", [P, TT, FI])
        sb("L", [P, 2, WIN + FH * KEYS]), sb("nmax", [P, 2, FH]), sb("rsum", [P, 2, FH]), sb("rinv", [P, 2, FH])
        sb("PT", [P, FC, 2, KEYS]), sb("OT", [P, FC, P])
        sb("stats", [P, TT, 6]), sb("mv", [P, TT, 2]), sb("ve", [P, TT]), sb("rstd", [P, TT])
        sb("hn", [P, TT, D]), sb("mT", [P, T]), sb("G", [P, 3, T]), sb("Hh", [P, 3, T])
        w["attn"] = {n: ctx.enter_context(nc.semaphore("attn_" + n)) for n in ATTN_SEMS}
        w["mlp"] = {n: ctx.enter_context(nc.semaphore("mlp_" + n)) for n in MLP_SEMS}
        w["gate_dve"] = ctx.enter_context(nc.semaphore("gate2_dve"))
        w["gate_pool"] = ctx.enter_context(nc.semaphore("gate2_pool"))
        s_load = ctx.enter_context(nc.semaphore("layer0_loaded"))
        s_prep = ctx.enter_context(nc.semaphore("tables_set"))
        s_sum = ctx.enter_context(nc.semaphore("summed"))
        s_st = ctx.enter_context(nc.semaphore("stored"))

        with nc.Block() as block:
            @block.sync
            def _(sp):
                sp.dma_start(w["rope"][:], d["rope"].rearrange("(t p) k e -> p t k e", p=P)).then_inc(s_load, 16)
                load_attention_weights(sp, c, d, 0, s_load)
                sp.wait_ge(s_load, 80)

            @block.gpsimd
            def _(pool):
                nc.gpsimd.memset(w["mhalf"][:], -0.5).then_inc(s_prep, 1)
                nc.gpsimd.memset(w["L"][:], 0.0).then_inc(s_prep, 1)
                nc.gpsimd.memset(c["hs"][:], 0.0).then_inc(s_prep, 1)
                nc.gpsimd.memset(w["Hh"][:], 1.0).then_inc(s_prep, 1)
                nc.gpsimd.memset(w["mask"][:], 0.0).then_inc(s_prep, 1)
                pool.wait_ge(s_prep, 5)
                nc.gpsimd.affine_select(out=w["mask"][:], in_=w["mask"][:], compare_op=ALU.is_ge, fill=NEG, base=0,
                                        pattern=[[1, KEYS]], channel_multiplier=-1).then_inc(s_prep, 1)
                pool.wait_ge(s_prep, 6)
                nc.gpsimd.affine_select(out=w["mask"][:], in_=w["mask"][:], compare_op=ALU.is_ge, fill=NEG, base=WIN,
                                        pattern=[[-1, KEYS]], channel_multiplier=1).then_inc(s_prep, 1)
                pool.wait_ge(s_prep, 7)

        with nc.Fori(0, DEPTH) as l:
            local_attention(nc, c, d, l, w)
            gated_mlp(nc, c, d, l, w)

        with nc.Block() as block:
            @block.vector
            def _(dve):
                for q in range(4):
                    a = c["acc"][:, 16 * q:16 * q + 16, :]
                    nc.vector.tensor_tensor(a, a, c["xf"][:, 16 * q:16 * q + 16, :], ALU.add).then_inc(s_sum, 1)

            @block.sync
            def _(sp):
                ov = d["out"].rearrange("b (t p) d -> p (b t) d", p=P)
                for q in range(4):
                    sp.wait_ge(s_sum, q + 1)
                    sp.dma_start(ov[:, 16 * q:16 * q + 16, :], c["acc"][:, 16 * q:16 * q + 16, :]).then_inc(s_st, 16)
                sp.wait_ge(s_st, 64)


def rope_constants():
    f = np.float32
    half = np.arange(0, DH, 2, dtype=f)
    inv_freq = f(1.0) / np.power(f(10000.0), half / f(DH))
    t = np.arange(T, dtype=f)
    ang = t[:, None] * inv_freq[None, :].astype(f)
    base = (half + f(0.4 * DH)) / f(1.4 * DH)
    power = (t - T // 2) / f(WIN // 2)
    scale = np.power(base[None, :], power[:, None])
    cos, sin = np.cos(ang), np.sin(ang)
    both = lambda a, b: np.concatenate([a, b], axis=1).astype(f)
    return np.stack([both(cos * scale, cos * scale), both(sin * scale, -sin * scale),
                     both(cos / scale, cos / scale), both(sin / scale, -sin / scale)], axis=1)


def program(nc, x, Wq, Wk, Wv, Wo, bo, rel, wqkv, q_scale, k_scale, wo, ln_g, ln_b, w1, b1, w2, b2, rope, out, ext_dram):
    with ExitStack() as ctx:
        c = {"acc": ctx.enter_context(nc.sbuf_tensor("acc", [P, NT, D], F32)),
             "xf": ctx.enter_context(nc.sbuf_tensor("xf", [P, NT, D], F32)),
             "ident": ctx.enter_context(nc.sbuf_tensor("ident", [P, P], F32)),
             "bank": [ctx.enter_context(nc.psum_tensor(f"bank{i}", [P, 512], F32)) for i in range(8)]}
        d = {"wqkv": wqkv, "q_scale": q_scale, "k_scale": k_scale, "wo": wo, "ln_g": ln_g, "ln_b": ln_b,
             "w1": w1, "b1": b1, "w2": w2, "b2": b2, "rope": rope, "out": out}
        causal_attention(nc, c, x, Wq, Wk, Wv, Wo, bo, rel, ext_dram)
        transformer(nc, c, d)


_INS = ["L0_attn_x", "L0_attn_Wq", "L0_attn_Wk", "L0_attn_Wv", "L0_attn_Wo", "L0_attn_bo", "L0_attn_rel_pos_bias",
        "L0_ffn_wqkv", "L0_ffn_q_scale", "L0_ffn_k_scale", "L0_ffn_wo", "L0_ffn_ln_g", "L0_ffn_ln_b", "L0_ffn_w1",
        "L0_ffn_b1", "L0_ffn_w2", "L0_ffn_b2"]


def kernel(**inputs):
    import numpy as _np
    import concourse.bacc as _bacc
    from concourse import mybir as _mybir
    from concourse.bass_utils import run_bass_kernel_spmd as _run

    nc = _bacc.Bacc("TRN2", target_bir_lowering=False, num_devices=1)
    arrays, args = {}, []
    for name in _INS:
        a = _np.ascontiguousarray(inputs[name])
        arrays[f"in_{name}"] = a
        args.append(nc.dram_tensor(f"in_{name}", a.shape, _mybir.dt.from_np(a.dtype), kind="ExternalInput").ap())
    rope = rope_constants()
    arrays["rope"] = rope
    args.append(nc.dram_tensor("rope", rope.shape, _mybir.dt.float32, kind="ExternalInput").ap())
    args.append(nc.dram_tensor("out_0", (16, 512, 128), _mybir.dt.float32, kind="ExternalOutput").ap())
    args.append(nc.dram_tensor("bias_rows", (16, 128, 384), _mybir.dt.float32, kind="Internal").ap())
    program(nc, *args)
    r = _run(nc, [arrays], core_ids=[0])
    return r.results[0]["out_0"]
```

```python
import numpy as np
import concourse.bass as bass
from concourse import mybir
from contextlib import ExitStack

F32 = mybir.dt.float32
F32R = mybir.dt.float32r
ALU = mybir.AluOpType
ACT = mybir.ActivationFunctionType
AX = mybir.AxisListType

P = 128
B, T, D = 16, 512, 128
TT = T // P
NT = B * TT
H, DH = 16, 64
HP = H // 2
HD = H * DH
NREL = 128
EXT = 384
NEG = -1.0e30
LN_EPS = 1e-5
FH = 8
FI = FH * DH
FC = FI // P
WIN = 64
KEYS = P + WIN
HID = 341
CH = [128, 128, 85]
DEPTH = 2

LOFF = [0, 128, 384, 768]
LSZ = 1280
POFF = [0, 512, 896, 1152]
RING = 4
LAG = 2


def at(b, per, k):
    if isinstance(b, int):
        return max(per * b + k, 0)
    return b * per + k


AHEAD = {13: ["XT"], 14: ["V0", "V1"], 15: ["G0", "V2", "V3"]}
START = [n for g in sorted(AHEAD) for n in AHEAD[g]]


def slot_items(g, last):
    own = [f"G{g + 1}"] if g < H - 1 else []
    own += [f"V{g + 2}"] if 2 <= g <= 5 else []
    return [(n, False) for n in own] + ([] if last else [(n, True) for n in AHEAD.get(g, [])])


def item_sequence(last):
    return [x for g in range(H) for x in slot_items(g, last)]


def item_place(b, par, name, keep):
    start = [n for n in START if keep(n)]
    full = [x for x in item_sequence(False) if keep(x[0])]
    per = len(full)
    if name in START:
        if isinstance(b, int) and b == 0:
            return per, start.index(name)
        return per, len(start) - per + full.index((name, True))
    last = isinstance(b, int) and b == B - 1
    seq = [x for x in item_sequence(True) if keep(x[0])] if last else full
    return per, len(start) + seq.index((name, False))


def item_count(b, name, split=False):
    keep = (lambda n: n[0] in "XG") if split else (lambda n: True)
    per, off = item_place(b, 0, name, keep)
    return at(b, per, off + 1)


def item_bank(b, par, name):
    per, off = item_place(b, par, name, lambda n: True)
    return (per * par + off) % 2


def item_before(b, par, name):
    last = isinstance(b, int) and b == B - 1
    own_ahead = name in START
    if own_ahead and isinstance(b, int) and b == 0:
        k = START.index(name)
        return (0, START[k - 2]) if k >= 2 else None
    shift = -1 if own_ahead else 0
    seq = item_sequence(last and not own_ahead)
    k = seq.index((name, own_ahead))
    if k >= 2:
        n, a = seq[k - 2]
        return (shift + (1 if a else 0), n)
    if not own_ahead and isinstance(b, int) and b == 0:
        return (0, START[k - 2])
    n, a = item_sequence(False)[k - 2]
    return (shift - 1 + (1 if a else 0), n)


def head_slots(eng, slot, extra=0):
    for g in range(H):
        slot(0, g, 0)
    with eng.Fori(0, B // 2 - 1) as i:
        for g in range(H):
            slot(i * 2 + 1, g, 1)
        for g in range(H):
            slot(i * 2 + 2, g, 0)
    for g in range(H):
        slot(B - 1, g, 1)
    for g in range(extra):
        slot(B, g, 0)


def has_scores(b):
    return not isinstance(b, int) or b < B


def has_next(b):
    return not isinstance(b, int) or b < B - 1


def has_before(b):
    return not isinstance(b, int) or b > 0


def lagging(b, g, par, lag):
    if g >= lag:
        out = (b, g - lag, par)
    elif isinstance(b, int) and b == 0:
        return None
    else:
        out = (b - 1, g - lag + H, 1 - par)
    return None if isinstance(out[0], int) and out[0] >= B else out


def causal_attention(nc, c, x, Wq, Wk, Wv, Wo, bo, rel, out, ext_dram):
    xf, ident, bank = c["xf"], c["ident"], c["bank"]
    with ExitStack() as ctx:
        def sb(name, shape, dt=F32):
            return ctx.enter_context(nc.sbuf_tensor(name, shape, dt))

        def sem(name):
            return ctx.enter_context(nc.semaphore(name))

        m_hi, m_lo = sb("m_hi", [P, H, D], F32R), sb("m_lo", [P, H, D], F32R)
        wv_hi, wv_lo = sb("wv_hi", [P, HD], F32R), sb("wv_lo", [P, HD], F32R)
        wo_hi, wo_lo = sb("wo_hi", [P, HP, D], F32R), sb("wo_lo", [P, HP, D], F32R)
        bo_b = sb("bo_b", [P, D])
        bias_tab = sb("bias_tab", [P, H, T])
        stats = sb("stats", [P, TT, 6])
        mv = sb("mv", [P, TT, 2])
        ve = sb("ve", [P, TT])
        rstd = sb("rstd", [P, TT])
        mhalf = sb("mhalf", [P, TT])
        xb = sb("xb", [P, 2, TT, D])
        xn = sb("xn", [P, TT, D])
        xT_hi, xT_lo = sb("xT_hi", [P, 2, T], F32R), sb("xT_lo", [P, 2, T], F32R)
        g_hi, g_lo = sb("g_hi", [P, 2, T], F32R), sb("g_lo", [P, 2, T], F32R)
        v = sb("v", [P, TT, HD])
        L = sb("L", [P, RING, LSZ])
        nmax = sb("nmax", [P, RING, TT])
        rsum = sb("rsum", [P, RING, TT])
        rinv = sb("rinv", [P, RING, TT])
        PT = sb("PT", [P, 2, LSZ])
        o_hi, o_lo = sb("o_hi", [P, T], F32R), sb("o_lo", [P, T], F32R)
        yT = sb("yT", [P, T])
        ext = PT[0:H, 0, 0:EXT]
        far_rows = L[:].rearrange("p r k -> p (r k)")[:, 3072:3072 + H * NREL]
        raw = L[:].rearrange("p r k -> p (r k)")[:, 0:3 * HD]
        wqT, wkT = v[:, 0, :], v[:, 1, :]
        wo_raw = v[:, 2, :]

        ps_scores, ps_probsT, ps_heads, ps_y, ps_item = bank[0:2], bank[2:4], bank[4], bank[5], bank[6:8]

        s_wq = sem("wq_wk_loaded")
        s_wv = sem("wv_wo_loaded")
        s_wT = sem("w_transposed")
        s_wTe = sem("wT_out")
        s_m = sem("m_done")
        s_mhi = sem("m_hi_out")
        s_mlo = sem("m_lo_out")
        s_whi = sem("wv_wo_hi")
        s_wlo = sem("wv_wo_lo")
        s_x = [sem("x_loaded_even"), sem("x_loaded_odd")]
        s_bo_b = sem("bo_loaded")
        s_rel = sem("rel_loaded")
        s_ext = sem("ext_built")
        s_extd = sem("ext_in_dram")
        s_tab = sem("bias_tab_loaded")
        s_gate_dve = sem("gate_dve")
        s_gate_pool = sem("gate_pool")
        s_far = sem("far_bias_filled")
        s_id0 = sem("ident_zeroed")
        s_id = sem("ident_built")
        s_mh = sem("mhalf_set")
        s_st = sem("stats_done")
        s_mv = sem("mean_var_done")
        s_ve = sem("var_eps_done")
        s_rstd = sem("rstd_done")
        s_xn = sem("xn_done")
        s_xf = sem("xf_kept")
        s_xbo = sem("x_plus_bo")
        s_item = sem("item_done")
        s_ihi = sem("item_hi_out")
        s_ilo = sem("item_lo_out")
        s_S = sem("scores_done")
        s_L = sem("logits_done")
        s_E = sem("exp_done")
        s_R = sem("rinv_done")
        s_N = sem("probs_done")
        s_T = sem("probsT_done")
        s_TE = sem("probsT_out")
        s_PV = sem("pv_done")
        s_Oh = sem("heads_hi_out")
        s_Ol = sem("heads_lo_out")
        s_Y = sem("y_pair_done")
        s_yT = sem("yT_out")
        s_yb = sem("y_back_done")
        s_add = sem("batch_summed")
        s_out = sem("batch_stored")

        block = ctx.enter_context(nc.Block())
        xv = x.rearrange("b (t p) d -> p (b t) d", p=P)
        ov = out.rearrange("b (t p) d -> p (b t) d", p=P)

        @block.sync
        def _(sp):
            sp.dma_start(raw[:, 0:HD], Wq).then_inc(s_wq, 16)
            sp.dma_start(raw[:, HD:2 * HD], Wk).then_inc(s_wq, 16)
            sp.dma_start(xb[:, 0], xv[:, 0:TT, :]).then_inc(s_x[0], 16)
            sp.dma_start(raw[:, 2 * HD:3 * HD], Wv).then_inc(s_wv, 16)
            sp.dma_start(wo_raw.rearrange("p (c n) -> p c n", c=HP), Wo.rearrange("(c p) n -> p c n", p=P)).then_inc(s_wv, 16)
            sp.dma_start(xb[:, 1], xv[:, TT:2 * TT, :]).then_inc(s_x[1], 16)

            def turn(b, par):
                sp.wait_ge(s_add, at(b, 1, 1))
                sp.dma_start(ov[:, bass.ds(b * TT, TT), :], xb[:, par]).then_inc(s_out, 16)
                if isinstance(b, int) and b >= B - 2:
                    return
                sp.wait_ge(s_out, at(b, 16, 16))
                sp.dma_start(xb[:, par], xv[:, bass.ds(b * TT + 2 * TT, TT), :]).then_inc(s_x[par], 16)
            with sp.Fori(0, B // 2 - 1) as i:
                turn(i * 2, 0)
                turn(i * 2 + 1, 1)
            turn(B - 2, 0)
            turn(B - 1, 1)
            sp.wait_ge(s_out, 16 * B)

        @block.gpsimd
        def _(pool):
            nc.gpsimd.memset(ident[:], 0.0).then_inc(s_id0, 1)
            nc.gpsimd.memset(mhalf[:], -0.5).then_inc(s_mh, 1)
            pool.wait_ge(s_id0, 1)
            nc.gpsimd.affine_select(out=ident[:], in_=ident[:], compare_op=ALU.not_equal, fill=1.0, base=0,
                                    pattern=[[-1, P]], channel_multiplier=1).then_inc(s_id, 1)
            pool.wait_ge(s_mh, 1)

            def scale_of(b):
                pool.wait_ge(s_ve, at(b, 1, 1))
                nc.gpsimd.tensor_tensor(rstd[:], ve[:], mhalf[:], ALU.pow).then_inc(s_rstd, 1)

            def keep(b, par):
                pool.wait_ge(s_xn, at(b, TT, TT))
                nc.gpsimd.tensor_copy(xf[:, bass.ds(b * TT, TT), :], xn[:]).then_inc(s_xf, 1)
                pool.wait_ge(s_bo_b, 16)
                nc.gpsimd.tensor_tensor(xb[:, par], xb[:, par], bo_b[:].unsqueeze(1).to_broadcast([P, TT, D]),
                                        ALU.add).then_inc(s_xbo, 1)
            scale_of(0)
            pool.wait_ge(s_wv, 32)
            nc.gpsimd.tensor_copy(wv_hi[:], raw[:, 2 * HD:3 * HD]).then_inc(s_whi, 1)
            nc.gpsimd.tensor_copy(wo_hi[:].rearrange("p c n -> p (c n)"), wo_raw).then_inc(s_whi, 1)
            pool.wait_ge(s_whi, 2)
            nc.gpsimd.tensor_tensor(wv_lo[:], raw[:, 2 * HD:3 * HD], wv_hi[:].bitcast(F32), ALU.subtract).then_inc(s_wlo, 1)
            nc.gpsimd.tensor_tensor(wo_lo[:].rearrange("p c n -> p (c n)"), wo_raw,
                                    wo_hi[:].rearrange("p c n -> p (c n)").bitcast(F32), ALU.subtract).then_inc(s_wlo, 1)
            keep(0, 0)

            def slot(b, g, par):
                head = lagging(b, g, par, 1)
                if head is not None:
                    hb, h, _ = head
                    pool.wait_ge(s_R, at(hb, H, h + 1))
                    pool.sem_inc(s_gate_pool, 1)
                    for i in range(TT):
                        a = L[:, h % RING, LOFF[i]:LOFF[i] + (i + 1) * P]
                        nc.gpsimd.tensor_scalar(a, a, rinv[:, h % RING, i:i + 1], 1.0, ALU.mult,
                                                ALU.mult).then_inc(s_N, 1)
                if g == 9 and has_next(b):
                    scale_of(b + 1)
                if g == 12 and has_next(b):
                    keep(b + 1, 1 - par)
            head_slots(pool, slot, 1)

        @block.scalar
        def _(act):
            act.dma_start(ext[:, P:P + NREL], rel).then_inc(s_rel, 16)
            act.dma_start(far_rows, bass.AP(rel.tensor, 0, [[0, P], [1, H * NREL]])).then_inc(s_rel, 16)
            act.dma_start(bo_b[:], bo.partition_broadcast(P)).then_inc(s_bo_b, 16)
            act.wait_ge(s_ext, 3)
            act.dma_start(ext_dram, ext.unsqueeze(1).to_broadcast([H, P, EXT])).then_inc(s_extd, 16)
            for k in range(4):
                act.wait_ge(s_wT, k + 1)
                dst = (wqT, wkT)[k // 2]
                nc.scalar.activation(dst[:, (k % 2) * 512:(k % 2) * 512 + 512], ps_scores[k % 2][:],
                                     ACT.Copy).then_inc(s_wTe, 1)
            act.wait_ge(s_extd, 16)
            toeplitz = bass.AP(ext_dram.tensor, P - 1, [[EXT - 1, P], [P * EXT, H], [1, 2 * P]])
            act.dma_start(bias_tab[:, :, T - 2 * P:T], toeplitz).then_inc(s_tab, 16)
            for k in range(4):
                act.wait_ge(s_m, k + 1)
                nc.scalar.activation(m_hi[:, 8 * (k // 2) + k % 2:8 * (k // 2) + 8:2, :],
                                     ps_probsT[k % 2][:].rearrange("p (h d) -> p h d", d=D),
                                     ACT.Copy).then_inc(s_mhi, 1)

            def evacuate(name, b, par):
                act.wait_ge(s_item, item_count(b, name))
                src = ps_item[item_bank(b, par, name)][:]
                if name == "XT":
                    act.wait_ge(s_S, at(b, 4 * H, -4 * H))
                    dst = xT_hi[:, par, :]
                elif name[0] == "G":
                    g = int(name[1:])
                    act.wait_ge(s_S, at(b, 4 * H, 4 * (g - 1)))
                    dst = g_hi[:, g % 2, :]
                else:
                    half, t = divmod(int(name[1]), TT)
                    act.wait_ge(s_PV, at(b, 4 * H, 32 * (half + 1) - 4 * H))
                    dst = v[:, t, half * 512:half * 512 + 512]
                nc.scalar.activation(dst, src, ACT.Copy).then_inc(s_ihi, 1)

            for name in START:
                if name == "V0":
                    act.wait_ge(s_wlo, 2)
                    act.wait_ge(s_m, 4)
                evacuate(name, 0, 0)

            def slot(b, g, par):
                items = [(n, b + 1 if a else b, 1 - par if a else par) for n, a in slot_items(g, not has_next(b))] \
                    if has_scores(b) else []
                if g == 3 and has_before(b):
                    act.wait_ge(s_Y, at(b, HP, 0))
                    nc.scalar.activation(yT[:], ps_y[:], ACT.Copy).then_inc(s_yT, 1)
                done = lagging(b, g, par, 3)
                if done is not None and done[1] % 2 == 1:
                    hb, h, _ = done
                    act.wait_ge(s_PV, at(hb, 4 * H, 4 * h + 4))
                    act.wait_ge(s_Y, at(hb, HP, h // 2))
                    nc.scalar.activation(o_hi[:], ps_heads[:], ACT.Copy).then_inc(s_Oh, 1)
                for i in range(TT):
                    if has_scores(b):
                        act.wait_ge(s_L, at(b, 4 * H, 4 * g + i + 1))
                        a = L[:, g % RING, LOFF[i]:LOFF[i] + (i + 1) * P]
                        nc.scalar.activation(a, a, ACT.Exp, bias=nmax[:, g % RING, i:i + 1], scale=-1.0,
                                             accum_out=rsum[:, g % RING, i:i + 1]).then_inc(s_E, 1)
                    for item in {1: items[0:1], 2: items[1:2], 3: items[2:]}.get(i, []):
                        evacuate(*item)
            head_slots(act, slot, 4)

        @block.vector
        def _(dve):
            def gate_dve():
                dve.sem_inc(s_gate_dve, 1)

            def statistics(b, par):
                dve.wait_ge(s_x[par], at(b, 8, 16 - 8 * par) if not isinstance(b, int) else 16 * (b // 2 + 1))
                for t in range(TT):
                    nc.vector.bn_stats(stats[:, t, :], xb[:, par, t, :]).then_inc(s_st, 1)
                dve.wait_ge(s_st, at(b, TT, TT))
                gate_dve()
                for t in range(TT):
                    nc.vector.bn_aggr(mv[:, t, :], stats[:, t, :]).then_inc(s_mv, 1)
                dve.wait_ge(s_mv, at(b, TT, TT))
                nc.vector.tensor_scalar(ve[:], mv[:, :, 1], LN_EPS, None, ALU.add).then_inc(s_ve, 1)

            def normalise(b, par):
                dve.wait_ge(s_rstd, at(b, 1, 1))
                dve.wait_ge(s_xf, at(b, 1, 0))
                for t in range(TT):
                    nc.vector.tensor_scalar(xn[:, t, :], xb[:, par, t, :], mv[:, t, 0:1], rstd[:, t:t + 1],
                                            ALU.subtract, ALU.mult).then_inc(s_xn, 1)

            def low_part(name, b, par):
                dve.wait_ge(s_ihi, item_count(b, name))
                src = ps_item[item_bank(b, par, name)][:]
                hi, lo = (xT_hi[:, par, :], xT_lo[:, par, :]) if name == "XT" else \
                    (g_hi[:, int(name[1:]) % 2, :], g_lo[:, int(name[1:]) % 2, :])
                nc.vector.tensor_tensor(lo, src, hi.bitcast(F32), ALU.subtract).then_inc(s_ilo, 1)

            dve.wait_ge(s_rel, 32)
            nc.vector.tensor_copy(ext[:, 0:P], ext[:, P:P + 1].to_broadcast([H, P])).then_inc(s_ext, 1)
            nc.vector.memset(ext[:, P + NREL:EXT], NEG).then_inc(s_ext, 2)
            statistics(0, 0)
            normalise(0, 0)
            for k in range(4):
                dve.wait_ge(s_mhi, k + 1)
                four = slice(8 * (k // 2) + k % 2, 8 * (k // 2) + 8, 2)
                nc.vector.tensor_tensor(m_lo[:, four, :], ps_probsT[k % 2][:].rearrange("p (h d) -> p h d", d=D),
                                        m_hi[:, four, :].bitcast(F32), ALU.subtract).then_inc(s_mlo, 1)
            nc.vector.tensor_copy(bias_tab[:, :, 0:T - 2 * P],
                                  far_rows[:, ::NREL].unsqueeze(2).to_broadcast([P, H, T - 2 * P])).then_inc(s_far, 1)
            for name in START:
                if name[0] in "XG":
                    low_part(name, 0, 0)
            dve.wait_ge(s_far, 1)
            dve.wait_ge(s_wlo, 2)
            dve.wait_ge(s_wT, 4)
            dve.wait_ge(s_tab, 16)

            def slot(b, g, par):
                tail = lagging(b, g, par, LAG)
                items = [(n, b + 1 if a else b, 1 - par if a else par) for n, a in slot_items(g, not has_next(b))] \
                    if has_scores(b) else []

                def logits(i):
                    if not has_scores(b):
                        return
                    dve.wait_ge(s_S, at(b, 4 * H, 4 * g + i + 1))
                    if i == 0:
                        dve.wait_ge(s_T, at(b, 4 * H, 4 * (g - RING + 1)))
                    gate_dve()
                    nc.vector.tensor_tensor_reduce(
                        out=L[:, g % RING, LOFF[i]:LOFF[i] + (i + 1) * P], in0=ps_scores[i % 2][:, 0:(i + 1) * P],
                        in1=bias_tab[:, g, T - (i + 1) * P:T], scale=-1.0 / DH, scalar=3.0e38,
                        op0=ALU.add, op1=ALU.min, accum_out=nmax[:, g % RING, i:i + 1]).then_inc(s_L, 1)

                def probs(j):
                    if tail is None:
                        return
                    hb, h, _ = tail
                    dve.wait_ge(s_T, at(hb, 4 * H, 4 * h + j + 1))
                    if j == 0:
                        dve.wait_ge(s_PV, at(hb, 4 * H, 4 * (h - 1)))
                    nc.vector.tensor_copy(PT[:, h % 2, POFF[j]:POFF[j] + T - j * P],
                                          ps_probsT[j % 2][:, 0:T - j * P]).then_inc(s_TE, 1)

                probs(0)
                logits(0)
                head = lagging(b, g, par, 1)
                if head is not None:
                    hb, h, _ = head
                    dve.wait_ge(s_E, at(hb, 4 * H, 4 * h + 4))
                    nc.vector.reciprocal(rinv[:, h % RING, :], rsum[:, h % RING, :]).then_inc(s_R, 1)
                done = lagging(b, g, par, 3)
                if done is not None and done[1] % 2 == 1:
                    hb, h, _ = done
                    dve.wait_ge(s_Oh, at(hb, HP, h // 2 + 1))
                    nc.vector.tensor_tensor(o_lo[:], ps_heads[:], o_hi[:].bitcast(F32), ALU.subtract).then_inc(s_Ol, 1)
                logits(1)
                probs(1)
                logits(2)
                for n in items[0:1]:
                    if n[0][0] in "XG":
                        low_part(*n)
                probs(2)
                logits(3)
                probs(3)
                for n in items[1:]:
                    if n[0][0] in "XG":
                        low_part(*n)
                if g == 3 and has_before(b):
                    dve.wait_ge(s_yb, at(b, 1, 0))
                    dve.wait_ge(s_xbo, at(b, 1, 0))
                    a = xb[:, 1 - par]
                    nc.vector.tensor_tensor(a, ps_y[:].rearrange("p (t d) -> p t d", d=D), a, ALU.add).then_inc(s_add, 1)
                if g == 8 and has_next(b):
                    statistics(b + 1, 1 - par)
                if g == 10 and has_next(b):
                    normalise(b + 1, 1 - par)
            head_slots(dve, slot, 4)

        @block.tensor
        def _(pe):
            pe.wait_ge(s_id, 1)
            pe.wait_ge(s_wq, 32)
            for k in range(4):
                if k >= 2:
                    pe.wait_ge(s_wTe, k - 1)
                for n in range(4):
                    o = (k // 2) * HD + (k % 2) * 512 + n * P
                    last = nc.tensor.transpose(ps_scores[k % 2][:, n * P:n * P + P], raw[:, o:o + P], ident[:])
                last.then_inc(s_wT, 1)
            pe.wait_ge(s_wTe, 4)
            for k in range(4):
                if k >= 2:
                    pe.wait_ge(s_mlo, k - 1)
                for n in range(4):
                    h = 8 * (k // 2) + 2 * n + k % 2
                    r, o = DH * (h % 2), (h // 2) * P
                    last = nc.tensor.matmul(ps_probsT[k % 2][:, n * P:n * P + P], wqT[r:r + DH, o:o + P],
                                            wkT[r:r + DH, o:o + P], start=True, stop=True)
                last.then_inc(s_m, 1)

            def product(out, a, b, start=True, stop=True):
                nc.tensor.matmul(out, a[0], b[0], start=start, stop=False)
                nc.tensor.matmul(out, a[1], b[0], start=False, stop=False)
                return nc.tensor.matmul(out, a[0], b[1], start=False, stop=stop)

            def make(name, b, par):
                prior = item_before(b, par, name)
                if prior is not None:
                    pb, pn = b + prior[0], prior[1]
                    if pn[0] in "XG":
                        pe.wait_ge(s_ilo, item_count(pb, pn, True))
                    else:
                        pe.wait_ge(s_ihi, item_count(pb, pn))
                out = ps_item[item_bank(b, par, name)]
                if name == "XT":
                    pe.wait_ge(s_xn, at(b, TT, TT))
                    for t in range(TT):
                        last = nc.tensor.transpose(out[:, t * P:t * P + P], xn[:, t, :], ident[:])
                elif name[0] == "G":
                    g = int(name[1:])
                    if g == 0:
                        pe.wait_ge(s_ilo, item_count(b, "XT", True))
                    last = product(out[:], (m_hi[:, g, :], m_lo[:, g, :]), (xT_hi[:, par, :], xT_lo[:, par, :]))
                else:
                    half, t = divmod(int(name[1]), TT)
                    if int(name[1]) == 0:
                        pe.wait_ge(s_ilo, item_count(b, "XT", True))
                    tok, col = slice(t * P, t * P + P), slice(half * 512, half * 512 + 512)
                    last = product(out[:], (xT_hi[:, par, tok], xT_lo[:, par, tok]), (wv_hi[:, col], wv_lo[:, col]))
                last.then_inc(s_item, 1)

            pe.wait_ge(s_mlo, 4)
            pe.wait_ge(s_wlo, 2)
            for name in START:
                make(name, 0, 0)

            def slot(b, g, par):
                tail = lagging(b, g, par, LAG)
                items = [(n, b + 1 if a else b, 1 - par if a else par) for n, a in slot_items(g, not has_next(b))] \
                    if has_scores(b) else []

                def scores(i):
                    if not has_scores(b):
                        return
                    if i == 0:
                        pe.wait_ge(s_ilo, item_count(b, f"G{g}", True))
                    pe.wait_ge(s_L, at(b, 4 * H, 4 * g + i - 1))
                    q, keys = slice(i * P, i * P + P), slice(0, (i + 1) * P)
                    product(ps_scores[i % 2][:, keys], (g_hi[:, g % 2, q], g_lo[:, g % 2, q]),
                            (xT_hi[:, par, keys], xT_lo[:, par, keys])).then_inc(s_S, 1)

                def transposes(j):
                    if tail is None:
                        return
                    hb, h, _ = tail
                    if j == 0:
                        pe.wait_ge(s_N, at(hb, 4 * H, 4 * h + 4))
                    pe.wait_ge(s_TE, at(hb, 4 * H, 4 * h + j - 1))
                    for i in range(j, TT):
                        last = nc.tensor.transpose(ps_probsT[j % 2][:, (i - j) * P:(i - j) * P + P],
                                                   L[:, h % RING, LOFF[i] + j * P:LOFF[i] + j * P + P], ident[:])
                    last.then_inc(s_T, 1)

                def values(j, head):
                    if head is None:
                        return
                    hb, h, _ = head
                    r = DH * (h % 2)
                    pe.wait_ge(s_TE, at(hb, 4 * H, 4 * h + j + 1))
                    if j == 0 and h % 2 == 0:
                        pe.wait_ge(s_Ol, at(hb, HP, h // 2))
                    if j == 0 and h % 8 == 0:
                        pe.wait_ge(s_ihi, item_count(hb, "V3" if h == 0 else "V7"))
                    nc.tensor.matmul(ps_heads[r:r + DH, j * P:T], v[:, j, h * DH:h * DH + DH],
                                     PT[:, h % 2, POFF[j]:POFF[j] + T - j * P], start=(j == 0),
                                     stop=(j == TT - 1)).then_inc(s_PV, 1)

                def y_share():
                    done = lagging(b, g, par, 3)
                    if done is None or done[1] % 2 == 0:
                        return
                    hb, h, _ = done
                    p = h // 2
                    pe.wait_ge(s_Ol, at(hb, HP, p + 1))
                    if p == 0:
                        pe.wait_ge(s_add, at(hb, 1, 0))
                    product(ps_y[:], (wo_hi[:, p, :], wo_lo[:, p, :]), (o_hi[:], o_lo[:]),
                            start=(p == 0), stop=(p == HP - 1)).then_inc(s_Y, 1)

                transposes(0)
                values(2, lagging(b, g, par, LAG + 1))
                values(3, lagging(b, g, par, LAG + 1))
                scores(0)
                scores(1)
                transposes(1)
                for n in items[0:1]:
                    make(*n)
                scores(2)
                values(0, tail)
                transposes(2)
                y_share()
                values(1, tail)
                scores(3)
                transposes(3)
                for n in items[1:]:
                    make(*n)
                if g == 3 and has_before(b):
                    pe.wait_ge(s_yT, at(b, 1, 0))
                    for t in range(TT):
                        last = nc.tensor.transpose(ps_y[:, t * P:t * P + P], yT[:, t * P:t * P + P], ident[:])
                    last.then_inc(s_yb, 1)
            head_slots(pe, slot, 4)


def tile_slots(eng, slot, lag=TT + 1):
    for b in range(2):
        for t in range(TT):
            slot(b, t)
    with eng.Fori(2, B) as b:
        for t in range(TT):
            slot(b, t)
    for n in range(lag):
        slot(B + n // TT, n % TT)


def tile_back(b, t, lag):
    up, ht = divmod(t - lag, TT)
    hb = b + up if up else b
    if isinstance(hb, int) and not 0 <= hb < B:
        return None
    return hb, ht


def batch_slots(eng, slot, lag):
    for b in range(lag):
        slot(b)
    with eng.Fori(lag, B) as b:
        slot(b)
    for b in range(B, B + lag):
        slot(b)


def batch_back(b, lag):
    if isinstance(b, int) and not 0 <= b - lag < B:
        return None
    return b - lag


def load_shifted(sp, hs, xf, b, t, s_hs):
    x_t = xf[:, bass.ds(b * TT + t, 1), :].squeeze(1)
    half = D // 2
    sp.dma_start(hs[:, t, 0:half], x_t[:, 0:half]).then_inc(s_hs, 16)
    sp.dma_start(hs[1:P, t, half:D], x_t[0:P - 1, half:D]).then_inc(s_hs, 16)
    if t > 0:
        x_p = xf[:, bass.ds(b * TT + t - 1, 1), :].squeeze(1)
        sp.dma_start(hs[0:1, t, half:D], x_p[P - 1:P, half:D]).then_inc(s_hs, 16)


def shifted_count(t):
    return 48 if t > 0 else 32


def load_attention_weights(eng, c, d, l, s):
    def row(a):
        return a[bass.ds(l, 1), :].to_broadcast([P, DH])
    eng.dma_start(c["wqkv"][:], d["wqkv"][bass.ds(l, 1), :, :].squeeze(0)).then_inc(s, 16)
    eng.dma_start(c["wo4"][:], d["wo"][bass.ds(l, 1), :, :].squeeze(0).rearrange("(c p) n -> p c n", p=P)).then_inc(s, 16)
    eng.dma_start(c["qk_scale"][:, 0, :], row(d["q_scale"])).then_inc(s, 16)
    eng.dma_start(c["qk_scale"][:, 1, :], row(d["k_scale"])).then_inc(s, 16)


def local_attention(nc, c, d, l, w):
    xf, ident, bank, hs, sem = c["xf"], c["ident"], c["bank"], c["hs"], w["attn"]
    ps_q, ps_k, ps_v, ps_s, ps_t, ps_o = bank[0], bank[1], bank[2], bank[3:5], bank[5:7], bank[7]
    hT_hi, hT_lo, w_hi, w_lo = w["hT_hi"], w["hT_lo"], w["w_hi"], w["w_lo"]
    sq, ssq, rn, rq8 = w["sq"], w["ssq"], w["rn"], w["rq8"]
    qa, qb, ka, kb = w["qa"], w["qb"], w["ka"], w["kb"]
    qr, kr, qT, kT, v, L, nmax, rsum, rinv, PT, OT = (w[n] for n in (
        "qr", "kr", "qT", "kT", "v", "L", "nmax", "rsum", "rinv", "PT", "OT"))
    tab, mask = w["tab"], w["mask"]

    block_ctx = nc.Block()
    block = block_ctx.__enter__()

    def first_key(t):
        return WIN if t == 0 else 0

    def Lh(par, h, lo, hi):
        o = WIN + h * KEYS
        return L[:, par, o + lo:o + hi]

    def evacuate_PT(eng, copy, tile, k, how=()):
        tb, tt = tile
        cols = KEYS if tt > 0 else P
        eng.wait_ge(sem["PT_done"], at(tb, 4 * TT, 4 * tt + k + 1))
        eng.wait_ge(sem["pv_done"], at(tb, 4 * TT, 4 * tt + k - 3))
        copy(PT[:, k, :, 0:cols], ps_t[k % 2][:, 0:2 * KEYS].rearrange("p (a k) -> p a k", a=2)[:, :, 0:cols],
             *how).then_inc(sem[f"PT_out{k}"], 1)

    @block.sync
    def _(sp):
        def slot(b, t):
            if not (isinstance(b, int) and b == 0):
                sp.wait_ge(sem["hT_done"], at(b, TT, t - TT + 1))
            load_shifted(sp, hs, xf, b, t, sem[f"hs{t}"])
        tile_slots(sp, slot, lag=0)
        s = sem["weights"]
        sp.dma_start(c["w1"][:], d["w1"][bass.ds(l, 1), :, :].squeeze(0)).then_inc(s, 16)
        sp.dma_start(c["w2"][:, 0:2, :], d["w2"][bass.ds(l, 1), 0:2 * P, :].squeeze(0).rearrange("(c p) n -> p c n", p=P)).then_inc(s, 16)
        sp.dma_start(c["w2"][0:CH[2], 2, :], d["w2"][bass.ds(l, 1), 2 * P:HID, :].squeeze(0)).then_inc(s, 16)
        sp.dma_start(c["w2"][CH[2]:CH[2] + 1, 2, :], d["b2"][bass.ds(l, 1), :]).then_inc(s, 16)
        with nc.allow_non_contiguous_dma(reason="a few columns, once a layer"):
            sp.dma_start(c["ln"][:, 0:1], d["ln_g"][bass.ds(l, 1), :].rearrange("l p -> p l")).then_inc(s, 16)
            sp.dma_start(c["ln"][:, 1:2], d["ln_b"][bass.ds(l, 1), :].rearrange("l p -> p l")).then_inc(s, 16)
            for part in range(2):
                for j in range(3):
                    o = part * HID + j * P
                    sp.dma_start(c["b1"][0:CH[j], part * 3 + j:part * 3 + j + 1],
                                 d["b1"][bass.ds(l, 1), o:o + CH[j]].rearrange("l p -> p l")).then_inc(s, 16)
        sp.wait_ge(s, 16 * 12)

    ACT_HEADS = 4

    @block.gpsimd
    def _(pool):
        for n in w["mlp"].values():
            pool.sem_clear(n)
        for k in range(4):
            nc.gpsimd.tensor_tensor(tab[:, :, k, :], w["rope"][:, :, k, :],
                                    c["qk_scale"][:, k // 2, :].unsqueeze(1).to_broadcast([P, TT, DH]),
                                    ALU.mult).then_inc(sem["tab"], 1)

        def halves(a, r):
            return a.rearrange("p (h r e) -> p h r e", h=FH, r=2)[:, :, r, :]

        def slot(b, t):
            two, four = tile_back(b, t, 2), tile_back(b, t, 4)
            if four is not None:
                tb, tt = four
                lo = first_key(tt)
                n = FH - ACT_HEADS
                pool.wait_ge(sem["rinv"], at(tb, TT, tt + 1))
                o = WIN + ACT_HEADS * KEYS
                a = L[:, tt % 2, o:o + n * KEYS].rearrange("p (h k) -> p h k", h=n)[:, :, lo:KEYS]
                nc.gpsimd.tensor_tensor(a, a, rinv[:, tt % 2, ACT_HEADS:FH].unsqueeze(2).to_broadcast([P, n, KEYS - lo]),
                                        ALU.mult).then_inc(sem["probs_pool"], 1)
            if two is not None:
                tb, tt = two
                r = tt % 2
                pool.wait_ge(sem["qab"], at(tb, TT, tt + 1))
                pool.wait_ge(sem["qT_done"], at(tb, TT, tt))
                for s in range(2):
                    nc.gpsimd.tensor_tensor(halves(qr[:], s), halves(qa[:, r, :], s), halves(qb[:, r, :], 1 - s),
                                            ALU.add).then_inc(sem["qr"], 1)
                pool.wait_ge(sem["kab"], at(tb, TT, tt + 1))
                pool.wait_ge(sem["kT_done"], at(tb, TT, tt))
                for s in range(2):
                    nc.gpsimd.tensor_tensor(halves(kr[:], s), halves(ka[:, r, :], s), halves(kb[:, r, :], 1 - s),
                                            ALU.add).then_inc(sem["k_rotated"], 1)
                pool.wait_ge(sem["ssq"], at(tb, TT, tt + 1))
                nc.gpsimd.tensor_tensor(rn[:, r, :], ssq[:, r, :], w["mhalf"][:], ALU.pow).then_inc(sem["rn"], 1)
                pool.wait_ge(sem["rn"], at(tb, TT, tt + 1))
                pool.wait_ge(sem["k_rotated"], at(tb, 2 * TT, 2 * tt + 2))
                kr3 = kr[:].rearrange("p (h e) -> p h e", h=FH)
                nc.gpsimd.tensor_tensor(kr3, kr3, rn[:, r, FH:2 * FH].unsqueeze(2).to_broadcast([P, FH, DH]),
                                        ALU.mult).then_inc(sem["kr"], 1)
                pool.wait_ge(sem["logits"], at(tb, 8 * TT, 8 * (tt - 1)))
                pool.sem_inc(w["gate_pool"], 1)
                nc.gpsimd.tensor_scalar(rq8[:, r, :], rn[:, r, 0:FH], -8.0, 1.0, ALU.mult, ALU.mult).then_inc(sem["rq8"], 1)
        tile_slots(pool, slot)

    @block.scalar
    def _(act):
        def slot(b, t):
            now, one, two, three, four, five = (tile_back(b, t, k) for k in range(6))
            def square(k):
                if one is None:
                    return
                ib, it = one
                act.wait_ge(sem["qk_done"], at(ib, 2 * TT, 2 * it + k + 1))
                act.wait_ge(sem["ssq"], at(ib, TT, it - 1))
                nc.scalar.activation(sq[:, it % 2, k, :], (ps_q, ps_k)[k][:], ACT.Square).then_inc(sem["sq"], 1)

            if five is not None:
                xb, xt = five
                act.wait_ge(sem["pv_done"], at(xb, 4 * TT, 4 * xt + 4))
                act.wait_ge(sem["wo_done"], at(xb, TT, xt))
                nc.scalar.activation(OT[:], ps_o[:].rearrange("p (c q) -> p c q", c=FC), ACT.Copy).then_inc(sem["OT_out"], 1)
            square(0)
            if three is not None:
                ob, ot = three
                act.wait_ge(sem["qT_done"], at(ob, TT, ot + 1))
                act.wait_ge(sem["scores"], at(ob, 8 * TT, 8 * ot))
                nc.scalar.activation(qT[:], ps_t[0][:], ACT.Copy).then_inc(sem["qT_out"], 1)
                act.wait_ge(sem["kT_done"], at(ob, TT, ot + 1))
                nc.scalar.activation(kT[:, :, ot * P:ot * P + P], ps_t[1][:].rearrange("p (c k) -> p c k", c=FC),
                                     ACT.Copy).then_inc(sem["kT_out"], 1)

            def probs(h):
                if four is None:
                    return
                tb, tt = four
                act.wait_ge(sem["rinv"], at(tb, TT, tt + 1))
                a = Lh(tt % 2, h, first_key(tt), KEYS)
                nc.scalar.activation(a, a, ACT.Copy, scale=rinv[:, tt % 2, h:h + 1]).then_inc(sem["probs_act"], 1)

            def exps(h):
                if three is None:
                    return
                act.wait_ge(sem["logits"], at(ob, 8 * TT, 8 * ot + h + 1))
                a = Lh(ot % 2, h, first_key(ot), KEYS)
                nc.scalar.activation(a, a, ACT.Exp, bias=nmax[:, ot % 2, h:h + 1], scale=-1.0,
                                     accum_out=rsum[:, ot % 2, h:h + 1]).then_inc(sem["exp"], 1)

            probs(0)
            probs(1)
            square(1)
            exps(0)
            probs(2)
            probs(3)
            exps(1)
            if two is not None:
                vb, vt = two
                act.wait_ge(sem["v_done"], at(vb, TT, vt + 1))
                act.wait_ge(sem["pv_done"], at(vb, 4 * TT, 4 * (vt - 2)))
                nc.scalar.activation(v[:, vt, :], ps_v[:], ACT.Copy).then_inc(sem["v_out"], 1)
            exps(2)
            exps(3)
            if four is not None:
                evacuate_PT(act, nc.scalar.activation, four, 1, (ACT.Copy,))
            exps(4)
            exps(5)
            exps(6)
            if now is not None:
                act.wait_ge(sem["hT_done"], at(b, TT, t + 1))
                nc.scalar.activation(hT_hi[:, t % 2, :], ps_t[0][:, 0:P], ACT.Copy).then_inc(sem["hT_hi"], 1)
            exps(7)
        tile_slots(act, slot)

    @block.vector
    def _(dve):
        def gate():
            dve.sem_inc(w["gate_dve"], 1)

        nc.vector.tensor_copy(w_hi[:], c["wqkv"][:]).then_inc(sem["w_hi"], 1)
        dve.wait_ge(sem["w_hi"], 1)
        nc.vector.tensor_tensor(w_lo[:], c["wqkv"][:], w_hi[:].bitcast(F32), ALU.subtract).then_inc(sem["w_lo"], 1)
        dve.wait_ge(sem["tab"], 4)

        def slot(b, t):
            now, one, two, three, four, five = (tile_back(b, t, k) for k in range(6))

            def logits(h):
                if three is None:
                    return
                ob, ot = three
                lo = first_key(ot)
                dve.wait_ge(sem["scores"], at(ob, 8 * TT, 8 * ot + h + 1))
                if h == 0:
                    dve.wait_ge(sem["PT_done"], at(ob, 4 * TT, 4 * (ot - 1)))
                    dve.wait_ge(sem["rq8"], at(ob, TT, ot + 1))
                gate()
                nc.vector.tensor_tensor_reduce(out=Lh(ot % 2, h, lo, KEYS), in0=ps_s[h % 2][:, lo:KEYS], in1=mask[:, lo:KEYS],
                                               scale=rq8[:, ot % 2, h:h + 1], scalar=3.0e38, op0=ALU.add, op1=ALU.min,
                                               accum_out=nmax[:, ot % 2, h:h + 1]).then_inc(sem["logits"], 1)

            def table_product(k):
                if one is None:
                    return
                ib, it = one
                src, dst = (ps_q, ps_k)[k // 2], (qa, qb, ka, kb)[k]
                if k % 2 == 0:
                    dve.wait_ge(sem["sq"], at(ib, 2 * TT, 2 * it + 1 + k // 2))
                    dve.wait_ge(sem[("qr", "k_rotated")[k // 2]], at(ib, 2 * TT, 2 * (it - 1)))
                ins = nc.vector.tensor_tensor(dst[:, it % 2, :].rearrange("p (h e) -> p h e", h=FH),
                                              src[:].rearrange("p (h e) -> p h e", h=FH),
                                              tab[:, it, k, :].unsqueeze(1).to_broadcast([P, FH, DH]), ALU.mult)
                if k % 2 == 1:
                    ins.then_inc(sem[("qab", "kab")[k // 2]], 1)

            def sums():
                if two is None:
                    return
                ib, it = two
                dve.wait_ge(sem["sq"], at(ib, 2 * TT, 2 * it + 2))
                dve.wait_ge(sem["ssq"], at(ib, TT, it))
                nc.vector.tensor_reduce(w["ssum"][:], sq[:, it % 2].rearrange("p k (h e) -> p (k h) e", e=DH), AX.X,
                                        ALU.add).then_inc(sem["ssum"], 1)
                dve.wait_ge(sem["ssum"], at(ib, TT, it + 1))
                dve.wait_ge(sem["rn"], at(ib, TT, it - 1))
                nc.vector.tensor_scalar(ssq[:, it % 2, :], w["ssum"][:], 1.0e-24, None, ALU.max).then_inc(sem["ssq"], 1)

            def probsT(k):
                if four is not None:
                    evacuate_PT(dve, nc.vector.tensor_copy, four, k)

            if four is not None:
                tb, tt = four
                dve.wait_ge(sem["exp"], at(tb, 8 * TT, 8 * tt + 8))
                nc.vector.reciprocal(rinv[:, tt % 2, :], rsum[:, tt % 2, :]).then_inc(sem["rinv"], 1)
            sums()
            table_product(0)
            table_product(1)
            logits(0)
            logits(1)
            if five is not None:
                xb, xt = five
                dve.wait_ge(sem["wo_done"], at(xb, TT, xt + 1))
                a = xf[:, bass.ds(xb * TT + xt, 1), :].squeeze(1)
                nc.vector.tensor_tensor(a, ps_o[:, 0:D], a, ALU.add).then_inc(sem["x_out"], 1)
            probsT(0)
            logits(2)
            logits(3)
            table_product(2)
            logits(4)
            logits(5)
            probsT(2)
            table_product(3)
            logits(6)
            logits(7)
            if now is not None:
                dve.wait_ge(sem["hT_hi"], at(b, TT, t + 1))
                nc.vector.tensor_tensor(hT_lo[:, t % 2, :], ps_t[0][:, 0:P], hT_hi[:, t % 2, :].bitcast(F32),
                                        ALU.subtract).then_inc(sem["hT_lo"], 1)
            probsT(3)
        tile_slots(dve, slot)

    @block.tensor
    def _(pe):
        pe.wait_ge(sem["w_lo"], 1)

        def slot(b, t):
            now, one, two, three, four, five = (tile_back(b, t, k) for k in range(6))

            def project(k, ps):
                ib, it = one
                col = slice(k * FI, k * FI + FI)
                nc.tensor.matmul(ps[:], hT_hi[:, it % 2, :], w_hi[:, col], start=True, stop=False)
                nc.tensor.matmul(ps[:], hT_lo[:, it % 2, :], w_hi[:, col], start=False, stop=False)
                return nc.tensor.matmul(ps[:], hT_hi[:, it % 2, :], w_lo[:, col], start=False, stop=True)

            def scores(h):
                if three is None:
                    return
                ob, ot = three
                k, r = h // 2, DH * (h % 2)
                if h == 0:
                    pe.wait_ge(sem["qT_out"], at(ob, TT, ot + 1))
                    pe.wait_ge(sem["kT_out"], at(ob, TT, ot + 1))
                pe.wait_ge(sem["logits"], at(ob, 8 * TT, 8 * ot + h - 1))
                lo = first_key(ot)
                nc.tensor.matmul(ps_s[h % 2][:, lo:KEYS], qT[r:r + DH, k, :],
                                 kT[r:r + DH, k, ot * P - WIN + lo:ot * P + P], start=True, stop=True).then_inc(sem["scores"], 1)

            def transposes(k):
                if four is None:
                    return
                tb, tt = four
                if 2 * k < ACT_HEADS:
                    pe.wait_ge(sem["probs_act"], at(tb, ACT_HEADS * TT, ACT_HEADS * tt + 2 * k + 2))
                else:
                    pe.wait_ge(sem["probs_pool"], at(tb, TT, tt + 1))
                if k >= 2:
                    pe.wait_ge(sem[f"PT_out{k - 2}"], at(tb, TT, tt + 1))
                elif three is not None:
                    pe.wait_ge(sem[("qT_out", "kT_out")[k]], at(three[0], TT, three[1] + 1))
                elif five is not None:
                    pe.wait_ge(sem[f"PT_out{k + 2}"], at(five[0], TT, five[1] + 1))
                ps = ps_t[k % 2]
                for a in range(2):
                    h = 2 * k + a
                    last = nc.tensor.transpose(ps[:, a * KEYS:a * KEYS + P], Lh(tt % 2, h, WIN, KEYS), ident[:])
                    if tt > 0:
                        last = nc.tensor.transpose(ps[:, a * KEYS + P:a * KEYS + KEYS], Lh(tt % 2, h, -WIN, WIN)[0:WIN],
                                                   ident[0:WIN, 0:WIN])
                last.then_inc(sem["PT_done"], 1)

            def values(k):
                if four is None:
                    return
                tb, tt = four
                if k == 0:
                    pe.wait_ge(sem["v_out"], at(tb, TT, tt + 1))
                    if five is not None:
                        pe.wait_ge(sem["x_out"], at(five[0], TT, five[1] + 1))
                pe.wait_ge(sem[f"PT_out{k}"], at(tb, TT, tt + 1))
                for a in range(2):
                    h, r = 2 * k + a, DH * a
                    last = nc.tensor.matmul(ps_o[r:r + DH, k * P:k * P + P], v[:, tt, h * DH:h * DH + DH],
                                            PT[:, k, a, 0:P], start=True, stop=(tt == 0))
                    if tt > 0:
                        last = nc.tensor.matmul(ps_o[r:r + DH, k * P:k * P + WIN], v[WIN:P, tt - 1, h * DH:h * DH + DH],
                                                PT[WIN:P, k, a, P:KEYS], start=False, stop=True)
                last.then_inc(sem["pv_done"], 1)

            if one is not None:
                ib, it = one
                pe.wait_ge(sem["hT_lo"], at(ib, TT, it + 1))
                pe.wait_ge(sem["qab"], at(ib, TT, it))
                project(0, ps_q).then_inc(sem["qk_done"], 1)
            if three is not None:
                ob, ot = three
                if one is not None:
                    pe.wait_ge(sem["hT_lo"], at(one[0], TT, one[1] + 1))
                elif five is not None:
                    pe.wait_ge(sem["PT_out2"], at(five[0], TT, five[1] + 1))
                pe.wait_ge(sem["qr"], at(ob, 2 * TT, 2 * ot + 2))
                for k in range(FC):
                    last = nc.tensor.transpose(ps_t[0][:, k * P:k * P + P], qr[:, k * P:k * P + P], ident[:])
                last.then_inc(sem["qT_done"], 1)
                if five is not None:
                    pe.wait_ge(sem["PT_out3"], at(five[0], TT, five[1] + 1))
                pe.wait_ge(sem["kr"], at(ob, TT, ot + 1))
                for k in range(FC):
                    last = nc.tensor.transpose(ps_t[1][:, k * P:k * P + P], kr[:, k * P:k * P + P], ident[:])
                last.then_inc(sem["kT_done"], 1)
            if one is not None:
                pe.wait_ge(sem["kab"], at(ib, TT, it))
                project(1, ps_k).then_inc(sem["qk_done"], 1)
            scores(0)
            scores(1)
            if five is not None:
                xb, xt = five
                pe.wait_ge(sem["OT_out"], at(xb, TT, xt + 1))
                for k in range(FC):
                    last = nc.tensor.matmul(ps_o[:, 0:D], OT[:, k, :], c["wo4"][:, k, :], start=(k == 0), stop=(k == FC - 1))
                last.then_inc(sem["wo_done"], 1)
            transposes(0)
            scores(2)
            scores(3)
            transposes(1)
            values(0)
            scores(4)
            scores(5)
            transposes(2)
            values(1)
            scores(6)
            scores(7)
            if now is not None:
                pe.wait_ge(sem[f"hs{t}"], at(b, shifted_count(t), shifted_count(t)))
                if three is not None:
                    pe.wait_ge(sem["qT_out"], at(three[0], TT, three[1] + 1))
                if four is not None:
                    pe.wait_ge(sem["PT_out2"], at(four[0], TT, four[1] + 1))
                nc.tensor.transpose(ps_t[0][:, 0:P], hs[:, t, :], ident[:]).then_inc(sem["hT_done"], 1)
            transposes(3)
            values(2)
            if one is not None:
                pe.wait_ge(sem["v_out"], at(ib, TT, it))
                project(2, ps_v).then_inc(sem["v_done"], 1)
            values(3)
        tile_slots(pe, slot)
    block_ctx.__exit__(None, None, None)


def gated_mlp(nc, c, d, l, w):
    xf, ident, bank, hs, sem = c["xf"], c["ident"], c["bank"], c["hs"], w["mlp"]
    ps_g, ps_a, ps_t, ps_y = bank[0:3], bank[3:6], bank[6], bank[7]
    stats, mv, ve, rstd, hn, hT, G, Hh = (w[n] for n in ("stats", "mv", "ve", "rstd", "hn", "mT", "G", "Hh"))

    block_ctx = nc.Block()
    block = block_ctx.__enter__()

    @block.sync
    def _(sp):
        load_attention_weights(sp, c, d, 1 - l, sem["weights"])

        def slot(b):
            for t in range(TT):
                if not (isinstance(b, int) and b == 0):
                    sp.wait_ge(sem["hn"], at(b, TT, t - TT + 1))
                load_shifted(sp, hs, xf, b, t, sem[f"hs{t}"])
        slot(0)
        with sp.Fori(1, B) as b:
            slot(b)
        sp.wait_ge(sem["weights"], 64)

    @block.gpsimd
    def _(pool):
        for n in w["attn"].values():
            pool.sem_clear(n)
        with pool.Fori(0, B) as b:
            pool.wait_ge(sem["ve"], b + 1)
            nc.gpsimd.tensor_tensor(rstd[:], ve[:], w["mhalf"][:, 0:TT], ALU.pow).then_inc(sem["rstd"], 1)

    @block.scalar
    def _(act):
        def slot(b):
            now, one = batch_back(b, 0), batch_back(b, 1)
            if one is not None:
                for j in range(3):
                    act.wait_ge(sem["ga_done"], at(one, 6, 2 * j + 1))
                    n = CH[j]
                    nc.scalar.activation(G[0:n, j, :], ps_g[j][0:n, :], ACT.Gelu, bias=c["b1"][0:n, 3 + j:4 + j]).then_inc(sem["gelu"], 1)
            if now is not None:
                act.wait_ge(sem["T_done"], at(b, 1, 1))
                nc.scalar.activation(hT[:], ps_t[:], ACT.Identity, scale=c["ln"][:, 0:1], bias=c["ln"][:, 1:2]).then_inc(sem["hT_out"], 1)
        batch_slots(act, slot, 1)

    @block.vector
    def _(dve):
        def gate():
            dve.sem_inc(w["gate_dve"], 1)

        def slot(b):
            now, one, two = (batch_back(b, k) for k in range(3))
            if now is not None:
                for t in range(TT):
                    dve.wait_ge(sem[f"hs{t}"], at(b, shifted_count(t), shifted_count(t)))
                    nc.vector.bn_stats(stats[:, t, :], hs[:, t, :]).then_inc(sem["stats"], 1)
                dve.wait_ge(sem["stats"], at(b, TT, TT))
                gate()
                for t in range(TT):
                    nc.vector.bn_aggr(mv[:, t, :], stats[:, t, :]).then_inc(sem["mv"], 1)
                dve.wait_ge(sem["mv"], at(b, TT, TT))
                nc.vector.tensor_scalar(ve[:], mv[:, :, 1], LN_EPS, None, ALU.add).then_inc(sem["ve"], 1)
            if two is not None:
                dve.wait_ge(sem["y_done"], at(two, 1, 1))
                a = xf[:, bass.ds(two * TT, TT), :]
                nc.vector.tensor_tensor(a, ps_y[:].rearrange("p (t d) -> p t d", d=D), a, ALU.add).then_inc(sem["x_out"], 1)
            if one is not None:
                for j in range(3):
                    n = CH[j]
                    dve.wait_ge(sem["gelu"], at(one, 3, j + 1))
                    dve.wait_ge(sem["ga_done"], at(one, 6, 2 * j + 2))
                    nc.vector.scalar_tensor_tensor(out=Hh[0:n, j, :], in0=ps_a[j][0:n, :], scalar=c["b1"][0:n, j:j + 1],
                                                   in1=G[0:n, j, :], op0=ALU.add, op1=ALU.mult).then_inc(sem["H"], 1)
            if now is not None:
                dve.wait_ge(sem["rstd"], at(b, 1, 1))
                dve.wait_ge(sem["T_done"], at(b, 1, 0))
                for t in range(TT):
                    nc.vector.tensor_scalar(hn[:, t, :], hs[:, t, :], mv[:, t, 0:1], rstd[:, t:t + 1],
                                            ALU.subtract, ALU.mult).then_inc(sem["hn"], 1)
        batch_slots(dve, slot, 2)

    @block.tensor
    def _(pe):
        def slot(b):
            now, one, two = (batch_back(b, k) for k in range(3))
            if two is not None:
                pe.wait_ge(sem["H"], at(two, 3, 3))
                if not (isinstance(two, int) and two == 0):
                    pe.wait_ge(sem["x_out"], at(two, 1, 0))
                for t in range(TT):
                    for j in range(3):
                        n = CH[j] + (1 if j == 2 else 0)
                        last = nc.tensor.matmul(ps_y[:, t * D:t * D + D], Hh[0:n, j, t * P:t * P + P], c["w2"][0:n, j, :],
                                                start=(j == 0), stop=(j == 2))
                last.then_inc(sem["y_done"], 1)
            if one is not None:
                pe.wait_ge(sem["hT_out"], at(one, 1, 1))
                for j in range(3):
                    n = CH[j]
                    for part, ps in ((1, ps_g[j]), (0, ps_a[j])):
                        o = part * HID + j * P
                        nc.tensor.matmul(ps[0:n, :], c["w1"][:, o:o + n], hT[:], start=True, stop=True).then_inc(sem["ga_done"], 1)
            if now is not None:
                pe.wait_ge(sem["hn"], at(b, TT, TT))
                for t in range(TT):
                    last = nc.tensor.transpose(ps_t[:, t * P:t * P + P], hn[:, t, :], ident[:])
                last.then_inc(sem["T_done"], 1)
        batch_slots(pe, slot, 2)
    block_ctx.__exit__(None, None, None)


ATTN_SEMS = ["hs0", "hs1", "hs2", "hs3", "weights", "tab", "w_hi", "w_lo", "hT_done", "hT_hi", "hT_lo", "qk_done", "v_done",
             "v_out", "sq", "ssum", "ssq", "rn", "rq8", "qab", "qr", "kab", "k_rotated", "kr", "qT_done", "qT_out", "kT_done",
             "kT_out", "scores", "logits", "exp", "rinv", "probs_act", "probs_pool", "PT_done", "PT_out0", "PT_out1", "PT_out2",
             "PT_out3", "pv_done", "OT_out", "wo_done", "x_out"]
MLP_SEMS = ["hs0", "hs1", "hs2", "hs3", "weights", "stats", "mv", "ve", "rstd", "hn", "T_done", "hT_out", "ga_done", "gelu", "H",
            "y_done", "x_out"]


def transformer(nc, c, d):
    with ExitStack() as ctx:
        w = {}

        def sb(name, shape, dt=F32):
            w[name] = ctx.enter_context(nc.sbuf_tensor("f_" + name, shape, dt))
            return w[name]
        c["hs"] = sb("hs", [P, TT, D])
        c["wqkv"] = sb("wqkv", [P, 3 * FI])
        c["wo4"] = sb("wo4", [P, FC, D])
        c["qk_scale"] = sb("qk_scale", [P, 2, DH])
        c["w1"] = sb("w1", [P, 2 * HID])
        c["w2"] = sb("w2", [P, 3, D])
        c["b1"] = sb("b1", [P, 6])
        c["ln"] = sb("ln", [P, 2])
        acc = sb("acc", [P, NT, D])
        sb("rope", [P, TT, 4, DH]), sb("tab", [P, TT, 4, DH]), sb("mask", [P, KEYS]), sb("mhalf", [P, 2 * FH])
        sb("w_hi", [P, 3 * FI], F32R), sb("w_lo", [P, 3 * FI], F32R)
        sb("hT_hi", [P, 2, P], F32R), sb("hT_lo", [P, 2, P], F32R)
        sb("sq", [P, 2, 2, FI]), sb("ssum", [P, 2 * FH]), sb("ssq", [P, 2, 2 * FH])
        sb("rn", [P, 2, 2 * FH]), sb("rq8", [P, 2, FH])
        for n in ("qa", "qb", "ka", "kb"):
            sb(n, [P, 2, FI])
        sb("qr", [P, FI]), sb("kr", [P, FI])
        sb("qT", [P, FC, P]), sb("kT", [P, FC, T]), sb("v", [P, TT, FI])
        sb("L", [P, 2, WIN + FH * KEYS]), sb("nmax", [P, 2, FH]), sb("rsum", [P, 2, FH]), sb("rinv", [P, 2, FH])
        sb("PT", [P, FC, 2, KEYS]), sb("OT", [P, FC, P])
        sb("stats", [P, TT, 6]), sb("mv", [P, TT, 2]), sb("ve", [P, TT]), sb("rstd", [P, TT])
        sb("hn", [P, TT, D]), sb("mT", [P, T]), sb("G", [P, 3, T]), sb("Hh", [P, 3, T])
        w["attn"] = {n: ctx.enter_context(nc.semaphore("attn_" + n)) for n in ATTN_SEMS}
        w["mlp"] = {n: ctx.enter_context(nc.semaphore("mlp_" + n)) for n in MLP_SEMS}
        w["gate_dve"] = ctx.enter_context(nc.semaphore("gate2_dve"))
        w["gate_pool"] = ctx.enter_context(nc.semaphore("gate2_pool"))
        s_acc = ctx.enter_context(nc.semaphore("out_read_back"))
        s_load = ctx.enter_context(nc.semaphore("layer0_loaded"))
        s_prep = ctx.enter_context(nc.semaphore("tables_set"))
        s_sum = ctx.enter_context(nc.semaphore("summed"))
        s_st = ctx.enter_context(nc.semaphore("stored"))

        with nc.Block() as block:
            @block.sync
            def _(sp):
                sp.dma_start(w["rope"][:], d["rope"].rearrange("(t p) k e -> p t k e", p=P)).then_inc(s_load, 16)
                load_attention_weights(sp, c, d, 0, s_load)
                sp.dma_start(acc[:], d["out"].rearrange("b (t p) d -> p (b t) d", p=P)).then_inc(s_acc, 16)
                sp.wait_ge(s_load, 80)

            @block.gpsimd
            def _(pool):
                nc.gpsimd.memset(w["mhalf"][:], -0.5).then_inc(s_prep, 1)
                nc.gpsimd.memset(w["L"][:], 0.0).then_inc(s_prep, 1)
                nc.gpsimd.memset(c["hs"][:], 0.0).then_inc(s_prep, 1)
                nc.gpsimd.memset(w["Hh"][:], 1.0).then_inc(s_prep, 1)
                nc.gpsimd.memset(w["mask"][:], 0.0).then_inc(s_prep, 1)
                pool.wait_ge(s_prep, 5)
                nc.gpsimd.affine_select(out=w["mask"][:], in_=w["mask"][:], compare_op=ALU.is_ge, fill=NEG, base=0,
                                        pattern=[[1, KEYS]], channel_multiplier=-1).then_inc(s_prep, 1)
                pool.wait_ge(s_prep, 6)
                nc.gpsimd.affine_select(out=w["mask"][:], in_=w["mask"][:], compare_op=ALU.is_ge, fill=NEG, base=WIN,
                                        pattern=[[-1, KEYS]], channel_multiplier=1).then_inc(s_prep, 1)
                pool.wait_ge(s_prep, 7)

        with nc.Fori(0, DEPTH) as l:
            local_attention(nc, c, d, l, w)
            gated_mlp(nc, c, d, l, w)

        with nc.Block() as block:
            @block.vector
            def _(dve):
                dve.wait_ge(s_acc, 16)
                for q in range(4):
                    a = acc[:, 16 * q:16 * q + 16, :]
                    nc.vector.tensor_tensor(a, a, c["xf"][:, 16 * q:16 * q + 16, :], ALU.add).then_inc(s_sum, 1)

            @block.sync
            def _(sp):
                ov = d["out"].rearrange("b (t p) d -> p (b t) d", p=P)
                for q in range(4):
                    sp.wait_ge(s_sum, q + 1)
                    sp.dma_start(ov[:, 16 * q:16 * q + 16, :], acc[:, 16 * q:16 * q + 16, :]).then_inc(s_st, 16)
                sp.wait_ge(s_st, 64)


def rope_constants():
    f = np.float32
    half = np.arange(0, DH, 2, dtype=f)
    inv_freq = f(1.0) / np.power(f(10000.0), half / f(DH))
    t = np.arange(T, dtype=f)
    ang = t[:, None] * inv_freq[None, :].astype(f)
    base = (half + f(0.4 * DH)) / f(1.4 * DH)
    power = (t - T // 2) / f(WIN // 2)
    scale = np.power(base[None, :], power[:, None])
    cos, sin = np.cos(ang), np.sin(ang)
    both = lambda a, b: np.concatenate([a, b], axis=1).astype(f)
    return np.stack([both(cos * scale, cos * scale), both(sin * scale, -sin * scale),
                     both(cos / scale, cos / scale), both(sin / scale, -sin / scale)], axis=1)


def program(nc, x, Wq, Wk, Wv, Wo, bo, rel, wqkv, q_scale, k_scale, wo, ln_g, ln_b, w1, b1, w2, b2, rope, out, ext_dram):
    with ExitStack() as ctx:
        c = {"xf": ctx.enter_context(nc.sbuf_tensor("xf", [P, NT, D], F32)),
             "ident": ctx.enter_context(nc.sbuf_tensor("ident", [P, P], F32)),
             "bank": [ctx.enter_context(nc.psum_tensor(f"bank{i}", [P, 512], F32)) for i in range(8)]}
        d = {"wqkv": wqkv, "q_scale": q_scale, "k_scale": k_scale, "wo": wo, "ln_g": ln_g, "ln_b": ln_b,
             "w1": w1, "b1": b1, "w2": w2, "b2": b2, "rope": rope, "out": out}
        causal_attention(nc, c, x, Wq, Wk, Wv, Wo, bo, rel, out, ext_dram)
        transformer(nc, c, d)


_INS = ["L0_attn_x", "L0_attn_Wq", "L0_attn_Wk", "L0_attn_Wv", "L0_attn_Wo", "L0_attn_bo", "L0_attn_rel_pos_bias",
        "L0_ffn_wqkv", "L0_ffn_q_scale", "L0_ffn_k_scale", "L0_ffn_wo", "L0_ffn_ln_g", "L0_ffn_ln_b", "L0_ffn_w1",
        "L0_ffn_b1", "L0_ffn_w2", "L0_ffn_b2"]


def kernel(**inputs):
    import numpy as _np
    import concourse.bacc as _bacc
    from concourse import mybir as _mybir
    from concourse.bass_utils import run_bass_kernel_spmd as _run

    nc = _bacc.Bacc("TRN2", target_bir_lowering=False, num_devices=1)
    arrays, args = {}, []
    for name in _INS:
        a = _np.ascontiguousarray(inputs[name])
        arrays[f"in_{name}"] = a
        args.append(nc.dram_tensor(f"in_{name}", a.shape, _mybir.dt.from_np(a.dtype), kind="ExternalInput").ap())
    rope = rope_constants()
    arrays["rope"] = rope
    args.append(nc.dram_tensor("rope", rope.shape, _mybir.dt.float32, kind="ExternalInput").ap())
    args.append(nc.dram_tensor("out_0", (16, 512, 128), _mybir.dt.float32, kind="ExternalOutput").ap())
    args.append(nc.dram_tensor("bias_rows", (16, 128, 384), _mybir.dt.float32, kind="Internal").ap())
    program(nc, *args)
    r = _run(nc, [arrays], core_ids=[0])
    return r.results[0]["out_0"]
```

```python
import numpy as np
import concourse.bass as bass
from concourse import mybir
from contextlib import ExitStack

F32 = mybir.dt.float32
F32R = mybir.dt.float32r
ALU = mybir.AluOpType
ACT = mybir.ActivationFunctionType
AX = mybir.AxisListType

P = 128
B, T, D = 16, 512, 128
TT = T // P
NT = B * TT
H, DH = 16, 64
HP = H // 2
HD = H * DH
NREL = 128
EXT = 384
NEG = -1.0e30
LN_EPS = 1e-5
FH = 8
FI = FH * DH
FC = FI // P
WIN = 64
HID = 341
CH = [128, 128, 85]
DEPTH = 2

LOFF = [0, 128, 384, 768]
LSZ = 1280
POFF = [0, 512, 896, 1152]
RING = 4
LAG = 2


def at(b, per, k):
    if isinstance(b, int):
        return max(per * b + k, 0)
    return b * per + k


AHEAD = {13: ["XT"], 14: ["V0", "V1"], 15: ["G0", "V2", "V3"]}
START = [n for g in sorted(AHEAD) for n in AHEAD[g]]


def slot_items(g, last):
    own = [f"G{g + 1}"] if g < H - 1 else []
    own += [f"V{g + 2}"] if 2 <= g <= 5 else []
    return [(n, False) for n in own] + ([] if last else [(n, True) for n in AHEAD.get(g, [])])


def item_sequence(last):
    return [x for g in range(H) for x in slot_items(g, last)]


def item_place(b, par, name, keep):
    start = [n for n in START if keep(n)]
    full = [x for x in item_sequence(False) if keep(x[0])]
    per = len(full)
    if name in START:
        if isinstance(b, int) and b == 0:
            return per, start.index(name)
        return per, len(start) - per + full.index((name, True))
    last = isinstance(b, int) and b == B - 1
    seq = [x for x in item_sequence(True) if keep(x[0])] if last else full
    return per, len(start) + seq.index((name, False))


def item_count(b, name, split=False):
    keep = (lambda n: n[0] in "XG") if split else (lambda n: True)
    per, off = item_place(b, 0, name, keep)
    return at(b, per, off + 1)


def item_bank(b, par, name):
    per, off = item_place(b, par, name, lambda n: True)
    return (per * par + off) % 2


def item_before(b, par, name):
    last = isinstance(b, int) and b == B - 1
    own_ahead = name in START
    if own_ahead and isinstance(b, int) and b == 0:
        k = START.index(name)
        return (0, START[k - 2]) if k >= 2 else None
    shift = -1 if own_ahead else 0
    seq = item_sequence(last and not own_ahead)
    k = seq.index((name, own_ahead))
    if k >= 2:
        n, a = seq[k - 2]
        return (shift + (1 if a else 0), n)
    if not own_ahead and isinstance(b, int) and b == 0:
        return (0, START[k - 2])
    n, a = item_sequence(False)[k - 2]
    return (shift - 1 + (1 if a else 0), n)


def head_slots(eng, slot, extra=0):
    for g in range(H):
        slot(0, g, 0)
    with eng.Fori(0, B // 2 - 1) as i:
        for g in range(H):
            slot(i * 2 + 1, g, 1)
        for g in range(H):
            slot(i * 2 + 2, g, 0)
    for g in range(H):
        slot(B - 1, g, 1)
    for g in range(extra):
        slot(B, g, 0)


def has_scores(b):
    return not isinstance(b, int) or b < B


def has_next(b):
    return not isinstance(b, int) or b < B - 1


def has_before(b):
    return not isinstance(b, int) or b > 0


def lagging(b, g, par, lag):
    if g >= lag:
        out = (b, g - lag, par)
    elif isinstance(b, int) and b == 0:
        return None
    else:
        out = (b - 1, g - lag + H, 1 - par)
    return None if isinstance(out[0], int) and out[0] >= B else out


def causal_attention(nc, c, x, Wq, Wk, Wv, Wo, bo, rel, out, ext_dram):
    xf, ident, bank = c["xf"], c["ident"], c["bank"]
    with ExitStack() as ctx:
        def sb(name, shape, dt=F32):
            return ctx.enter_context(nc.sbuf_tensor(name, shape, dt))

        def sem(name):
            return ctx.enter_context(nc.semaphore(name))

        m_hi, m_lo = sb("m_hi", [P, H, D], F32R), sb("m_lo", [P, H, D], F32R)
        wv_hi, wv_lo = sb("wv_hi", [P, HD], F32R), sb("wv_lo", [P, HD], F32R)
        wo_hi, wo_lo = sb("wo_hi", [P, HP, D], F32R), sb("wo_lo", [P, HP, D], F32R)
        bo_b = sb("bo_b", [P, D])
        bias_tab = sb("bias_tab", [P, H, T])
        stats = sb("stats", [P, TT, 6])
        mv = sb("mv", [P, TT, 2])
        ve = sb("ve", [P, TT])
        rstd = sb("rstd", [P, TT])
        mhalf = sb("mhalf", [P, TT])
        xb = sb("xb", [P, 2, TT, D])
        xn = sb("xn", [P, TT, D])
        xT_hi, xT_lo = sb("xT_hi", [P, 2, T], F32R), sb("xT_lo", [P, 2, T], F32R)
        g_hi, g_lo = sb("g_hi", [P, 2, T], F32R), sb("g_lo", [P, 2, T], F32R)
        v = sb("v", [P, TT, HD])
        L = sb("L", [P, RING, LSZ])
        nmax = sb("nmax", [P, RING, TT])
        rsum = sb("rsum", [P, RING, TT])
        rinv = sb("rinv", [P, RING, TT])
        PT = sb("PT", [P, 2, LSZ])
        o_hi, o_lo = sb("o_hi", [P, T], F32R), sb("o_lo", [P, T], F32R)
        yT = sb("yT", [P, T])
        ext = PT[0:H, 0, 0:EXT]
        far_rows = L[:].rearrange("p r k -> p (r k)")[:, 3072:3072 + H * NREL]
        raw = L[:].rearrange("p r k -> p (r k)")[:, 0:3 * HD]
        wqT, wkT = v[:, 0, :], v[:, 1, :]
        wo_raw = v[:, 2, :]

        ps_scores, ps_probsT, ps_heads, ps_y, ps_item = bank[0:2], bank[2:4], bank[4], bank[5], bank[6:8]

        s_wq = sem("wq_wk_loaded")
        s_wv = sem("wv_wo_loaded")
        s_wT = sem("w_transposed")
        s_wTe = sem("wT_out")
        s_m = sem("m_done")
        s_mhi = sem("m_hi_out")
        s_mlo = sem("m_lo_out")
        s_whi = sem("wv_wo_hi")
        s_wlo = sem("wv_wo_lo")
        s_x = [sem("x_loaded_even"), sem("x_loaded_odd")]
        s_bo_b = sem("bo_loaded")
        s_rel = sem("rel_loaded")
        s_ext = sem("ext_built")
        s_extd = sem("ext_in_dram")
        s_tab = sem("bias_tab_loaded")
        s_gate_dve = sem("gate_dve")
        s_gate_pool = sem("gate_pool")
        s_far = sem("far_bias_filled")
        s_id0 = sem("ident_zeroed")
        s_id = sem("ident_built")
        s_mh = sem("mhalf_set")
        s_st = sem("stats_done")
        s_mv = sem("mean_var_done")
        s_ve = sem("var_eps_done")
        s_rstd = sem("rstd_done")
        s_xn = sem("xn_done")
        s_xf = sem("xf_kept")
        s_xbo = sem("x_plus_bo")
        s_item = sem("item_done")
        s_ihi = sem("item_hi_out")
        s_ilo = sem("item_lo_out")
        s_S = sem("scores_done")
        s_L = sem("logits_done")
        s_E = sem("exp_done")
        s_R = sem("rinv_done")
        s_N = sem("probs_done")
        s_T = sem("probsT_done")
        s_TE = sem("probsT_out")
        s_PV = sem("pv_done")
        s_Oh = sem("heads_hi_out")
        s_Ol = sem("heads_lo_out")
        s_Y = sem("y_pair_done")
        s_yT = sem("yT_out")
        s_yb = sem("y_back_done")
        s_add = sem("batch_summed")
        s_out = sem("batch_stored")

        block = ctx.enter_context(nc.Block())
        xv = x.rearrange("b (t p) d -> p (b t) d", p=P)
        ov = out.rearrange("b (t p) d -> p (b t) d", p=P)

        @block.sync
        def _(sp):
            sp.dma_start(raw[:, 0:HD], Wq).then_inc(s_wq, 16)
            sp.dma_start(raw[:, HD:2 * HD], Wk).then_inc(s_wq, 16)
            sp.dma_start(xb[:, 0], xv[:, 0:TT, :]).then_inc(s_x[0], 16)
            sp.dma_start(raw[:, 2 * HD:3 * HD], Wv).then_inc(s_wv, 16)
            sp.dma_start(wo_raw.rearrange("p (c n) -> p c n", c=HP), Wo.rearrange("(c p) n -> p c n", p=P)).then_inc(s_wv, 16)
            sp.dma_start(xb[:, 1], xv[:, TT:2 * TT, :]).then_inc(s_x[1], 16)

            def turn(b, par):
                sp.wait_ge(s_add, at(b, 1, 1))
                sp.dma_start(ov[:, bass.ds(b * TT, TT), :], xb[:, par]).then_inc(s_out, 16)
                if isinstance(b, int) and b >= B - 2:
                    return
                sp.wait_ge(s_out, at(b, 16, 16))
                sp.dma_start(xb[:, par], xv[:, bass.ds(b * TT + 2 * TT, TT), :]).then_inc(s_x[par], 16)
            with sp.Fori(0, B // 2 - 1) as i:
                turn(i * 2, 0)
                turn(i * 2 + 1, 1)
            turn(B - 2, 0)
            turn(B - 1, 1)
            sp.wait_ge(s_out, 16 * B)

        @block.gpsimd
        def _(pool):
            nc.gpsimd.memset(ident[:], 0.0).then_inc(s_id0, 1)
            nc.gpsimd.memset(mhalf[:], -0.5).then_inc(s_mh, 1)
            pool.wait_ge(s_id0, 1)
            nc.gpsimd.affine_select(out=ident[:], in_=ident[:], compare_op=ALU.not_equal, fill=1.0, base=0,
                                    pattern=[[-1, P]], channel_multiplier=1).then_inc(s_id, 1)
            pool.wait_ge(s_mh, 1)

            def scale_of(b):
                pool.wait_ge(s_ve, at(b, 1, 1))
                nc.gpsimd.tensor_tensor(rstd[:], ve[:], mhalf[:], ALU.pow).then_inc(s_rstd, 1)

            def keep(b, par):
                pool.wait_ge(s_xn, at(b, TT, TT))
                nc.gpsimd.tensor_copy(xf[:, bass.ds(b * TT, TT), :], xn[:]).then_inc(s_xf, 1)
                pool.wait_ge(s_bo_b, 16)
                nc.gpsimd.tensor_tensor(xb[:, par], xb[:, par], bo_b[:].unsqueeze(1).to_broadcast([P, TT, D]),
                                        ALU.add).then_inc(s_xbo, 1)
            scale_of(0)
            pool.wait_ge(s_wv, 32)
            nc.gpsimd.tensor_copy(wv_hi[:], raw[:, 2 * HD:3 * HD]).then_inc(s_whi, 1)
            nc.gpsimd.tensor_copy(wo_hi[:].rearrange("p c n -> p (c n)"), wo_raw).then_inc(s_whi, 1)
            pool.wait_ge(s_whi, 2)
            nc.gpsimd.tensor_tensor(wv_lo[:], raw[:, 2 * HD:3 * HD], wv_hi[:].bitcast(F32), ALU.subtract).then_inc(s_wlo, 1)
            nc.gpsimd.tensor_tensor(wo_lo[:].rearrange("p c n -> p (c n)"), wo_raw,
                                    wo_hi[:].rearrange("p c n -> p (c n)").bitcast(F32), ALU.subtract).then_inc(s_wlo, 1)
            keep(0, 0)

            def slot(b, g, par):
                head = lagging(b, g, par, 1)
                if head is not None:
                    hb, h, _ = head
                    pool.wait_ge(s_R, at(hb, H, h + 1))
                    pool.sem_inc(s_gate_pool, 1)
                    for i in range(TT):
                        a = L[:, h % RING, LOFF[i]:LOFF[i] + (i + 1) * P]
                        nc.gpsimd.tensor_scalar(a, a, rinv[:, h % RING, i:i + 1], 1.0, ALU.mult,
                                                ALU.mult).then_inc(s_N, 1)
                if g == 9 and has_next(b):
                    scale_of(b + 1)
                if g == 12 and has_next(b):
                    keep(b + 1, 1 - par)
            head_slots(pool, slot, 1)

        @block.scalar
        def _(act):
            act.dma_start(ext[:, P:P + NREL], rel).then_inc(s_rel, 16)
            act.dma_start(far_rows, bass.AP(rel.tensor, 0, [[0, P], [1, H * NREL]])).then_inc(s_rel, 16)
            act.dma_start(bo_b[:], bo.partition_broadcast(P)).then_inc(s_bo_b, 16)
            act.wait_ge(s_ext, 3)
            act.dma_start(ext_dram, ext.unsqueeze(1).to_broadcast([H, P, EXT])).then_inc(s_extd, 16)
            for k in range(4):
                act.wait_ge(s_wT, k + 1)
                dst = (wqT, wkT)[k // 2]
                nc.scalar.activation(dst[:, (k % 2) * 512:(k % 2) * 512 + 512], ps_scores[k % 2][:],
                                     ACT.Copy).then_inc(s_wTe, 1)
            act.wait_ge(s_extd, 16)
            toeplitz = bass.AP(ext_dram.tensor, P - 1, [[EXT - 1, P], [P * EXT, H], [1, 2 * P]])
            act.dma_start(bias_tab[:, :, T - 2 * P:T], toeplitz).then_inc(s_tab, 16)
            for k in range(4):
                act.wait_ge(s_m, k + 1)
                nc.scalar.activation(m_hi[:, 8 * (k // 2) + k % 2:8 * (k // 2) + 8:2, :],
                                     ps_probsT[k % 2][:].rearrange("p (h d) -> p h d", d=D),
                                     ACT.Copy).then_inc(s_mhi, 1)

            def evacuate(name, b, par):
                act.wait_ge(s_item, item_count(b, name))
                src = ps_item[item_bank(b, par, name)][:]
                if name == "XT":
                    act.wait_ge(s_S, at(b, 4 * H, -4 * H))
                    dst = xT_hi[:, par, :]
                elif name[0] == "G":
                    g = int(name[1:])
                    act.wait_ge(s_S, at(b, 4 * H, 4 * (g - 1)))
                    dst = g_hi[:, g % 2, :]
                else:
                    half, t = divmod(int(name[1]), TT)
                    act.wait_ge(s_PV, at(b, 4 * H, 32 * (half + 1) - 4 * H))
                    dst = v[:, t, half * 512:half * 512 + 512]
                nc.scalar.activation(dst, src, ACT.Copy).then_inc(s_ihi, 1)

            for name in START:
                if name == "V0":
                    act.wait_ge(s_wlo, 2)
                    act.wait_ge(s_m, 4)
                evacuate(name, 0, 0)

            def slot(b, g, par):
                items = [(n, b + 1 if a else b, 1 - par if a else par) for n, a in slot_items(g, not has_next(b))] \
                    if has_scores(b) else []
                if g == 3 and has_before(b):
                    act.wait_ge(s_Y, at(b, HP, 0))
                    nc.scalar.activation(yT[:], ps_y[:], ACT.Copy).then_inc(s_yT, 1)
                done = lagging(b, g, par, 3)
                if done is not None and done[1] % 2 == 1:
                    hb, h, _ = done
                    act.wait_ge(s_PV, at(hb, 4 * H, 4 * h + 4))
                    act.wait_ge(s_Y, at(hb, HP, h // 2))
                    nc.scalar.activation(o_hi[:], ps_heads[:], ACT.Copy).then_inc(s_Oh, 1)
                for i in range(TT):
                    if has_scores(b):
                        act.wait_ge(s_L, at(b, 4 * H, 4 * g + i + 1))
                        a = L[:, g % RING, LOFF[i]:LOFF[i] + (i + 1) * P]
                        nc.scalar.activation(a, a, ACT.Exp, bias=nmax[:, g % RING, i:i + 1], scale=-1.0,
                                             accum_out=rsum[:, g % RING, i:i + 1]).then_inc(s_E, 1)
                    for item in {1: items[0:1], 2: items[1:2], 3: items[2:]}.get(i, []):
                        evacuate(*item)
            head_slots(act, slot, 4)

        @block.vector
        def _(dve):
            def gate_dve():
                dve.sem_inc(s_gate_dve, 1)

            def statistics(b, par):
                dve.wait_ge(s_x[par], at(b, 8, 16 - 8 * par) if not isinstance(b, int) else 16 * (b // 2 + 1))
                for t in range(TT):
                    nc.vector.bn_stats(stats[:, t, :], xb[:, par, t, :]).then_inc(s_st, 1)
                dve.wait_ge(s_st, at(b, TT, TT))
                gate_dve()
                for t in range(TT):
                    nc.vector.bn_aggr(mv[:, t, :], stats[:, t, :]).then_inc(s_mv, 1)
                dve.wait_ge(s_mv, at(b, TT, TT))
                nc.vector.tensor_scalar(ve[:], mv[:, :, 1], LN_EPS, None, ALU.add).then_inc(s_ve, 1)

            def normalise(b, par):
                dve.wait_ge(s_rstd, at(b, 1, 1))
                dve.wait_ge(s_xf, at(b, 1, 0))
                for t in range(TT):
                    nc.vector.tensor_scalar(xn[:, t, :], xb[:, par, t, :], mv[:, t, 0:1], rstd[:, t:t + 1],
                                            ALU.subtract, ALU.mult).then_inc(s_xn, 1)

            def low_part(name, b, par):
                dve.wait_ge(s_ihi, item_count(b, name))
                src = ps_item[item_bank(b, par, name)][:]
                hi, lo = (xT_hi[:, par, :], xT_lo[:, par, :]) if name == "XT" else \
                    (g_hi[:, int(name[1:]) % 2, :], g_lo[:, int(name[1:]) % 2, :])
                nc.vector.tensor_tensor(lo, src, hi.bitcast(F32), ALU.subtract).then_inc(s_ilo, 1)

            dve.wait_ge(s_rel, 32)
            nc.vector.tensor_copy(ext[:, 0:P], ext[:, P:P + 1].to_broadcast([H, P])).then_inc(s_ext, 1)
            nc.vector.memset(ext[:, P + NREL:EXT], NEG).then_inc(s_ext, 2)
            statistics(0, 0)
            normalise(0, 0)
            for k in range(4):
                dve.wait_ge(s_mhi, k + 1)
                four = slice(8 * (k // 2) + k % 2, 8 * (k // 2) + 8, 2)
                nc.vector.tensor_tensor(m_lo[:, four, :], ps_probsT[k % 2][:].rearrange("p (h d) -> p h d", d=D),
                                        m_hi[:, four, :].bitcast(F32), ALU.subtract).then_inc(s_mlo, 1)
            nc.vector.tensor_copy(bias_tab[:, :, 0:T - 2 * P],
                                  far_rows[:, ::NREL].unsqueeze(2).to_broadcast([P, H, T - 2 * P])).then_inc(s_far, 1)
            for name in START:
                if name[0] in "XG":
                    low_part(name, 0, 0)
            dve.wait_ge(s_far, 1)
            dve.wait_ge(s_wlo, 2)
            dve.wait_ge(s_wT, 4)
            dve.wait_ge(s_tab, 16)

            def slot(b, g, par):
                tail = lagging(b, g, par, LAG)
                items = [(n, b + 1 if a else b, 1 - par if a else par) for n, a in slot_items(g, not has_next(b))] \
                    if has_scores(b) else []

                def logits(i):
                    if not has_scores(b):
                        return
                    dve.wait_ge(s_S, at(b, 4 * H, 4 * g + i + 1))
                    if i == 0:
                        dve.wait_ge(s_T, at(b, 4 * H, 4 * (g - RING + 1)))
                    gate_dve()
                    nc.vector.tensor_tensor_reduce(
                        out=L[:, g % RING, LOFF[i]:LOFF[i] + (i + 1) * P], in0=ps_scores[i % 2][:, 0:(i + 1) * P],
                        in1=bias_tab[:, g, T - (i + 1) * P:T], scale=-1.0 / DH, scalar=3.0e38,
                        op0=ALU.add, op1=ALU.min, accum_out=nmax[:, g % RING, i:i + 1]).then_inc(s_L, 1)

                def probs(j):
                    if tail is None:
                        return
                    hb, h, _ = tail
                    dve.wait_ge(s_T, at(hb, 4 * H, 4 * h + j + 1))
                    if j == 0:
                        dve.wait_ge(s_PV, at(hb, 4 * H, 4 * (h - 1)))
                    nc.vector.tensor_copy(PT[:, h % 2, POFF[j]:POFF[j] + T - j * P],
                                          ps_probsT[j % 2][:, 0:T - j * P]).then_inc(s_TE, 1)

                probs(0)
                logits(0)
                head = lagging(b, g, par, 1)
                if head is not None:
                    hb, h, _ = head
                    dve.wait_ge(s_E, at(hb, 4 * H, 4 * h + 4))
                    nc.vector.reciprocal(rinv[:, h % RING, :], rsum[:, h % RING, :]).then_inc(s_R, 1)
                done = lagging(b, g, par, 3)
                if done is not None and done[1] % 2 == 1:
                    hb, h, _ = done
                    dve.wait_ge(s_Oh, at(hb, HP, h // 2 + 1))
                    nc.vector.tensor_tensor(o_lo[:], ps_heads[:], o_hi[:].bitcast(F32), ALU.subtract).then_inc(s_Ol, 1)
                logits(1)
                probs(1)
                logits(2)
                probs(2)
                for n in items[0:1]:
                    if n[0][0] in "XG":
                        low_part(*n)
                logits(3)
                probs(3)
                for n in items[1:]:
                    if n[0][0] in "XG":
                        low_part(*n)
                if g == 3 and has_before(b):
                    dve.wait_ge(s_yb, at(b, 1, 0))
                    dve.wait_ge(s_xbo, at(b, 1, 0))
                    a = xb[:, 1 - par]
                    nc.vector.tensor_tensor(a, ps_y[:].rearrange("p (t d) -> p t d", d=D), a, ALU.add).then_inc(s_add, 1)
                if g == 8 and has_next(b):
                    statistics(b + 1, 1 - par)
                if g == 10 and has_next(b):
                    normalise(b + 1, 1 - par)
            head_slots(dve, slot, 4)

        @block.tensor
        def _(pe):
            pe.wait_ge(s_id, 1)
            pe.wait_ge(s_wq, 32)
            for k in range(4):
                if k >= 2:
                    pe.wait_ge(s_wTe, k - 1)
                for n in range(4):
                    o = (k // 2) * HD + (k % 2) * 512 + n * P
                    last = nc.tensor.transpose(ps_scores[k % 2][:, n * P:n * P + P], raw[:, o:o + P], ident[:])
                last.then_inc(s_wT, 1)
            pe.wait_ge(s_wTe, 4)
            for k in range(4):
                if k >= 2:
                    pe.wait_ge(s_mlo, k - 1)
                for n in range(4):
                    h = 8 * (k // 2) + 2 * n + k % 2
                    r, o = DH * (h % 2), (h // 2) * P
                    last = nc.tensor.matmul(ps_probsT[k % 2][:, n * P:n * P + P], wqT[r:r + DH, o:o + P],
                                            wkT[r:r + DH, o:o + P], start=True, stop=True)
                last.then_inc(s_m, 1)

            def product(out, a, b, start=True, stop=True):
                nc.tensor.matmul(out, a[0], b[0], start=start, stop=False)
                nc.tensor.matmul(out, a[1], b[0], start=False, stop=False)
                return nc.tensor.matmul(out, a[0], b[1], start=False, stop=stop)

            def make(name, b, par):
                prior = item_before(b, par, name)
                if prior is not None:
                    pb, pn = b + prior[0], prior[1]
                    if pn[0] in "XG":
                        pe.wait_ge(s_ilo, item_count(pb, pn, True))
                    else:
                        pe.wait_ge(s_ihi, item_count(pb, pn))
                out = ps_item[item_bank(b, par, name)]
                if name == "XT":
                    pe.wait_ge(s_xn, at(b, TT, TT))
                    for t in range(TT):
                        last = nc.tensor.transpose(out[:, t * P:t * P + P], xn[:, t, :], ident[:])
                elif name[0] == "G":
                    g = int(name[1:])
                    if g == 0:
                        pe.wait_ge(s_ilo, item_count(b, "XT", True))
                    last = product(out[:], (m_hi[:, g, :], m_lo[:, g, :]), (xT_hi[:, par, :], xT_lo[:, par, :]))
                else:
                    half, t = divmod(int(name[1]), TT)
                    if int(name[1]) == 0:
                        pe.wait_ge(s_ilo, item_count(b, "XT", True))
                    tok, col = slice(t * P, t * P + P), slice(half * 512, half * 512 + 512)
                    last = product(out[:], (xT_hi[:, par, tok], xT_lo[:, par, tok]), (wv_hi[:, col], wv_lo[:, col]))
                last.then_inc(s_item, 1)

            pe.wait_ge(s_mlo, 4)
            pe.wait_ge(s_wlo, 2)
            for name in START:
                make(name, 0, 0)

            def slot(b, g, par):
                tail = lagging(b, g, par, LAG)
                items = [(n, b + 1 if a else b, 1 - par if a else par) for n, a in slot_items(g, not has_next(b))] \
                    if has_scores(b) else []

                def scores(i):
                    if not has_scores(b):
                        return
                    if i == 0:
                        pe.wait_ge(s_ilo, item_count(b, f"G{g}", True))
                    pe.wait_ge(s_L, at(b, 4 * H, 4 * g + i - 1))
                    q, keys = slice(i * P, i * P + P), slice(0, (i + 1) * P)
                    product(ps_scores[i % 2][:, keys], (g_hi[:, g % 2, q], g_lo[:, g % 2, q]),
                            (xT_hi[:, par, keys], xT_lo[:, par, keys])).then_inc(s_S, 1)

                def transposes(j):
                    if tail is None:
                        return
                    hb, h, _ = tail
                    if j == 0:
                        pe.wait_ge(s_N, at(hb, 4 * H, 4 * h + 4))
                    pe.wait_ge(s_TE, at(hb, 4 * H, 4 * h + j - 1))
                    for i in range(j, TT):
                        last = nc.tensor.transpose(ps_probsT[j % 2][:, (i - j) * P:(i - j) * P + P],
                                                   L[:, h % RING, LOFF[i] + j * P:LOFF[i] + j * P + P], ident[:])
                    last.then_inc(s_T, 1)

                def values(j, head):
                    if head is None:
                        return
                    hb, h, _ = head
                    r = DH * (h % 2)
                    pe.wait_ge(s_TE, at(hb, 4 * H, 4 * h + j + 1))
                    if j == 0 and h % 2 == 0:
                        pe.wait_ge(s_Ol, at(hb, HP, h // 2))
                    if j == 0 and h % 8 == 0:
                        pe.wait_ge(s_ihi, item_count(hb, "V3" if h == 0 else "V7"))
                    nc.tensor.matmul(ps_heads[r:r + DH, j * P:T], v[:, j, h * DH:h * DH + DH],
                                     PT[:, h % 2, POFF[j]:POFF[j] + T - j * P], start=(j == 0),
                                     stop=(j == TT - 1)).then_inc(s_PV, 1)

                def y_share():
                    done = lagging(b, g, par, 3)
                    if done is None or done[1] % 2 == 0:
                        return
                    hb, h, _ = done
                    p = h // 2
                    pe.wait_ge(s_Ol, at(hb, HP, p + 1))
                    if p == 0:
                        pe.wait_ge(s_add, at(hb, 1, 0))
                    product(ps_y[:], (wo_hi[:, p, :], wo_lo[:, p, :]), (o_hi[:], o_lo[:]),
                            start=(p == 0), stop=(p == HP - 1)).then_inc(s_Y, 1)

                transposes(0)
                scores(0)
                values(2, lagging(b, g, par, LAG + 1))
                scores(1)
                values(3, lagging(b, g, par, LAG + 1))
                transposes(1)
                for n in items[0:1]:
                    make(*n)
                scores(2)
                values(0, tail)
                transposes(2)
                y_share()
                values(1, tail)
                scores(3)
                transposes(3)
                for n in items[1:]:
                    make(*n)
                if g == 3 and has_before(b):
                    pe.wait_ge(s_yT, at(b, 1, 0))
                    for t in range(TT):
                        last = nc.tensor.transpose(ps_y[:, t * P:t * P + P], yT[:, t * P:t * P + P], ident[:])
                    last.then_inc(s_yb, 1)
            head_slots(pe, slot, 4)


def tile_slots(eng, slot, lag=TT + 1):
    for b in range(2):
        for t in range(TT):
            slot(b, t)
    with eng.Fori(2, B) as b:
        for t in range(TT):
            slot(b, t)
    for n in range(lag):
        slot(B + n // TT, n % TT)


def tile_back(b, t, lag):
    up, ht = divmod(t - lag, TT)
    hb = b + up if up else b
    if isinstance(hb, int) and not 0 <= hb < B:
        return None
    return hb, ht


def batch_slots(eng, slot, lag):
    for b in range(4):
        slot(b, b % 2)
    with eng.Fori(0, B // 2 - 2) as i:
        for r in range(2):
            slot(i * 2 + (4 + r), r)
    for b in range(B, B + lag):
        slot(b, b % 2)


def batch_back(b, lag):
    if isinstance(b, int) and not 0 <= b - lag < B:
        return None
    return b - lag


def load_shifted(sp, hs, xf, b, t, s_hs):
    x_t = xf[:, bass.ds(b * TT + t, 1), :].squeeze(1)
    half = D // 2
    sp.dma_start(hs[:, t, 0:half], x_t[:, 0:half]).then_inc(s_hs, 16)
    sp.dma_start(hs[1:P, t, half:D], x_t[0:P - 1, half:D]).then_inc(s_hs, 16)
    if t > 0:
        x_p = xf[:, bass.ds(b * TT + t - 1, 1), :].squeeze(1)
        sp.dma_start(hs[0:1, t, half:D], x_p[P - 1:P, half:D]).then_inc(s_hs, 16)


def load_shifted_batch(sp, hs, xf, b, r, s_hs):
    x_b = xf[:, bass.ds(b * TT, TT), :]
    half = D // 2
    sp.dma_start(hs[:, r, :, 0:half], x_b[:, :, 0:half]).then_inc(s_hs, 16)
    sp.dma_start(hs[1:P, r, :, half:D], x_b[0:P - 1, :, half:D]).then_inc(s_hs, 16)
    sp.dma_start(hs[0:1, r, 1:TT, half:D], x_b[P - 1:P, 0:TT - 1, half:D]).then_inc(s_hs, 16)


def shifted_count(t):
    return 48 if t > 0 else 32


def load_attention_weights(eng, c, d, l, s):
    def row(a):
        return a[bass.ds(l, 1), :].to_broadcast([P, DH])
    eng.dma_start(c["wqkv"][:], d["wqkv"][bass.ds(l, 1), :, :].squeeze(0)).then_inc(s, 16)
    eng.dma_start(c["wo4"][:], d["wo"][bass.ds(l, 1), :, :].squeeze(0).rearrange("(c p) n -> p c n", p=P)).then_inc(s, 16)
    eng.dma_start(c["qk_scale"][:, 0, :], row(d["q_scale"])).then_inc(s, 16)
    eng.dma_start(c["qk_scale"][:, 1, :], row(d["k_scale"])).then_inc(s, 16)


def local_attention(nc, c, d, l, w):
    xf, ident, bank, hs, sem = c["xf"], c["ident"], c["bank"], c["hs"], w["attn"]
    ps_q, ps_k, ps_v, ps_s, ps_t, ps_o = bank[0], bank[1], bank[2], bank[3:5], bank[5:7], bank[7]
    hT_hi, hT_lo, w_hi, w_lo = w["hT_hi"], w["hT_lo"], w["w_hi"], w["w_lo"]
    sq, ssq, rn, rq8 = w["sq"], w["ssq"], w["rn"], w["rq8"]
    qa, qb, ka, kb = w["qa"], w["qb"], w["ka"], w["kb"]
    qr, kr, qT, kT, v, L, nmax, rsum, rinv, PT, OT = (w[n] for n in (
        "qr", "kr", "qT", "kT", "v", "L", "nmax", "rsum", "rinv", "PT", "OT"))
    tab, mask = w["tab"], w["mask"]

    vm = w["vm"]
    ACT_HEADS = 4

    block_ctx = nc.Block()
    block = block_ctx.__enter__()

    def evacuate_PT(eng, copy, tile, k, how=()):
        tb, tt = tile
        eng.wait_ge(sem["PT_done"], at(tb, 4 * TT, 4 * tt + k + 1))
        eng.wait_ge(sem["pv_done"], at(tb, 4 * TT, 4 * tt + k - 3))
        copy(PT[:, k].rearrange("p a q -> p (a q)"), ps_t[k % 2][:, 0:2 * P], *how).then_inc(sem[f"PT_out{k}"], 1)

    @block.sync
    def _(sp):
        s = sem["weights"]
        sp.dma_start(c["w1"][:], d["w1"][bass.ds(l, 1), :, :].squeeze(0)).then_inc(s, 16)
        sp.dma_start(c["w2"][:, 0:2, :], d["w2"][bass.ds(l, 1), 0:2 * P, :].squeeze(0).rearrange("(c p) n -> p c n", p=P)).then_inc(s, 16)
        sp.dma_start(c["w2"][0:CH[2], 2, :], d["w2"][bass.ds(l, 1), 2 * P:HID, :].squeeze(0)).then_inc(s, 16)
        sp.dma_start(c["w2"][CH[2]:CH[2] + 1, 2, :], d["b2"][bass.ds(l, 1), :]).then_inc(s, 16)
        with nc.allow_non_contiguous_dma(reason="a few columns, once a layer"):
            sp.dma_start(c["ln"][:, 0:1], d["ln_g"][bass.ds(l, 1), :].rearrange("l p -> p l")).then_inc(s, 16)
            sp.dma_start(c["ln"][:, 1:2], d["ln_b"][bass.ds(l, 1), :].rearrange("l p -> p l")).then_inc(s, 16)
            for part in range(2):
                for j in range(3):
                    o = part * HID + j * P
                    sp.dma_start(c["b1"][0:CH[j], part * 3 + j:part * 3 + j + 1],
                                 d["b1"][bass.ds(l, 1), o:o + CH[j]].rearrange("l p -> p l")).then_inc(s, 16)

        def slot(b, t):
            if not isinstance(b, int) or 0 < b < B:
                sp.wait_ge(sem["hT_done"], at(b, TT, t - TT + 1))
                load_shifted(sp, hs, xf, b, t, sem[f"hs{t}"])
            two = tile_back(b, t, 2)
            if two is not None:
                vb, vt = two
                sp.wait_ge(sem["v_out"], at(vb, TT, vt + 1))
                if vt > 0:
                    sp.dma_start(vm[0:WIN, vt - 1, :], v[0:WIN, vt, :]).then_inc(sem[f"vm{vt}"], 16)
                if vt < TT - 1:
                    sp.dma_start(vm[WIN:P, vt, :], v[WIN:P, vt, :]).then_inc(sem[f"vm{vt}"], 16)
        tile_slots(sp, slot, lag=2)
        sp.wait_ge(sem["x_out"], 2 * TT)
        for b in range(2):
            load_shifted_batch(sp, w["hs2"], xf, b, b, w["mlp"][f"hs{b}"])
        for b in range(2):
            sp.wait_ge(w["mlp"][f"hs{b}"], 48)
        sp.wait_ge(s, 16 * 12)

    @block.gpsimd
    def _(pool):
        for n in w["mlp"].values():
            pool.sem_clear(n)
        for k in range(4):
            nc.gpsimd.tensor_tensor(tab[:, :, k, :], w["rope"][:, :, k, :],
                                    c["qk_scale"][:, k // 2, :].unsqueeze(1).to_broadcast([P, TT, DH]),
                                    ALU.mult).then_inc(sem["tab"], 1)

        def halves(a, r):
            return a.rearrange("p (h r e) -> p h r e", h=FH, r=2)[:, :, r, :]

        def slot(b, t):
            two, four = tile_back(b, t, 2), tile_back(b, t, 4)
            if four is not None:
                tb, tt = four
                n = FH - ACT_HEADS
                pool.wait_ge(sem["rinv"], at(tb, TT, tt + 1))
                a = L[:, tt % 2, ACT_HEADS:FH, :]
                nc.gpsimd.tensor_tensor(a, a, rinv[:, tt % 2, ACT_HEADS:FH].unsqueeze(2).to_broadcast([P, n, P]),
                                        ALU.mult).then_inc(sem["probs_pool"], 1)
            if two is not None:
                tb, tt = two
                r = tt % 2
                pool.wait_ge(sem["qab"], at(tb, TT, tt + 1))
                pool.wait_ge(sem["qT_done"], at(tb, TT, tt))
                for s in range(2):
                    nc.gpsimd.tensor_tensor(halves(qr[:], s), halves(qa[:, r, :], s), halves(qb[:, r, :], 1 - s),
                                            ALU.add).then_inc(sem["qr"], 1)
                pool.wait_ge(sem["kab"], at(tb, TT, tt + 1))
                pool.wait_ge(sem["kT_done"], at(tb, TT, tt))
                for s in range(2):
                    nc.gpsimd.tensor_tensor(halves(kr[:], s), halves(ka[:, r, :], s), halves(kb[:, r, :], 1 - s),
                                            ALU.add).then_inc(sem["k_rotated"], 1)
                pool.wait_ge(sem["ssq"], at(tb, TT, tt + 1))
                nc.gpsimd.tensor_tensor(rn[:, r, :], ssq[:, r, :], w["mhalf"][:], ALU.pow).then_inc(sem["rn"], 1)
                pool.wait_ge(sem["rn"], at(tb, TT, tt + 1))
                pool.wait_ge(sem["k_rotated"], at(tb, 2 * TT, 2 * tt + 2))
                kr3 = kr[:].rearrange("p (h e) -> p h e", h=FH)
                nc.gpsimd.tensor_tensor(kr3, kr3, rn[:, r, FH:2 * FH].unsqueeze(2).to_broadcast([P, FH, DH]),
                                        ALU.mult).then_inc(sem["kr"], 1)
                pool.wait_ge(sem["logits"], at(tb, 8 * TT, 8 * (tt - 1)))
                pool.sem_inc(w["gate_pool"], 1)
                nc.gpsimd.tensor_scalar(rq8[:, r, :], rn[:, r, 0:FH], -8.0, 1.0, ALU.mult, ALU.mult).then_inc(sem["rq8"], 1)
        tile_slots(pool, slot)

    @block.scalar
    def _(act):
        def slot(b, t):
            now, one, two, three, four, five = (tile_back(b, t, k) for k in range(6))
            def square(k):
                if one is None:
                    return
                ib, it = one
                act.wait_ge(sem["qk_done"], at(ib, 2 * TT, 2 * it + k + 1))
                act.wait_ge(sem["ssq"], at(ib, TT, it - 1))
                nc.scalar.activation(sq[:, it % 2, k, :], (ps_q, ps_k)[k][:], ACT.Square).then_inc(sem["sq"], 1)

            if three is not None:
                ob, ot = three

            def probs(h):
                if four is None:
                    return
                tb, tt = four
                act.wait_ge(sem["rinv"], at(tb, TT, tt + 1))
                a = L[:, tt % 2, h, :]
                nc.scalar.activation(a, a, ACT.Copy, scale=rinv[:, tt % 2, h:h + 1]).then_inc(sem["probs_act"], 1)

            def exps(h):
                if three is None:
                    return
                act.wait_ge(sem["logits"], at(ob, 8 * TT, 8 * ot + h + 1))
                a = L[:, ot % 2, h, :]
                nc.scalar.activation(a, a, ACT.Exp, bias=nmax[:, ot % 2, h:h + 1], scale=-1.0,
                                     accum_out=rsum[:, ot % 2, h:h + 1]).then_inc(sem["exp"], 1)

            if five is not None:
                xb, xt = five
                act.wait_ge(sem["pv_done"], at(xb, 4 * TT, 4 * xt + 4))
                act.wait_ge(sem["wo_done"], at(xb, TT, xt))
                nc.scalar.activation(OT[:], ps_o[:].rearrange("p (c q) -> p c q", c=FC), ACT.Copy).then_inc(sem["OT_out"], 1)
            square(0)
            probs(0)
            probs(1)
            exps(0)
            exps(1)
            probs(2)
            square(1)
            probs(3)
            if two is not None:
                vb, vt = two
                act.wait_ge(sem["v_done"], at(vb, TT, vt + 1))
                act.wait_ge(sem["pv_done"], at(vb, 4 * TT, 4 * (vt - 2)))
                nc.scalar.activation(v[:, vt, :], ps_v[:], ACT.Copy).then_inc(sem["v_out"], 1)
            exps(2)
            exps(3)
            if four is not None:
                evacuate_PT(act, nc.scalar.activation, four, 1, (ACT.Copy,))
            exps(4)
            exps(5)
            if now is not None:
                act.wait_ge(sem["hT_done"], at(b, TT, t + 1))
                nc.scalar.activation(hT_hi[:, t % 2, :], ps_t[0][:, 0:P], ACT.Copy).then_inc(sem["hT_hi"], 1)
            exps(6)
            exps(7)
            if two is not None:
                act.wait_ge(sem["qT_done"], at(vb, TT, vt + 1))
                act.wait_ge(sem["scores"], at(vb, 8 * TT, 8 * vt))
                nc.scalar.activation(qT[:], ps_t[0][:], ACT.Copy).then_inc(sem["qT_out"], 1)
                act.wait_ge(sem["kT_done"], at(vb, TT, vt + 1))
                nc.scalar.activation(kT[:, :, vt * P:vt * P + P], ps_v[:].rearrange("p (c k) -> p c k", c=FC),
                                     ACT.Copy).then_inc(sem["kT_out"], 1)
        tile_slots(act, slot)

    @block.vector
    def _(dve):
        def gate():
            dve.sem_inc(w["gate_dve"], 1)

        nc.vector.tensor_copy(w_hi[:], c["wqkv"][:]).then_inc(sem["w_hi"], 1)
        dve.wait_ge(sem["w_hi"], 1)
        nc.vector.tensor_tensor(w_lo[:], c["wqkv"][:], w_hi[:].bitcast(F32), ALU.subtract).then_inc(sem["w_lo"], 1)
        dve.wait_ge(sem["tab"], 4)

        def slot(b, t):
            now, one, two, three, four, five = (tile_back(b, t, k) for k in range(6))

            def logits(h):
                if three is None:
                    return
                ob, ot = three
                dve.wait_ge(sem["scores"], at(ob, 8 * TT, 8 * ot + h + 1))
                if h == 0:
                    dve.wait_ge(sem["PT_done"], at(ob, 4 * TT, 4 * (ot - 1)))
                    dve.wait_ge(sem["rq8"], at(ob, TT, ot + 1))
                gate()
                nc.vector.tensor_tensor_reduce(out=L[:, ot % 2, h, :], in0=ps_s[h % 2][:, 0:P], in1=mask[:, min(ot, 1), :],
                                               scale=rq8[:, ot % 2, h:h + 1], scalar=3.0e38, op0=ALU.add, op1=ALU.min,
                                               accum_out=nmax[:, ot % 2, h:h + 1]).then_inc(sem["logits"], 1)

            def table_product(k, tile):
                if tile is None:
                    return
                ib, it = tile
                src, dst = (ps_q, ps_k)[k // 2], (qa, qb, ka, kb)[k]
                if k % 2 == 0:
                    dve.wait_ge(sem["sq"], at(ib, 2 * TT, 2 * it + 1 + k // 2))
                    dve.wait_ge(sem[("qr", "k_rotated")[k // 2]], at(ib, 2 * TT, 2 * (it - 1)))
                ins = nc.vector.tensor_tensor(dst[:, it % 2, :].rearrange("p (h e) -> p h e", h=FH),
                                              src[:].rearrange("p (h e) -> p h e", h=FH),
                                              tab[:, it, k, :].unsqueeze(1).to_broadcast([P, FH, DH]), ALU.mult)
                if k % 2 == 1:
                    ins.then_inc(sem[("qab", "kab")[k // 2]], 1)

            def sums(k, tile):
                if tile is None:
                    return
                ib, it = tile
                dve.wait_ge(sem["sq"], at(ib, 2 * TT, 2 * it + 1 + k))
                if k == 0:
                    dve.wait_ge(sem["ssq"], at(ib, TT, it))
                nc.vector.tensor_reduce(w["ssum"][:, k * FH:k * FH + FH], sq[:, it % 2, k].rearrange("p (h e) -> p h e", e=DH),
                                        AX.X, ALU.add).then_inc(sem["ssum"], 1)
                if k == 1:
                    dve.wait_ge(sem["ssum"], at(ib, 2 * TT, 2 * it + 2))
                    dve.wait_ge(sem["rn"], at(ib, TT, it - 1))
                    nc.vector.tensor_scalar(ssq[:, it % 2, :], w["ssum"][:], 1.0e-24, None, ALU.max).then_inc(sem["ssq"], 1)

            def probsT(k):
                if four is not None:
                    evacuate_PT(dve, nc.vector.tensor_copy, four, k)

            if four is not None:
                tb, tt = four
                dve.wait_ge(sem["exp"], at(tb, 8 * TT, 8 * tt + 8))
                nc.vector.reciprocal(rinv[:, tt % 2, :], rsum[:, tt % 2, :]).then_inc(sem["rinv"], 1)
            sums(1, two)
            table_product(3, two)
            logits(0)
            logits(1)
            table_product(0, one)
            table_product(1, one)
            if five is not None:
                xb, xt = five
                dve.wait_ge(sem["wo_done"], at(xb, TT, xt + 1))
                a = xf[:, bass.ds(xb * TT + xt, 1), :].squeeze(1)
                nc.vector.tensor_tensor(a, ps_o[:, 0:D], a, ALU.add).then_inc(sem["x_out"], 1)
            probsT(0)
            logits(2)
            logits(3)
            table_product(2, one)
            logits(4)
            logits(5)
            probsT(2)
            logits(6)
            if now is not None:
                dve.wait_ge(sem["hT_hi"], at(b, TT, t + 1))
                nc.vector.tensor_tensor(hT_lo[:, t % 2, :], ps_t[0][:, 0:P], hT_hi[:, t % 2, :].bitcast(F32),
                                        ALU.subtract).then_inc(sem["hT_lo"], 1)
            logits(7)
            probsT(3)
            sums(0, one)
        tile_slots(dve, slot)

    @block.tensor
    def _(pe):
        pe.wait_ge(sem["w_lo"], 1)

        def slot(b, t):
            now, one, two, three, four, five = (tile_back(b, t, k) for k in range(6))

            def project(k, ps, tile):
                ib, it = tile
                col = slice(k * FI, k * FI + FI)
                nc.tensor.matmul(ps[:], hT_hi[:, it % 2, :], w_hi[:, col], start=True, stop=False)
                nc.tensor.matmul(ps[:], hT_lo[:, it % 2, :], w_hi[:, col], start=False, stop=False)
                return nc.tensor.matmul(ps[:], hT_hi[:, it % 2, :], w_lo[:, col], start=False, stop=True)

            def scores(h):
                if three is None:
                    return
                ob, ot = three
                k, r = h // 2, DH * (h % 2)
                if h == 0:
                    pe.wait_ge(sem["qT_out"], at(ob, TT, ot + 1))
                    pe.wait_ge(sem["kT_out"], at(ob, TT, ot + 1))
                pe.wait_ge(sem["logits"], at(ob, 8 * TT, 8 * ot + h - 1))
                out, own = ps_s[h % 2], ot * P
                if ot == 0:
                    nc.tensor.matmul(out[:, 0:P], qT[r:r + DH, k, :], kT[r:r + DH, k, own:own + P],
                                     start=True, stop=True).then_inc(sem["scores"], 1)
                else:
                    pe.sem_inc(w["gate_pe"], 1)
                    nc.tensor.matmul(out[0:WIN, 0:WIN], qT[r:r + DH, k, 0:WIN], kT[r:r + DH, k, own:own + WIN],
                                     start=True, stop=True)
                    nc.tensor.matmul(out[WIN:P, 0:P], qT[r:r + DH, k, WIN:P], kT[r:r + DH, k, own:own + P],
                                     start=True, stop=True)
                    nc.tensor.matmul(out[0:WIN, WIN:P], qT[r:r + DH, k, 0:WIN], kT[r:r + DH, k, own - WIN:own],
                                     start=True, stop=True).then_inc(sem["scores"], 1)

            def transposes(k):
                if four is None:
                    return
                tb, tt = four
                if 2 * k < ACT_HEADS:
                    pe.wait_ge(sem["probs_act"], at(tb, ACT_HEADS * TT, ACT_HEADS * tt + 2 * k + 2))
                else:
                    pe.wait_ge(sem["probs_pool"], at(tb, TT, tt + 1))
                if k >= 2:
                    pe.wait_ge(sem[f"PT_out{k - 2}"], at(tb, TT, tt + 1))
                elif k == 0 and three is not None:
                    pe.wait_ge(sem["qT_out"], at(three[0], TT, three[1] + 1))
                elif five is not None:
                    pe.wait_ge(sem[f"PT_out{k + 2}"], at(five[0], TT, five[1] + 1))
                ps = ps_t[k % 2]
                for a in range(2):
                    h = 2 * k + a
                    last = nc.tensor.transpose(ps[:, a * P:a * P + P], L[:, tt % 2, h, :], ident[:])
                last.then_inc(sem["PT_done"], 1)

            def values(k):
                if four is None:
                    return
                tb, tt = four
                if k == 0:
                    pe.wait_ge(sem["v_out"], at(tb, TT, tt + 1))
                    if tt > 0:
                        for n in (tt - 1, tt):
                            per = 32 if 0 < n < TT - 1 else 16
                            pe.wait_ge(sem[f"vm{n}"], at(tb, per, per))
                    if five is not None:
                        pe.wait_ge(sem["x_out"], at(five[0], TT, five[1] + 1))
                pe.wait_ge(sem[f"PT_out{k}"], at(tb, TT, tt + 1))
                for a in range(2):
                    h, r = 2 * k + a, DH * a
                    head, o = slice(h * DH, h * DH + DH), k * P
                    if tt == 0:
                        last = nc.tensor.matmul(ps_o[r:r + DH, o:o + P], v[:, 0, head], PT[:, k, a, :], start=True, stop=True)
                    else:
                        nc.tensor.matmul(ps_o[r:r + DH, o:o + WIN], vm[:, tt - 1, head], PT[:, k, a, 0:WIN], start=True, stop=True)
                        last = nc.tensor.matmul(ps_o[r:r + DH, o + WIN:o + P], v[:, tt, head], PT[:, k, a, WIN:P],
                                                start=True, stop=True)
                last.then_inc(sem["pv_done"], 1)

            if one is not None:
                ib, it = one
                pe.wait_ge(sem["hT_lo"], at(ib, TT, it + 1))
                pe.wait_ge(sem["sq"], at(ib, 2 * TT, 2 * it - 1))
                pe.wait_ge(sem["qab"], at(ib, TT, it))
                project(0, ps_q, one).then_inc(sem["qk_done"], 1)
            scores(0)
            scores(1)
            if one is not None:
                pe.wait_ge(sem["kab"], at(ib, TT, it))
                project(1, ps_k, one).then_inc(sem["qk_done"], 1)
            if five is not None:
                xb, xt = five
                pe.wait_ge(sem["OT_out"], at(xb, TT, xt + 1))
                for k in range(FC):
                    last = nc.tensor.matmul(ps_o[:, 0:D], OT[:, k, :], c["wo4"][:, k, :], start=(k == 0), stop=(k == FC - 1))
                last.then_inc(sem["wo_done"], 1)
            if two is not None:
                pe.wait_ge(sem["kT_out"], at(two[0], TT, two[1]))
                pe.wait_ge(sem["v_out"], at(two[0], TT, two[1]))
                project(2, ps_v, two).then_inc(sem["v_done"], 1)
            transposes(0)
            scores(2)
            scores(3)
            transposes(1)
            values(0)
            scores(4)
            scores(5)
            transposes(2)
            scores(6)
            values(1)
            if now is not None:
                pe.wait_ge(sem[f"hs{t}"], at(b, shifted_count(t), shifted_count(t)))
                if three is not None:
                    pe.wait_ge(sem["qT_out"], at(three[0], TT, three[1] + 1))
                if four is not None:
                    pe.wait_ge(sem["PT_out2"], at(four[0], TT, four[1] + 1))
                nc.tensor.transpose(ps_t[0][:, 0:P], hs[:, t, :], ident[:]).then_inc(sem["hT_done"], 1)
            scores(7)
            transposes(3)
            values(2)
            if two is not None:
                if now is not None:
                    pe.wait_ge(sem["hT_lo"], at(b, TT, t + 1))
                pe.wait_ge(sem["qr"], at(two[0], 2 * TT, 2 * two[1] + 2))
                for k in range(FC):
                    last = nc.tensor.transpose(ps_t[0][:, k * P:k * P + P], qr[:, k * P:k * P + P], ident[:])
                last.then_inc(sem["qT_done"], 1)
            if two is not None:
                pe.wait_ge(sem["v_out"], at(two[0], TT, two[1] + 1))
                pe.wait_ge(sem["kr"], at(two[0], TT, two[1] + 1))
                for k in range(FC):
                    last = nc.tensor.transpose(ps_v[:, k * P:k * P + P], kr[:, k * P:k * P + P], ident[:])
                last.then_inc(sem["kT_done"], 1)
            values(3)
        tile_slots(pe, slot)
    block_ctx.__exit__(None, None, None)


def gated_mlp(nc, c, d, l, w):
    xf, ident, bank, sem = c["xf"], c["ident"], c["bank"], w["mlp"]
    ps_g, ps_a, ps_t, ps_y = bank[0:3], bank[3:6], bank[6], bank[7]
    stats, mv, ve, rstd, hn, hT, hT_hi, hT_lo, G, Hh = (w[n] for n in (
        "stats", "mv", "ve", "rstd", "hn", "mT", "mT_hi", "mT_lo", "G", "Hh"))
    hs, w1_hi, w1_lo = w["hs2"], w["w1_hi"], w["w1_lo"]

    block_ctx = nc.Block()
    block = block_ctx.__enter__()

    @block.sync
    def _(sp):
        load_attention_weights(sp, c, d, 1 - l, sem["weights"])

        def slot(b, r):
            if isinstance(b, int) and (b < 2 or b >= B):
                return
            sp.wait_ge(sem["hn"], at(b, TT, -TT))
            load_shifted_batch(sp, hs, xf, b, r, sem[f"hs{r}"])
        batch_slots(sp, slot, 0)
        sp.wait_ge(sem["x_out"], 1)
        for t in range(TT):
            load_shifted(sp, c["hs"], xf, 0, t, w["attn"][f"hs{t}"])
        for t in range(TT):
            sp.wait_ge(w["attn"][f"hs{t}"], shifted_count(t))
        sp.wait_ge(sem["weights"], 64)

    @block.gpsimd
    def _(pool):
        for n in w["attn"].values():
            pool.sem_clear(n)
        nc.gpsimd.tensor_copy(w1_hi[:], c["w1"][:]).then_inc(sem["w_hi"], 1)
        pool.wait_ge(sem["w_hi"], 1)
        nc.gpsimd.tensor_tensor(w1_lo[:], c["w1"][:], w1_hi[:].bitcast(F32), ALU.subtract).then_inc(sem["w_lo"], 1)

        def slot(b, r):
            now, one = batch_back(b, 0), batch_back(b, 1)
            if one is not None:
                pool.wait_ge(sem["hT_out"], at(one, 1, 1))
                pool.wait_ge(sem["hT_hi"], at(one, 1, 1))
                nc.gpsimd.tensor_tensor(hT_lo[:, 1 - r, :], hT[:], hT_hi[:, 1 - r, :].bitcast(F32),
                                        ALU.subtract).then_inc(sem["hT_lo"], 1)
            if now is not None:
                pool.wait_ge(sem["ve"], at(b, 1, 1))
                nc.gpsimd.tensor_tensor(rstd[:], ve[:], w["mhalf"][:, 0:TT], ALU.pow).then_inc(sem["rstd"], 1)
        batch_slots(pool, slot, 3)

    @block.scalar
    def _(act):
        def slot(b, r):
            one, two = batch_back(b, 1), batch_back(b, 2)

            def gelu(j):
                if two is None:
                    return
                act.wait_ge(sem["ga_done"], at(two, 6, 2 * j + 1))
                act.wait_ge(sem["H"], at(two, 3, j - 2))
                n = CH[j]
                nc.scalar.activation(G[0:n, j, :], ps_g[j][0:n, :], ACT.Gelu, bias=c["b1"][0:n, 3 + j:4 + j]).then_inc(sem["gelu"], 1)
            gelu(0)
            if one is not None:
                act.wait_ge(sem["T_done"], at(one, 1, 1))
                act.wait_ge(sem["hT_lo"], at(one, 1, 0))
                nc.scalar.activation(hT[:], ps_t[:], ACT.Identity, scale=c["ln"][:, 0:1], bias=c["ln"][:, 1:2]).then_inc(sem["hT_out"], 1)
                act.wait_ge(sem["ga_done"], at(one, 6, -6))
                nc.scalar.activation(hT_hi[:, 1 - r, :], ps_t[:], ACT.Identity, scale=c["ln"][:, 0:1],
                                     bias=c["ln"][:, 1:2]).then_inc(sem["hT_hi"], 1)
            gelu(1)
            gelu(2)
        batch_slots(act, slot, 3)

    @block.vector
    def _(dve):
        def gate():
            dve.sem_inc(w["gate_dve"], 1)

        def slot(b, r):
            now, one, two, three = (batch_back(b, k) for k in range(4))
            if one is not None:
                dve.wait_ge(sem["rstd"], at(one, 1, 1))
                dve.wait_ge(sem["T_done"], at(one, 1, 0))
                for t in range(TT):
                    nc.vector.tensor_scalar(hn[:, t, :], hs[:, 1 - r, t, :], mv[:, t, 0:1], rstd[:, t:t + 1],
                                            ALU.subtract, ALU.mult).then_inc(sem["hn"], 1)

            def gated(j):
                if two is None:
                    return
                n = CH[j]
                dve.wait_ge(sem["gelu"], at(two, 3, j + 1))
                dve.wait_ge(sem["ga_done"], at(two, 6, 2 * j + 2))
                if j == 0:
                    dve.wait_ge(sem["y_done"], at(two, 1, -1))
                nc.vector.scalar_tensor_tensor(out=Hh[0:n, r, j, :], in0=ps_a[j][0:n, :], scalar=c["b1"][0:n, j:j + 1],
                                               in1=G[0:n, j, :], op0=ALU.add, op1=ALU.mult).then_inc(sem["H"], 1)
            gated(0)
            if now is not None:
                dve.wait_ge(sem[f"hs{r}"], at(b, 24, 48 - 24 * r) if not isinstance(b, int) else 48 * (b // 2 + 1))
                for t in range(TT):
                    nc.vector.bn_stats(stats[:, t, :], hs[:, r, t, :]).then_inc(sem["stats"], 1)
                dve.wait_ge(sem["stats"], at(b, TT, TT))
                dve.wait_ge(sem["hn"], at(b, TT, 0))
                gate()
                for t in range(TT):
                    nc.vector.bn_aggr(mv[:, t, :], stats[:, t, :]).then_inc(sem["mv"], 1)
                dve.wait_ge(sem["mv"], at(b, TT, TT))
                nc.vector.tensor_scalar(ve[:], mv[:, :, 1], LN_EPS, None, ALU.add).then_inc(sem["ve"], 1)
            if three is not None:
                dve.wait_ge(sem["y_done"], at(three, 1, 1))
                a = xf[:, bass.ds(three * TT, TT), :]
                nc.vector.tensor_tensor(a, ps_y[:].rearrange("p (t d) -> p t d", d=D), a, ALU.add).then_inc(sem["x_out"], 1)
            gated(1)
            gated(2)
        batch_slots(dve, slot, 3)

    @block.tensor
    def _(pe):
        def slot(b, r):
            one, two, three = (batch_back(b, k) for k in range(1, 4))

            def hidden(j):
                if two is None:
                    return
                n = CH[j]
                for part, ps in ((1, ps_g[j]), (0, ps_a[j])):
                    col = slice(part * HID + j * P, part * HID + j * P + n)
                    nc.tensor.matmul(ps[0:n, :], w1_hi[:, col], hT_hi[:, r, :], start=True, stop=False)
                    nc.tensor.matmul(ps[0:n, :], w1_lo[:, col], hT_hi[:, r, :], start=False, stop=False)
                    nc.tensor.matmul(ps[0:n, :], w1_hi[:, col], hT_lo[:, r, :], start=False, stop=True).then_inc(sem["ga_done"], 1)

            def second(tiles):
                for t in tiles:
                    for j in range(3):
                        n = CH[j] + (1 if j == 2 else 0)
                        last = nc.tensor.matmul(ps_y[:, t * D:t * D + D], Hh[0:n, 1 - r, j, t * P:t * P + P], c["w2"][0:n, j, :],
                                                start=(j == 0), stop=(j == 2))
                return last

            if two is not None:
                pe.wait_ge(sem["w_lo"], 1)
                pe.wait_ge(sem["hT_lo"], at(two, 1, 1))
                pe.wait_ge(sem["H"], at(two, 3, -2))
            hidden(0)
            if three is not None:
                pe.wait_ge(sem["H"], at(three, 3, 3))
                pe.wait_ge(sem["x_out"], at(three, 1, 0))
                second(range(2))
            if one is not None:
                pe.wait_ge(sem["hn"], at(one, TT, TT))
                pe.wait_ge(sem["hT_hi"], at(one, 1, 0))
                for t in range(TT):
                    last = nc.tensor.transpose(ps_t[:, t * P:t * P + P], hn[:, t, :], ident[:])
                last.then_inc(sem["T_done"], 1)
            if three is not None:
                second(range(2, TT)).then_inc(sem["y_done"], 1)
            if two is not None:
                pe.wait_ge(sem["H"], at(two, 3, 0))
            hidden(1)
            hidden(2)
        batch_slots(pe, slot, 3)
    block_ctx.__exit__(None, None, None)


ATTN_SEMS = ["hs0", "hs1", "hs2", "hs3", "weights", "tab", "w_hi", "w_lo", "hT_done", "hT_hi", "hT_lo", "qk_done", "v_done",
             "v_out", "sq", "ssum", "ssq", "rn", "rq8", "qab", "qr", "kab", "k_rotated", "kr", "qT_done", "qT_out", "kT_done",
             "kT_out", "scores", "logits", "exp", "rinv", "probs_act", "probs_pool", "PT_done", "PT_out0", "PT_out1", "PT_out2",
             "PT_out3", "vm0", "vm1", "vm2", "vm3", "pv_done", "OT_out", "wo_done", "x_out"]
MLP_SEMS = ["hs0", "hs1", "weights", "w_hi", "w_lo", "stats", "mv", "ve", "rstd", "hn", "T_done", "hT_out", "hT_hi", "hT_lo",
            "ga_done", "gelu", "H", "y_done", "x_out"]


def transformer(nc, c, d):
    with ExitStack() as ctx:
        w = {}

        def sb(name, shape, dt=F32):
            w[name] = ctx.enter_context(nc.sbuf_tensor("f_" + name, shape, dt))
            return w[name]
        c["hs"] = sb("hs", [P, TT, D])
        c["wqkv"] = sb("wqkv", [P, 3 * FI])
        c["wo4"] = sb("wo4", [P, FC, D])
        c["qk_scale"] = sb("qk_scale", [P, 2, DH])
        c["w1"] = sb("w1", [P, 2 * HID])
        c["w2"] = sb("w2", [P, 3, D])
        c["b1"] = sb("b1", [P, 6])
        c["ln"] = sb("ln", [P, 2])
        acc = sb("acc", [P, NT, D])
        sb("rope", [P, TT, 4, DH]), sb("tab", [P, TT, 4, DH]), sb("mask", [P, 2, P]), sb("mhalf", [P, 2 * FH])
        sb("w_hi", [P, 3 * FI], F32R), sb("w_lo", [P, 3 * FI], F32R)
        sb("hT_hi", [P, 2, P], F32R), sb("hT_lo", [P, 2, P], F32R)
        sb("sq", [P, 2, 2, FI]), sb("ssum", [P, 2 * FH]), sb("ssq", [P, 2, 2 * FH])
        sb("rn", [P, 2, 2 * FH]), sb("rq8", [P, 2, FH])
        for n in ("qa", "qb", "ka", "kb"):
            sb(n, [P, 2, FI])
        sb("qr", [P, FI]), sb("kr", [P, FI])
        sb("qT", [P, FC, P]), sb("kT", [P, FC, T]), sb("v", [P, TT, FI])
        sb("L", [P, 2, FH, P]), sb("nmax", [P, 2, FH]), sb("rsum", [P, 2, FH]), sb("rinv", [P, 2, FH])
        sb("PT", [P, FC, 2, P]), sb("vm", [P, TT - 1, FI]), sb("OT", [P, FC, P])
        sb("stats", [P, TT, 6]), sb("mv", [P, TT, 2]), sb("ve", [P, TT]), sb("rstd", [P, TT])
        sb("hn", [P, TT, D]), sb("mT", [P, T]), sb("G", [P, 3, T]), sb("Hh", [P, 2, 3, T])
        w["mT_hi"], w["mT_lo"] = (w[n][:, 0:2 * T].rearrange("p (r t) -> p r t", r=2) for n in ("w_hi", "w_lo"))
        sb("hs2", [P, 2, TT, D])
        sb("w1_hi", [P, 2 * HID], F32R), sb("w1_lo", [P, 2 * HID], F32R)
        w["attn"] = {n: ctx.enter_context(nc.semaphore("attn_" + n)) for n in ATTN_SEMS}
        w["mlp"] = {n: ctx.enter_context(nc.semaphore("mlp_" + n)) for n in MLP_SEMS}
        w["gate_dve"] = ctx.enter_context(nc.semaphore("gate2_dve"))
        w["gate_pe"] = ctx.enter_context(nc.semaphore("gate2_pe"))
        w["gate_pool"] = ctx.enter_context(nc.semaphore("gate2_pool"))
        s_acc = ctx.enter_context(nc.semaphore("out_read_back"))
        s_load = ctx.enter_context(nc.semaphore("layer0_loaded"))
        s_prep = ctx.enter_context(nc.semaphore("tables_set"))
        s_fill = ctx.enter_context(nc.semaphore("buffers_filled"))
        s_sum = ctx.enter_context(nc.semaphore("summed"))
        s_st = ctx.enter_context(nc.semaphore("stored"))

        with nc.Block() as block:
            @block.sync
            def _(sp):
                sp.dma_start(w["rope"][:], d["rope"].rearrange("(t p) k e -> p t k e", p=P)).then_inc(s_load, 16)
                load_attention_weights(sp, c, d, 0, s_load)
                sp.wait_ge(s_fill, 1)
                for t in range(TT):
                    load_shifted(sp, c["hs"], c["xf"], 0, t, w["attn"][f"hs{t}"])
                sp.dma_start(acc[:], d["out"].rearrange("b (t p) d -> p (b t) d", p=P)).then_inc(s_acc, 16)
                sp.wait_ge(s_load, 80)
                for t in range(TT):
                    sp.wait_ge(w["attn"][f"hs{t}"], shifted_count(t))

            @block.vector
            def _(dve):
                nc.vector.memset(c["hs"][:], 0.0).then_inc(s_fill, 1)
                nc.vector.memset(w["hs2"][:], 0.0).then_inc(s_fill, 1)
                nc.vector.memset(w["Hh"][:, :, 2, :], 1.0).then_inc(s_fill, 1)
                dve.wait_ge(s_fill, 3)

            @block.gpsimd
            def _(pool):
                nc.gpsimd.memset(w["mhalf"][:], -0.5).then_inc(s_prep, 1)
                nc.gpsimd.memset(w["mask"][:], 0.0).then_inc(s_prep, 1)
                pool.wait_ge(s_prep, 2)
                mask, before = w["mask"], w["mask"][0:WIN, 1, WIN:P]
                nc.gpsimd.affine_select(out=mask[:], in_=mask[:], compare_op=ALU.is_ge, fill=NEG, base=0,
                                        pattern=[[0, 2], [-1, P]], channel_multiplier=1).then_inc(s_prep, 1)
                pool.wait_ge(s_prep, 3)
                nc.gpsimd.affine_select(out=mask[:], in_=mask[:], compare_op=ALU.is_ge, fill=NEG, base=WIN,
                                        pattern=[[0, 2], [1, P]], channel_multiplier=-1).then_inc(s_prep, 1)
                pool.wait_ge(s_prep, 4)
                nc.gpsimd.memset(before, 0.0).then_inc(s_prep, 1)
                pool.wait_ge(s_prep, 5)
                nc.gpsimd.affine_select(out=before, in_=before, compare_op=ALU.is_ge, fill=NEG, base=0,
                                        pattern=[[1, WIN]], channel_multiplier=-1).then_inc(s_prep, 1)
                pool.wait_ge(s_prep, 6)

        with nc.Fori(0, DEPTH) as l:
            local_attention(nc, c, d, l, w)
            gated_mlp(nc, c, d, l, w)

        with nc.Block() as block:
            @block.vector
            def _(dve):
                dve.wait_ge(s_acc, 16)
                for q in range(4):
                    a = acc[:, 16 * q:16 * q + 16, :]
                    nc.vector.tensor_tensor(a, a, c["xf"][:, 16 * q:16 * q + 16, :], ALU.add).then_inc(s_sum, 1)

            @block.sync
            def _(sp):
                ov = d["out"].rearrange("b (t p) d -> p (b t) d", p=P)
                for q in range(4):
                    sp.wait_ge(s_sum, q + 1)
                    sp.dma_start(ov[:, 16 * q:16 * q + 16, :], acc[:, 16 * q:16 * q + 16, :]).then_inc(s_st, 16)
                sp.wait_ge(s_st, 64)


def rope_constants():
    f = np.float32
    half = np.arange(0, DH, 2, dtype=f)
    inv_freq = f(1.0) / np.power(f(10000.0), half / f(DH))
    t = np.arange(T, dtype=f)
    ang = t[:, None] * inv_freq[None, :].astype(f)
    base = (half + f(0.4 * DH)) / f(1.4 * DH)
    power = (t - T // 2) / f(WIN // 2)
    scale = np.power(base[None, :], power[:, None])
    cos, sin = np.cos(ang), np.sin(ang)
    both = lambda a, b: np.concatenate([a, b], axis=1).astype(f)
    return np.stack([both(cos * scale, cos * scale), both(sin * scale, -sin * scale),
                     both(cos / scale, cos / scale), both(sin / scale, -sin / scale)], axis=1)


def program(nc, x, Wq, Wk, Wv, Wo, bo, rel, wqkv, q_scale, k_scale, wo, ln_g, ln_b, w1, b1, w2, b2, rope, out, ext_dram):
    with ExitStack() as ctx:
        c = {"xf": ctx.enter_context(nc.sbuf_tensor("xf", [P, NT, D], F32)),
             "ident": ctx.enter_context(nc.sbuf_tensor("ident", [P, P], F32)),
             "bank": [ctx.enter_context(nc.psum_tensor(f"bank{i}", [P, 512], F32)) for i in range(8)]}
        d = {"wqkv": wqkv, "q_scale": q_scale, "k_scale": k_scale, "wo": wo, "ln_g": ln_g, "ln_b": ln_b,
             "w1": w1, "b1": b1, "w2": w2, "b2": b2, "rope": rope, "out": out}
        causal_attention(nc, c, x, Wq, Wk, Wv, Wo, bo, rel, out, ext_dram)
        transformer(nc, c, d)


_INS = ["L0_attn_x", "L0_attn_Wq", "L0_attn_Wk", "L0_attn_Wv", "L0_attn_Wo", "L0_attn_bo", "L0_attn_rel_pos_bias",
        "L0_ffn_wqkv", "L0_ffn_q_scale", "L0_ffn_k_scale", "L0_ffn_wo", "L0_ffn_ln_g", "L0_ffn_ln_b", "L0_ffn_w1",
        "L0_ffn_b1", "L0_ffn_w2", "L0_ffn_b2"]


def kernel(**inputs):
    import numpy as _np
    import concourse.bacc as _bacc
    from concourse import mybir as _mybir
    from concourse.bass_utils import run_bass_kernel_spmd as _run

    nc = _bacc.Bacc("TRN2", target_bir_lowering=False, num_devices=1)
    arrays, args = {}, []
    for name in _INS:
        a = _np.ascontiguousarray(inputs[name])
        arrays[f"in_{name}"] = a
        args.append(nc.dram_tensor(f"in_{name}", a.shape, _mybir.dt.from_np(a.dtype), kind="ExternalInput").ap())
    rope = rope_constants()
    arrays["rope"] = rope
    args.append(nc.dram_tensor("rope", rope.shape, _mybir.dt.float32, kind="ExternalInput").ap())
    args.append(nc.dram_tensor("out_0", (16, 512, 128), _mybir.dt.float32, kind="ExternalOutput").ap())
    args.append(nc.dram_tensor("bias_rows", (16, 128, 384), _mybir.dt.float32, kind="Internal").ap())
    program(nc, *args)
    r = _run(nc, [arrays], core_ids=[0])
    return r.results[0]["out_0"]
```
